# Optimizing a Trainium2 kernel written in Bass

```python
import numpy as np
import jax
import jax.numpy as jnp

def _softmax(x, axis=-1):
    return jax.nn.softmax(x, axis=axis)

def _gelu(x):
    return jax.nn.gelu(x, approximate=True)

def _silu(x):
    return jax.nn.silu(x)

def _sigmoid(x):
    return jax.nn.sigmoid(x)

def _layernorm(x, axis=-1, eps=1e-05):
    m = jnp.mean(x, axis=axis, keepdims=True)
    v = jnp.var(x, axis=axis, keepdims=True)
    return (x - m) / jnp.sqrt(v + eps)

def _scatter_add(tgt, idx, src, axis=0):
    return tgt.at[idx].add(src)

def _segment_sum(src, seg, n):
    return jax.ops.segment_sum(src, seg, n)
kernel_name = 'mk_gnn_preln_d2_gnn_r8_807c98'

def setup_inputs(seed: int=0):
    np.random.seed(seed)
    _w = jnp.asarray

    def _rec_inputs():
        import jax
        import jax.numpy as jnp
        _gk = jax.random.key(seed)
        x = -0.0001126 + 1 * jax.random.normal(jax.random.fold_in(_gk, 1), (3750, 256), jnp.float32)
        _s = jax.random.randint(jax.random.fold_in(_gk, 2), (60000,), 0, 3750, jnp.int32)
        _d = jax.random.randint(jax.random.fold_in(_gk, 3), (60000,), 0, 3750, jnp.int32)
        _loop = jnp.arange(3750, dtype=jnp.int32)
        src = jnp.concatenate([_s, _d, _loop])
        dst = jnp.concatenate([_d, _s, _loop])
        _o = jnp.argsort(dst, stable=True)
        src = src[_o]
        dst = dst[_o]
        edge_attr_256 = -5.16925e-05 + 1.00005 * jax.random.normal(jax.random.fold_in(_gk, 13), (123750, 256), jnp.float32)
        return (x, src, dst, edge_attr_256)
    x, src, dst, edge_attr_256 = _rec_inputs()

    def _L0_gnn_setup():
        import jax, jax.numpy as jnp
        import numpy as np
        N = 3750
        E = 60000
        G = 256
        H = 8
        D = G // H
        SCALE = G ** (-0.5)
        LN_EPS = 1e-05

        def _segment_softmax(logits, seg, num_segments):
            m = jax.ops.segment_max(logits, seg, num_segments=num_segments)
            e = jnp.exp(logits - m[seg])
            z = jax.ops.segment_sum(e, seg, num_segments=num_segments)
            return e / z[seg]
        key = jax.random.key(seed)
        k0, k1, k2, k3 = jax.random.split(key, 4)
        s = jax.random.normal(k0, (N, G), dtype=jnp.float32)
        src = jax.random.randint(k1, (E,), 0, N, dtype=jnp.int32)
        dst = jax.random.randint(k2, (E,), 0, N, dtype=jnp.int32)
        Wqkv = jax.random.normal(k3, (G, 3 * G), dtype=jnp.float32) * G ** (-0.5)
        gamma = jnp.ones((G,), dtype=jnp.float32)
        beta = jnp.zeros((G,), dtype=jnp.float32)
        return {'s': s, 'Wqkv': Wqkv, 'gamma': gamma, 'beta': beta, 'src': src, 'dst': dst}
    _L0_gnn_all = _L0_gnn_setup()
    _L0_gnn_in = {k: v for k, v in _L0_gnn_all.items() if k in ('Wqkv', 'gamma', 'beta')}
    del _L0_gnn_all

    def _L1_gnn_setup():
        import jax, jax.numpy as jnp
        import numpy as np
        N_NODES = 12500
        N_EDGES = 50000
        C = 256
        NUM_GRAPHS = 512
        EPS = 1e-05
        key = jax.random.key(seed)
        ks = jax.random.split(key, 12)
        x = jax.random.normal(ks[0], (N_NODES, C), dtype=jnp.float32)
        edge_index = jax.random.randint(ks[1], (2, N_EDGES), 0, N_NODES, dtype=jnp.int32)
        edge_attr = jax.random.normal(ks[2], (N_EDGES, C), dtype=jnp.float32)
        batch = jnp.sort(jax.random.randint(ks[3], (N_NODES,), 0, NUM_GRAPHS, dtype=jnp.int32))
        s1 = 1.0 / np.sqrt(C)
        s2 = 1.0 / np.sqrt(2 * C)
        W1 = jax.random.normal(ks[4], (C, 2 * C), dtype=jnp.float32) * s1
        b1 = jnp.zeros((2 * C,), dtype=jnp.float32)
        bn_gamma = jnp.ones((2 * C,), dtype=jnp.float32)
        bn_beta = jnp.zeros((2 * C,), dtype=jnp.float32)
        W2 = jax.random.normal(ks[5], (2 * C, C), dtype=jnp.float32) * s2
        b2 = jnp.zeros((C,), dtype=jnp.float32)
        ln_w = jnp.ones((C,), dtype=jnp.float32)
        ln_b = jnp.zeros((C,), dtype=jnp.float32)
        gn_w = jnp.ones((C,), dtype=jnp.float32)
        gn_b = jnp.zeros((C,), dtype=jnp.float32)
        gn_ms = jnp.ones((C,), dtype=jnp.float32)
        return dict(x=x, edge_index=edge_index, edge_attr=edge_attr, batch=batch, W1=W1, b1=b1, bn_gamma=bn_gamma, bn_beta=bn_beta, W2=W2, b2=b2, ln_w=ln_w, ln_b=ln_b, gn_w=gn_w, gn_b=gn_b, gn_ms=gn_ms)
    _L1_gnn_all = _L1_gnn_setup()
    _L1_gnn_in = {k: v for k, v in _L1_gnn_all.items() if k in ('W1', 'b1', 'bn_gamma', 'bn_beta', 'W2', 'b2', 'ln_w', 'ln_b', 'gn_w', 'gn_b', 'gn_ms')}
    del _L1_gnn_all
    return {'x': x, 'src': src, 'dst': dst, 'edge_attr_256': edge_attr_256, 'L0_gnn_Wqkv': _L0_gnn_in['Wqkv'], 'L0_gnn_gamma': _L0_gnn_in['gamma'], 'L0_gnn_beta': _L0_gnn_in['beta'], 'L1_gnn_W1': _L1_gnn_in['W1'], 'L1_gnn_b1': _L1_gnn_in['b1'], 'L1_gnn_bn_gamma': _L1_gnn_in['bn_gamma'], 'L1_gnn_bn_beta': _L1_gnn_in['bn_beta'], 'L1_gnn_W2': _L1_gnn_in['W2'], 'L1_gnn_b2': _L1_gnn_in['b2'], 'L1_gnn_ln_w': _L1_gnn_in['ln_w'], 'L1_gnn_ln_b': _L1_gnn_in['ln_b'], 'L1_gnn_gn_w': _L1_gnn_in['gn_w'], 'L1_gnn_gn_b': _L1_gnn_in['gn_b'], 'L1_gnn_gn_ms': _L1_gnn_in['gn_ms']}

def reference(x, src, dst, edge_attr_256, L0_gnn_Wqkv, L0_gnn_gamma, L0_gnn_beta, L1_gnn_W1, L1_gnn_b1, L1_gnn_bn_gamma, L1_gnn_bn_beta, L1_gnn_W2, L1_gnn_b2, L1_gnn_ln_w, L1_gnn_ln_b, L1_gnn_gn_w, L1_gnn_gn_b, L1_gnn_gn_ms):
    import jax
    import jax.numpy as jnp

    def _L0_gnn_ref(s, Wqkv, gamma, beta, src, dst):
        import jax, jax.numpy as jnp
        import numpy as np
        N = 3750
        E = 60000
        G = 256
        H = 8
        D = G // H
        SCALE = G ** (-0.5)
        LN_EPS = 1e-05

        def _segment_softmax(logits, seg, num_segments):
            m = jax.ops.segment_max(logits, seg, num_segments=num_segments)
            e = jnp.exp(logits - m[seg])
            z = jax.ops.segment_sum(e, seg, num_segments=num_segments)
            return e / z[seg]
        mu = jnp.mean(s, axis=-1, keepdims=True)
        var = jnp.mean((s - mu) ** 2, axis=-1, keepdims=True)
        x = (s - mu) * jax.lax.rsqrt(var + LN_EPS) * gamma + beta
        qkv = x @ Wqkv
        q, k, v = jnp.split(qkv, 3, axis=-1)
        q = q.reshape(N, H, D)
        k = k.reshape(N, H, D)
        v = v.reshape(N, H, D)
        att = q[src] * k[dst] * SCALE
        att = _segment_softmax(att, dst, N)
        msg = v[src] * att
        rst = jax.ops.segment_sum(msg, dst, num_segments=N)
        return rst.reshape(N, G)

    def _L1_gnn_ref(x, edge_index, edge_attr, batch, W1, b1, bn_gamma, bn_beta, W2, b2, ln_w, ln_b, gn_w, gn_b, gn_ms):
        import jax, jax.numpy as jnp
        import numpy as np
        N_NODES = 12500
        N_EDGES = 50000
        C = 256
        NUM_GRAPHS = 512
        EPS = 1e-05
        src, dst = (edge_index[0], edge_index[1])
        msg = jax.nn.relu(x[src] + edge_attr)
        agg = jnp.zeros_like(x).at[dst].add(msg)
        h = x + agg
        h = h @ W1 + b1
        mu = jnp.mean(h, axis=0)
        var = jnp.mean((h - mu) ** 2, axis=0)
        h = (h - mu) / jnp.sqrt(var + EPS) * bn_gamma + bn_beta
        h = jax.nn.relu(h) @ W2 + b2
        cnt = jax.ops.segment_sum(jnp.ones((h.shape[0],), h.dtype), batch, NUM_GRAPHS)
        denom = jnp.maximum(cnt, 1.0) * C
        mean_g = jax.ops.segment_sum(h.sum(axis=1), batch, NUM_GRAPHS) / denom
        h = h - mean_g[batch][:, None]
        var_g = jax.ops.segment_sum((h * h).sum(axis=1), batch, NUM_GRAPHS) / denom
        h = h * jax.lax.rsqrt(var_g + EPS)[batch][:, None] * ln_w + ln_b
        cnt_c = jnp.maximum(cnt, 1.0)[:, None]
        mean = jax.ops.segment_sum(h, batch, NUM_GRAPHS) / cnt_c
        out = h - mean[batch] * gn_ms
        var2 = jax.ops.segment_sum(out * out, batch, NUM_GRAPHS) / cnt_c
        out = out * jax.lax.rsqrt(var2 + EPS)[batch] * gn_w + gn_b
        out = jax.nn.relu(out)
        return x + out
    edge_index = jnp.stack([src, dst])
    batch0 = jnp.zeros((3750,), jnp.int32)
    h = jnp.maximum(_layernorm(x, axis=-1), 0.0)
    x = x + _L0_gnn_ref(h, L0_gnn_Wqkv, L0_gnn_gamma, L0_gnn_beta, src, dst)
    h = jnp.maximum(_layernorm(x, axis=-1), 0.0)
    x = x + _L1_gnn_ref(h, edge_index, edge_attr_256, batch0, L1_gnn_W1, L1_gnn_b1, L1_gnn_bn_gamma, L1_gnn_bn_beta, L1_gnn_W2, L1_gnn_b2, L1_gnn_ln_w, L1_gnn_ln_b, L1_gnn_gn_w, L1_gnn_gn_b, L1_gnn_gn_ms)
    return x

_drawn_inputs = setup_inputs


def setup_inputs(seed=0):
    import zlib

    import numpy as np

    out = dict(_drawn_inputs(seed))
    spreads = {'L0_gnn_gamma': (1.0, 0.2),
     'L0_gnn_beta': (0.0, 0.1),
     'L1_gnn_b1': (0.0, 0.8),
     'L1_gnn_bn_gamma': (1.0, 0.2),
     'L1_gnn_bn_beta': (0.0, 0.1),
     'L1_gnn_b2': (0.0, 0.505),
     'L1_gnn_ln_w': (1.0, 0.6),
     'L1_gnn_ln_b': (0.0, 0.8),
     'L1_gnn_gn_w': (1.0, 0.2),
     'L1_gnn_gn_b': (0.0, 0.1),
     'L1_gnn_gn_ms': (1.0, 0.2)}
    factors = {}
    for name, (base, spread) in spreads.items():
        noise = np.random.default_rng([zlib.crc32(name.encode()), seed]).standard_normal(out[name].shape)
        drawn = base * np.exp(spread * noise) if base else spread * noise
        out[name] = jnp.asarray(drawn.astype(out[name].dtype))
    for name, factor in factors.items():
        out[name] = (out[name] * factor).astype(out[name].dtype)
    return out
```

```python
from contextlib import ExitStack

import numpy as np
import concourse.bass as bass
from concourse import mybir

F32 = mybir.dt.float32
I32 = mybir.dt.int32
ALU = mybir.AluOpType
ACT = mybir.ActivationFunctionType
AX = mybir.AxisListType

P = 128
NODES, EDGES, CH, HID = 3750, 123750, 256, 512
NB = 30
NP = NODES // NB
PAD_NODES = P * NB
WIN = 8
NWIN = -(-EDGES // WIN)
LANE_WIN = -(-NWIN // P)
LANE_ROWS = -(-(NWIN + NODES) // (4 * P)) * 4
ROWS = P * LANE_ROWS
GROUPS = LANE_ROWS // 4
BLK = 375
NBLK = EDGES // BLK
DPART = 110
NCHUNK = 10
CCOLS = NODES // NCHUNK
FAR = 1.0e6
NEG = -1.0e30
EPS = 1e-5
SCALE = CH ** -0.5
RING = 4
FRING = 5

PARAMS = [("gamma", 2), ("beta", 2), ("b1", 4), ("bn_g", 4), ("bn_b", 4), ("b2", 2), ("ln_w", 2),
          ("ln_b", 2), ("gn_w", 2), ("gn_b", 2), ("gn_ms", 2)]
NPAR = sum(n for _, n in PARAMS)


def build(nc, x, src, dst, edge, wqkv, w1, w2, params, out):
    assert LANE_ROWS % RING == 0 and NBLK * BLK == EDGES and NP * NB == NODES and NB % 2 == 0
    with ExitStack() as ctx:
        def sb(name, shape, dt=F32):
            return ctx.enter_context(nc.sbuf_tensor(name, shape, dt))

        def sem(name):
            return ctx.enter_context(nc.semaphore(name))

        def dram(name, shape, dt=F32):
            return nc.dram_tensor(name, shape, dt, kind="Internal").ap()

        dst_f = dram("dst_f", (NBLK, BLK))
        blk_last = dram("blk_last", (NBLK,))
        src4 = dram("src4", (P * LANE_WIN, 4 * WIN))
        marks = dram("marks", (ROWS, 3))
        kmark = dram("kmark", (ROWS, CH))
        qv_tab = dram("qv_tab", (PAD_NODES, 2 * CH))
        h_tab = dram("h_tab", (PAD_NODES, CH))
        hist_m = dram("hist_m", (ROWS, CH))
        hist_zs = dram("hist_zs", (ROWS + P, 2 * CH))
        hist_a = dram("hist_a", (ROWS + P, CH))

        xs = sb("xs", [P, NB, CH])
        hs = sb("hs", [P, NB, CH])
        ks = sb("ks", [P, NB * CH])
        ring = sb("ring", [P, RING * WIN * 2 * CH])
        ident = sb("ident", [P, P])
        upper = sb("upper", [P, P])
        ones = sb("ones", [P, P])
        zeros = sb("zeros", [P, LANE_ROWS * 3])
        wq_sb = sb("wq_sb", [P, 2, 3 * CH])
        w1_sb = sb("w1_sb", [P, 2, HID])
        w2_sb = sb("w2_sb", [P, 4, CH])
        par = sb("par", [P, NPAR])
        stats = sb("stats", [P, 4 * NCHUNK, 6])
        mv = sb("mv", [P, NB, 2])
        rstd = sb("rstd", [P, NB])
        nmr = sb("nmr", [P, NB])
        eps = sb("eps", [P, 1])
        xn = sb("xn", [P, 2, CH])
        xT = sb("xT", [P, 2, 2, P])
        stage = sb("stage", [P, 2, 2 * CH])

        nid_i = sb("nid_i", [P, NB + 1], I32)
        nid = sb("nid", [P, NB + 1])
        cnt = sb("cnt", [P, NB + 1])
        blk_i = sb("blk_i", [P, NB + 1], I32)
        start = sb("start", [P, NB + 1])
        n_i = sb("n_i", [P, 2, NB + 1], I32)
        s3 = sb("s3", [P, 2, NB + 1])
        has = sb("has", [P, NB])
        nrow = sb("nrow", [P, NB])
        incl = sb("incl", [P, NB])
        rs = sb("rs", [P, NB])
        nt = sb("nt", [P, 4, NB])
        sidx = sb("sidx", [P, NB], I32)
        fidx = sb("fidx", [P, NB], I32)
        lane_i = sb("lane_i", [P, 2, NB], I32)
        mk = sb("mk", [P, NB, 3])
        offs = sb("offs", [P, 2])

        row_i = sb("row_i", [P, LANE_ROWS], I32)
        row = sb("row", [P, LANE_ROWS])
        fld = sb("fld", [P, 3, LANE_ROWS])
        win_i = sb("win_i", [P, LANE_ROWS], I32)
        kcont = sb("kcont", [P, LANE_ROWS])
        brk = sb("brk", [P, LANE_ROWS])
        acont = sb("acont", [P, LANE_ROWS])
        mneg = sb("mneg", [P, LANE_ROWS])
        w_i = sb("w_i", [P, WIN], I32)
        wslot = sb("wslot", [P, WIN])
        sneg = sb("sneg", [P, LANE_ROWS, WIN])
        pack = sb("pack", [P, LANE_ROWS + RING, WIN + 1], I32)
        idx = sb("idx", [P, RING, WIN + 1], I32)
        bn = sb("bn", [P, 3, 4])
        mvd = sb("mvd", [P, 4, 2])
        gn = sb("gn", [P, 15, 2])
        l3 = sb("l3", [P, 3])
        l3t = sb("l3t", [3, 2, P])
        lane = sb("lane", [P, 6])
        lane_j = sb("lane_j", [P, 3], I32)
        flagb = sb("flagb", [P, 2, P])

        banks = [ctx.enter_context(nc.psum_tensor(f"bank{i}", [P, 512], F32)) for i in range(8)]

        blk_sb = ring[:, 0:NBLK]
        cmp1 = ring[:, 512:512 + (NB + 1) * NBLK].rearrange("p (b k) -> p b k", b=NB + 1)
        dblk = ring[:, 0:(NB + 1) * BLK].rearrange("p (b k) -> p b k", b=NB + 1)
        dst_sb = ring[0:DPART, 1024:1024 + EDGES // DPART].bitcast(I32)
        dstf_sb = ring[0:DPART, 4096:4096 + EDGES // DPART]
        dlast_sb = ring[0:DPART, 6144:6144 + NBLK // DPART]
        src_sb = ring[:, 10752:10752 + (LANE_WIN + 3) * WIN].bitcast(I32)
        src4_sb = ring[:, 12000:12000 + LANE_WIN * 4 * WIN]
        LW = LANE_ROWS * WIN
        hsf = hs[:, :, :].rearrange("p b c -> p (b c)")
        valid = hsf[:, 0:LW].rearrange("p (r w) -> p r w", w=WIN)
        srow = hsf[:, LW:2 * LW].rearrange("p (r w) -> p r w", w=WIN)
        src4_row = hsf[:, 2 * LW:2 * LW + GROUPS * 4 * WIN]
        seltmp = hsf[:, 3 * LW:3 * LW + GROUPS * WIN].rearrange("p (g w) -> p g w", w=WIN)
        tmp0 = 4 * LW
        mkr = hsf[:, tmp0:tmp0 + 3 * LANE_ROWS].rearrange("p (r f) -> p r f", f=3)
        win, winc, t0, t1, fmx, delta = (hsf[:, tmp0 + (3 + n) * LANE_ROWS:tmp0 + (4 + n) * LANE_ROWS] for n in range(6))
        delta = delta[:, 0:GROUPS]
        at = [0]

        def carve(*shape):
            n = int(np.prod(shape))
            v = ks[:, at[0]:at[0] + n]
            at[0] += n
            assert at[0] <= NB * CH
            return v if len(shape) == 1 else v.rearrange("p (a b) -> p a b", a=shape[0])

        kcur = carve(CH)
        km = carve(RING, CH)
        mx1 = carve(4, CH)
        mx2 = carve(2, CH)
        mx3 = carve(CH)
        top = carve(RING, CH)
        zs = carve(RING, 2 * CH)
        alpha = carve(2, CH)
        carry = carve(2, 2 * CH)
        hst = mx1.rearrange("p a b -> p (a b)")
        acc = zs[:, :, 0:CH]
        qv = ring[:, :].rearrange("p (r w h c) -> p r w h c", r=RING, w=WIN, h=2)
        hmsg = ring[:, 0:RING * WIN * CH].rearrange("p (r w c) -> p r w c", r=RING, w=WIN)
        eat = ring[:, RING * WIN * CH:].rearrange("p (r n) -> p r n", r=RING)
        fin = ring[:, 0:FRING * 2 * CH].rearrange("p (r n) -> p r n", r=FRING)
        join = ring[:, 4096:4096 + 24 * P].rearrange("p (n c) -> p n c", c=P)
        y1 = ring[:, 0:4 * NODES].rearrange("p (m n) -> p m n", m=4)
        hT = ks[:, 0:2 * NODES].rearrange("p (m n) -> p m n", m=2)
        y2 = hT

        def pv(name, m):
            first = sum(w for _, w in PARAMS[:[n for n, _ in PARAMS].index(name)])
            return par[:, first + m:first + m + 1]

        def pvs(name):
            n = dict(PARAMS)[name]
            first = sum(w for _, w in PARAMS[:[k for k, _ in PARAMS].index(name)])
            return par[:, first:first + n]

        dst_in, src_in, x_in, w_in, par_in = (sem(n) for n in ("dst_in", "src_in", "x_in", "w_in", "par_in"))
        dstf_out, blk_in, src4_out, zero_k, zero_m = (sem(n) for n in ("dstf_out", "blk_in", "src4_out", "zero_k", "zero_m"))
        consts0, consts, iotas, memsets = (sem(n) for n in ("consts0", "consts", "iotas", "memsets"))
        dve = sem("dve")
        bnst, aggr = sem("bnst"), sem("aggr")
        dstf_done, src4_done, blk_done, node_done, win_done, qidx_done = (
            sem(n) for n in ("dstf_done", "src4_done", "blk_done", "node_done", "win_done", "qidx_done"))
        blk_gathered, marks_out, marks_in, k_out, src4_gathered, kinit = (
            sem(n) for n in ("blk_gathered", "marks_out", "marks_in", "k_out", "src4_gathered", "kinit"))
        ln_var, ln_std, ln_norm = sem("ln_var"), sem("ln_std"), sem("ln_norm")
        h_ready, xn_ready, tr_ready, xT_ready, qkv_ready, qkv_evac = (
            sem(n) for n in ("h_ready", "xn_ready", "tr_ready", "xT_ready", "qkv_ready", "qkv_evac"))
        qv_out = [sem(f"qv_out{i}") for i in range(2)]
        small_in, small_out = sem("small_in"), sem("small_out")
        state0, km_in, qv_in = sem("state0"), [sem(f"km_in{i}") for i in range(RING)], [sem(f"qv_in{i}") for i in range(RING)]
        a_step, exp_ready, weighted, psum_ready, state_ready = (
            sem(n) for n in ("a_step", "exp_ready", "weighted", "psum_ready", "state_ready"))
        hist_out = [sem(f"hist_out{i}") for i in range(RING)]
        hst_in, join_done, join_out = sem("hst_in"), sem("join_done"), sem("join_out")
        join_arg, join_exp, idx_ready, gathering = (sem(n) for n in ("join_arg", "join_exp", "idx_ready", "gathering"))
        g_ready, xh_done = sem("g_ready"), sem("xh_done")
        fin_in, fin_step, fin_used = [sem(f"fin_in{i}") for i in range(FRING)], sem("fin_step"), sem("fin_used")
        h_out = sem("h_out")
        msg_in = [sem(f"msg_in{i}") for i in range(RING)]
        added, relued, carried, sum_ready, acc_ready = (
            sem(n) for n in ("added", "relued", "carried", "sum_ready", "acc_ready"))
        hista_out = [sem(f"hista_out{i}") for i in range(RING)]
        hsa_in, joina_out = sem("hsa_in"), sem("joina_out")
        agg_in, agg_add, agg_tr, agg_cp = [sem(f"agg_in{i}") for i in range(FRING)], sem("agg_add"), sem("agg_tr"), sem("agg_cp")
        y1_mm, y1_ev, y1_bn, bn_var, bn_std, bn_ready, y1_act = (
            sem(n) for n in ("y1_mm", "y1_ev", "y1_bn", "bn_var", "bn_std", "bn_ready", "y1_act"))
        y2_mm, y2_ev, y2_bn = sem("y2_mm"), sem("y2_ev"), sem("y2_bn")
        g_var, g_std, out_aff, out_tr, out_add, out_st = (
            sem(n) for n in ("g_var", "g_std", "out_aff", "out_tr", "out_add", "out_st"))

        block = ctx.enter_context(nc.Block())
        lanes = lambda t, a: t[0:ROWS, :].rearrange("(p c) f -> p c f", p=P)[:, a, :]

        @block.sync
        def _(sp):
            sp.dma_start(dst_sb, dst.rearrange("(p n) -> p n", p=DPART)).then_inc(dst_in, 16)
            sp.dma_start(xs[:, :, :], x.rearrange("(p b) c -> p b c", p=P)).then_inc(x_in, 16)
            sp.dma_start(src_sb, src).then_inc(src_in, 16)
            sp.dma_start(par[:, :], params).then_inc(par_in, 16)
            sp.dma_start(wq_sb[:, :, :], wqkv).then_inc(w_in, 16)
            sp.dma_start(w1_sb[:, :, :], w1).then_inc(w_in, 16)
            sp.dma_start(w2_sb[:, :, :], w2).then_inc(w_in, 16)
            sp.wait_ge(dstf_done, 2)
            sp.dma_start(dst_f.rearrange("(p b) n -> p (b n)", p=DPART), dstf_sb).then_inc(dstf_out, 16)
            sp.dma_start(blk_last.rearrange("(p n) -> p n", p=DPART), dlast_sb).then_inc(dstf_out, 16)
            sp.wait_ge(dstf_out, 32)
            sp.dma_start(blk_sb, blk_last.rearrange("(a n) -> a n", a=1).to_broadcast([P, NBLK])).then_inc(blk_in, 16)
            sp.wait_ge(memsets, 1)
            sp.dma_start(marks.rearrange("(p c) f -> p (c f)", p=P), zeros[:, :]).then_inc(zero_m, 16)
            sp.wait_ge(src4_done, 4)
            sp.dma_start(src4.rearrange("(p n) d -> p (n d)", p=P), src4_sb).then_inc(src4_out, 16)
            sp.dma_start(kmark.rearrange("(p c) f -> p c f", p=P),
                         zeros[:, None, 0:CH].to_broadcast([P, LANE_ROWS, CH])).then_inc(zero_k, 16)

            def store_qv(b, u):
                sp.wait_ge(qkv_evac, b + 1)
                sp.dma_start(qv_tab.rearrange("(p b) c -> p b c", p=P)[:, b, :], stage[:, u, :]).then_inc(qv_out[u], 16)

            with sp.Fori(0, NB // 2) as i:
                for u in range(2):
                    store_qv(2 * i + u, u)
            sp.wait_ge(marks_out, 16 * NB)
            sp.dma_start(mkr.rearrange("p r f -> p (r f)"), marks.rearrange("(p c) f -> p (c f)", p=P)).then_inc(marks_in, 16)

            def load_km(i, u):
                sp.dma_start(km[:, u, :], lanes(kmark, 4 * i + u)).then_inc(km_in[u], 16)

            def store_state(i, u):
                sp.wait_ge(state_ready, 4 * i + u + 1)
                sp.dma_start(lanes(hist_m, 4 * i + u), top[:, u, :]).then_inc(hist_out[u], 16)
                sp.dma_start(lanes(hist_zs, 4 * i + u), zs[:, u, :]).then_inc(hist_out[u], 16)

            sp.wait_ge(k_out, 16 * NB)
            load_km(0, 0)
            load_km(0, 1)
            for u in range(RING):
                if u >= 2:
                    sp.wait_ge(a_step, 8 * (u - 2) + 1)
                load_km((u + 2) // RING, (u + 2) % RING)
                store_state(0, u)
            with sp.Fori(1, LANE_ROWS // RING - 1) as i:
                for u in range(RING):
                    sp.wait_ge(a_step, 32 * i + 8 * u - 15)
                    load_km(i + (u + 2) // RING, (u + 2) % RING)
                    store_state(i, u)
            tail = LANE_ROWS // RING - 1
            for u in range(RING):
                if u < 2:
                    sp.wait_ge(a_step, 32 * tail + 8 * u - 15)
                    load_km(tail, u + 2)
                store_state(tail, u)

            sp.wait_ge(join_done, 1)
            sp.dma_start(hist_zs[ROWS:ROWS + P, :], carry[:, 0, :]).then_inc(join_out, 16)
            sp.wait_ge(h_ready, 2 * NB)
            sp.dma_start(h_tab.rearrange("(p b) c -> p b c", p=P), hs[:, :, :]).then_inc(h_out, 16)

            def store_acc(i, u):
                sp.wait_ge(acc_ready, 4 * i + u + 1)
                sp.dma_start(lanes(hist_a, 4 * i + u), acc[:, u, :]).then_inc(hista_out[u], 16)

            with sp.Fori(0, LANE_ROWS // RING) as i:
                for u in range(RING):
                    store_acc(i, u)
            sp.wait_ge(join_done, 2)
            sp.dma_start(hist_a[ROWS:ROWS + P, :], carry[:, 0, 0:CH]).then_inc(joina_out, 16)
            for g in range(3):
                sp.wait_ge(out_add, (g + 1) * NB // 3)
                sp.dma_start(out.rearrange("(p b) c -> p b c", p=NP)[:, g * NB // 3:(g + 1) * NB // 3, :],
                             xs[0:NP, g * NB // 3:(g + 1) * NB // 3, :]).then_inc(out_st, 16)
            sp.wait_ge(out_st, 48)

        @block.gpsimd
        def _(pool):
            pool.memset(zeros[:, :], 0.0).then_inc(memsets, 1)
            pool.memset(ident[:, :], 0.0).then_inc(consts0, 1)
            pool.memset(ones[:, :], 1.0).then_inc(consts0, 1)
            pool.iota(nid_i[:, :], pattern=[[1, NB + 1]], base=0, channel_multiplier=NB).then_inc(iotas, 1)
            pool.iota(row_i[:, :], pattern=[[1, LANE_ROWS]], base=0, channel_multiplier=LANE_ROWS).then_inc(iotas, 1)
            pool.iota(w_i[:, :], pattern=[[1, WIN]], base=0, channel_multiplier=0).then_inc(iotas, 1)
            pool.wait_ge(consts0, 2)
            pool.affine_select(out=ident[:, :], in_=ident[:, :], compare_op=ALU.not_equal, fill=1.0, base=0,
                               pattern=[[-1, P]], channel_multiplier=1).then_inc(consts, 1)
            pool.affine_select(out=upper[:, :], in_=ones[:, :], compare_op=ALU.is_gt, fill=0.0, base=0,
                               pattern=[[1, P]], channel_multiplier=-1).then_inc(consts, 1)
            pool.wait_ge(blk_done, 1)
            for b in range(NB + 1):
                pool.indirect_dma_start(dblk[:, b, :], None, dst_f[:, :],
                                        bass.IndirectOffsetOnAxis(ap=blk_i[:, b:b + 1], axis=0),
                                        bounds_check=NBLK - 1, oob_is_err=False).then_inc(blk_gathered, 16)
            pool.wait_ge(node_done, 1)
            pool.wait_ge(zero_m, 16)
            for b in range(NB):
                pool.indirect_dma_start(marks[:, :], bass.IndirectOffsetOnAxis(ap=sidx[:, b:b + 1], axis=0),
                                        mk[:, b, :], None, bounds_check=ROWS - 1, oob_is_err=False).then_inc(marks_out, 16)
            pool.wait_ge(qkv_evac, NB)
            pool.wait_ge(zero_k, 16)
            for b in range(NB):
                pool.indirect_dma_start(kmark[:, :], bass.IndirectOffsetOnAxis(ap=sidx[:, b:b + 1], axis=0),
                                        ks[:, b * CH:(b + 1) * CH], None, bounds_check=ROWS - 1,
                                        oob_is_err=False).then_inc(k_out, 16)
            pool.wait_ge(win_done, 2)
            pool.wait_ge(src4_out, 16)
            for g in range(GROUPS):
                pool.indirect_dma_start(src4_row[:, g * 4 * WIN:(g + 1) * 4 * WIN], None, src4[:, :],
                                        bass.IndirectOffsetOnAxis(ap=win_i[:, 4 * g:4 * g + 1], axis=0),
                                        bounds_check=P * LANE_WIN - 1, oob_is_err=False).then_inc(src4_gathered, 16)
            pool.wait_ge(k_out, 16 * NB)
            pool.indirect_dma_start(kcur, None, kmark[:, :], bass.IndirectOffsetOnAxis(ap=lane_j[:, 0:1], axis=0),
                                    bounds_check=ROWS - 1, oob_is_err=False).then_inc(kinit, 16)

            last_node, last_window = pool.to_reg(PAD_NODES - 1), pool.to_reg(NWIN - 1)

            def gather_qv(t, u):
                pool.wait_ge(idx_ready, t + 1)
                pool.sem_inc(gathering, 1)
                for w in range(WIN):
                    pool.indirect_dma_start(qv[:, u, w, :, :].rearrange("p h c -> p (h c)"), None, qv_tab[:, :],
                                            bass.IndirectOffsetOnAxis(ap=idx[:, u, w:w + 1], axis=0),
                                            bounds_check=last_node, oob_is_err=False).then_inc(qv_in[u], 16)

            for u in range(2):
                pool.wait_ge(qv_out[u], 16 * (NB // 2))
            for u in range(RING):
                gather_qv(u, u)
            with pool.Fori(1, LANE_ROWS // RING) as i:
                for u in range(RING):
                    gather_qv(4 * i + u, u)

            for u in range(RING):
                pool.wait_ge(hist_out[u], 32 * (LANE_ROWS // RING))
            pool.indirect_dma_start(hst[:, 0:CH], None, hist_m[:, :], bass.IndirectOffsetOnAxis(ap=lane_j[:, 1:2], axis=0),
                                    bounds_check=ROWS - 1, oob_is_err=False).then_inc(hst_in, 16)
            pool.indirect_dma_start(hst[:, CH:3 * CH], None, hist_zs[0:ROWS, :], bass.IndirectOffsetOnAxis(ap=lane_j[:, 1:2], axis=0),
                                    bounds_check=ROWS - 1, oob_is_err=False).then_inc(hst_in, 16)
            pool.wait_ge(join_out, 16)

            for b in range(NB):
                if b >= FRING:
                    pool.wait_ge(fin_step, 3 * (b - FRING + 1))
                pool.indirect_dma_start(fin[:, b % FRING, :], None, hist_zs[:, :],
                                        bass.IndirectOffsetOnAxis(ap=fidx[:, b:b + 1], axis=0),
                                        bounds_check=ROWS + P - 1, oob_is_err=False).then_inc(fin_in[b % FRING], 16)

            def gather_msg(t, u):
                pool.wait_ge(idx_ready, LANE_ROWS + RING + t + 1)
                pool.sem_inc(gathering, 1)
                pool.indirect_dma_start(eat[:, u, :], None, edge[:, :],
                                        bass.IndirectOffsetOnAxis(ap=idx[:, u, WIN:WIN + 1], axis=0),
                                        bounds_check=last_window, oob_is_err=False).then_inc(msg_in[u], 16)
                for w in range(WIN):
                    pool.indirect_dma_start(hmsg[:, u, w, :], None, h_tab[:, :],
                                            bass.IndirectOffsetOnAxis(ap=idx[:, u, w:w + 1], axis=0),
                                            bounds_check=last_node, oob_is_err=False).then_inc(msg_in[u], 16)

            pool.wait_ge(fin_step, 3 * NB)
            pool.wait_ge(h_out, 16)
            for u in range(RING):
                gather_msg(u, u)
            with pool.Fori(1, LANE_ROWS // RING) as i:
                for u in range(RING):
                    gather_msg(4 * i + u, u)
            for u in range(RING):
                pool.wait_ge(hista_out[u], 16 * (LANE_ROWS // RING))
            pool.indirect_dma_start(hst[:, 0:CH], None, hist_a[0:ROWS, :], bass.IndirectOffsetOnAxis(ap=lane_j[:, 1:2], axis=0),
                                    bounds_check=ROWS - 1, oob_is_err=False).then_inc(hsa_in, 16)
            pool.wait_ge(joina_out, 16)
            for b in range(NB):
                if b >= FRING:
                    pool.wait_ge(agg_add, b - FRING + 1)
                pool.indirect_dma_start(fin[:, b % FRING, 0:CH], None, hist_a[:, :],
                                        bass.IndirectOffsetOnAxis(ap=fidx[:, b:b + 1], axis=0),
                                        bounds_check=ROWS + P - 1, oob_is_err=False).then_inc(agg_in[b % FRING], 16)

        @block.scalar
        def _(act):
            def std_of_var(n):
                act.wait_ge(ln_var, n)
                act.activation(rstd[:, :], mv[:, :, 1], ACT.Sqrt, bias=eps[:, 0:1]).then_inc(ln_std, 1)

            def relu_ln(b):
                act.activation(hs[:, b, :], xs[:, b, :], ACT.Relu, bias=nmr[:, bass.ds(b, 1)],
                               scale=rstd[:, bass.ds(b, 1)]).then_inc(h_ready, 1)

            std_of_var(1)
            act.wait_ge(ln_norm, 1)
            relu_ln(0)
            with act.Fori(1, NB) as b:
                relu_ln(b)
            std_of_var(2)
            act.wait_ge(ln_norm, 2)
            act.wait_ge(par_in, 16)

            def normalise(b, u, warm):
                if warm:
                    act.wait_ge(tr_ready, b - 1)
                act.activation(xn[:, u, :], hs[:, b, :], ACT.Identity, bias=nmr[:, bass.ds(b, 1)],
                               scale=rstd[:, bass.ds(b, 1)]).then_inc(xn_ready, 1)

            def scale_T(b, u, warm):
                act.wait_ge(tr_ready, b + 1)
                if warm:
                    act.wait_ge(qkv_ready, b - 1)
                for h in range(2):
                    last = act.activation(xT[:, u, h, :], banks[u][:, h * P:(h + 1) * P], ACT.Identity,
                                          bias=pv("beta", h), scale=pv("gamma", h))
                last.then_inc(xT_ready, 1)

            def evac_qkv(b, u, warm):
                act.wait_ge(qkv_ready, b + 1)
                if warm:
                    act.wait_ge(qv_out[u], 8 * b - 8 * u)
                act.activation(stage[:, u, :], banks[2 + u][:, :], ACT.Copy)
                act.activation(ks[:, bass.ds(b * CH, CH)], banks[4 + u][:, 0:CH], ACT.Copy).then_inc(qkv_evac, 1)

            normalise(0, 0, False)
            normalise(1, 1, False)
            scale_T(0, 0, False)
            for b in (2, 3):
                normalise(b, b % 2, True)
                scale_T(b - 1, (b - 1) % 2, b > 2)
                evac_qkv(b - 2, b % 2, False)
            with act.Fori(2, NB // 2) as i:
                for u in range(2):
                    normalise(2 * i + u, u, True)
                    scale_T(2 * i + u - 1, 1 - u, True)
                    evac_qkv(2 * i + u - 2, u, True)
            scale_T(NB - 1, 1, True)
            evac_qkv(NB - 2, 0, True)
            evac_qkv(NB - 1, 1, True)

            def next_idx(i, u):
                act.activation(idx[:, u, :], pack[:, 4 * i + u + RING, :], ACT.Copy).then_inc(idx_ready, 1)

            def first_idx():
                for u in range(RING):
                    act.activation(idx[:, u, :], pack[:, u, :], ACT.Copy).then_inc(idx_ready, 1)

            def exps(i, u):
                act.wait_ge(a_step, 32 * i + 8 * u + 8)
                act.activation(alpha[:, u % 2, :], alpha[:, u % 2, :], ACT.Exp, scale=SCALE)
                for w in range(WIN):
                    last = act.activation(qv[:, u, w, 0, :], qv[:, u, w, 0, :], ACT.Exp,
                                          bias=sneg[:, 4 * i + u, w:w + 1], scale=SCALE)
                last.then_inc(exp_ready, 1)

            def evac_state(i, u):
                act.wait_ge(psum_ready, 4 * i + u + 1)
                act.activation(zs[:, u, :], banks[u % 2][:, :], ACT.Copy).then_inc(state_ready, 1)
                next_idx(i, u)

            act.wait_ge(qidx_done, 1)
            first_idx()
            exps(0, 0)
            for u in range(1, RING):
                exps(0, u)
                evac_state(0, u - 1)
            with act.Fori(1, LANE_ROWS // RING) as i:
                for u in range(RING):
                    exps(i, u)
                    evac_state(i if u else i - 1, (u - 1) % RING)
            evac_state(LANE_ROWS // RING - 1, RING - 1)

            for h in range(2):
                act.wait_ge(join_arg, h + 1)
                act.activation(join[:, 16:20, :], join[:, 16:20, :], ACT.Exp, scale=SCALE).then_inc(join_exp, 1)

            std_of_var(3)
            act.wait_ge(ln_norm, 3)
            relu_ln(0)
            with act.Fori(1, NB) as b:
                relu_ln(b)

            def relus(i, u):
                act.wait_ge(added, 4 * i + u + 1)
                for w in range(WIN):
                    last = act.activation(hmsg[:, u, w, :], hmsg[:, u, w, :], ACT.Relu,
                                          bias=sneg[:, 4 * i + u, w:w + 1])
                last.then_inc(relued, 1)

            def evac_acc(i, u):
                act.wait_ge(sum_ready, 4 * i + u + 1)
                act.activation(acc[:, u, :], banks[u % 2][:, 0:CH], ACT.Copy).then_inc(acc_ready, 1)
                next_idx(i, u)

            first_idx()
            relus(0, 0)
            for u in range(1, RING):
                relus(0, u)
                evac_acc(0, u - 1)
            with act.Fori(1, LANE_ROWS // RING) as i:
                for u in range(RING):
                    relus(i, u)
                    evac_acc(i if u else i - 1, (u - 1) % RING)
            evac_acc(LANE_ROWS // RING - 1, RING - 1)

            def columns(b, u):
                act.wait_ge(agg_tr, b + 1)
                act.activation(hT[:, :, bass.ds(b * NP, NP)],
                               banks[2 + u][:, 0:2 * P].rearrange("p (m n) -> p m n", m=2)[:, :, 0:NP],
                               ACT.Copy).then_inc(agg_cp, 1)

            with act.Fori(0, NB // 2) as i:
                for u in range(2):
                    columns(2 * i + u, u)

            def bias1(n, u):
                for m in range(4):
                    act.wait_ge(y1_mm, 4 * n + m + 1)
                    act.activation(y1[:, m, bass.ds(n * CCOLS, CCOLS)], banks[4 * u + m][:, 0:CCOLS], ACT.Identity,
                                   bias=pv("b1", m)).then_inc(y1_ev, 1)

            with act.Fori(0, NCHUNK // 2) as i:
                for u in range(2):
                    bias1(2 * i + u, u)
            act.wait_ge(bn_var, 1)
            act.activation(bn[:, 0, :], bn[:, 0, :], ACT.Sqrt, bias=eps[:, 0:1]).then_inc(bn_std, 1)
            act.wait_ge(bn_ready, 1)

            def relu1(n):
                for m in range(4):
                    last = act.activation(y1[:, m, bass.ds(n * CCOLS, CCOLS)], y1[:, m, bass.ds(n * CCOLS, CCOLS)],
                                          ACT.Relu, bias=bn[:, 2, m:m + 1], scale=bn[:, 1, m:m + 1])
                last.then_inc(y1_act, 1)

            def bias2(n, u):
                act.wait_ge(y2_mm, n + 1)
                for m in range(2):
                    last = act.activation(y2[:, m, bass.ds(n * CCOLS, CCOLS)], banks[2 * u + m][:, 0:CCOLS],
                                          ACT.Identity, bias=pv("b2", m))
                last.then_inc(y2_ev, 1)

            relu1(0)
            relu1(1)
            bias2(0, 0)
            with act.Fori(1, NCHUNK // 2) as i:
                for u in range(2):
                    relu1(2 * i + u)
                    bias2(2 * i + u - 1, 1 - u)
            bias2(NCHUNK - 1, 1)
            for n in range(2):
                act.wait_ge(g_var, n + 1)
                act.activation(gn[:, 12, :], gn[:, 12, :], ACT.Sqrt, bias=eps[:, 0:1]).then_inc(g_std, 1)
            act.wait_ge(g_ready, 1)

            def affine(b, u, warm):
                if warm:
                    act.wait_ge(out_tr, b - 1)
                for m in range(2):
                    last = act.activation(xT[:, u, m, 0:NP], y2[:, m, bass.ds(b * NP, NP)], ACT.Relu,
                                          bias=gn[:, 14, m:m + 1], scale=gn[:, 13, m:m + 1])
                last.then_inc(out_aff, 1)

            affine(0, 0, False)
            affine(1, 1, False)
            with act.Fori(1, NB // 2) as i:
                for u in range(2):
                    affine(2 * i + u, u, True)

        @block.tensor
        def _(pe):
            pe.wait_ge(consts, 2)
            pe.wait_ge(w_in, 48)

            def turn(b, u, warm):
                pe.wait_ge(xn_ready, b + 1)
                if warm:
                    pe.wait_ge(xT_ready, b - 1)
                for h in range(2):
                    last = pe.transpose(banks[u][:, h * P:(h + 1) * P], xn[:, u, h * P:(h + 1) * P], ident[:, :])
                last.then_inc(tr_ready, 1)

            def project(b, u, warm):
                pe.wait_ge(xT_ready, b + 1)
                if warm:
                    pe.wait_ge(qkv_evac, b - 1)
                for h in range(2):
                    pe.matmul(banks[2 + u][:, :], xT[:, u, h, :], wq_sb[:, h, 0:2 * CH], start=(h == 0), stop=(h == 1))
                for h in range(2):
                    last = pe.matmul(banks[4 + u][:, 0:CH], xT[:, u, h, :], wq_sb[:, h, 2 * CH:3 * CH],
                                     start=(h == 0), stop=(h == 1))
                last.then_inc(qkv_ready, 1)

            turn(0, 0, False)
            turn(1, 1, False)
            project(0, 0, False)
            turn(2, 0, True)
            project(1, 1, False)
            turn(3, 1, True)
            project(2, 0, True)
            with pe.Fori(2, NB // 2) as i:
                for u in range(2):
                    turn(2 * i + u, u, True)
                    project(2 * i + u - 1, 1 - u, True)
            project(NB - 1, 1, True)

            pe.wait_ge(small_in, 1)
            pe.matmul(banks[6][:, 0:1], upper[:, :], incl[:, NB - 1:NB], start=True, stop=True)
            pe.matmul(banks[6][:, 1:2], ones[:, :], incl[:, NB - 1:NB], start=True, stop=True).then_inc(small_out, 1)
            pe.wait_ge(small_in, 2)
            pe.transpose(banks[6][0:3, P:2 * P], l3[:, :], ident[:, :]).then_inc(small_out, 1)
            pe.wait_ge(small_in, 3)
            pe.transpose(banks[6][:, 2 * P:2 * P + 3], l3t[:, 1, :], ident[0:3, 0:3]).then_inc(small_out, 1)
            pe.wait_ge(small_in, 4)
            pe.matmul(banks[7][:, 0:P], ones[:, :], xT[:, 0, 0, :], start=True, stop=True).then_inc(small_out, 1)

            def sum_slots(i, u, warm):
                pe.wait_ge(weighted, 8 * i + 2 * u + 1)
                if warm:
                    pe.wait_ge(state_ready, 4 * i + u - 1)
                for w in range(WIN):
                    pe.matmul(banks[u % 2][:, :], ident[:, :], qv[:, u, w, :, :].rearrange("p h c -> p (h c)"),
                              start=(w == 0), stop=False)
                pe.wait_ge(weighted, 8 * i + 2 * u + 2)
                pe.matmul(banks[u % 2][:, :], ident[:, :], carry[:, u % 2, :], start=False, stop=True)\
                  .then_inc(psum_ready, 1)

            for u in range(RING):
                sum_slots(0, u, u > 1)
            with pe.Fori(1, LANE_ROWS // RING) as i:
                for u in range(RING):
                    sum_slots(i, u, True)

            def turn_all(pairs):
                for to, of in pairs:
                    last = pe.transpose(to, of, ident[:, :])
                last.then_inc(small_out, 1)

            pe.wait_ge(state_ready, LANE_ROWS)
            pe.wait_ge(hst_in, 32)
            end = [top[:, RING - 1, n * P:(n + 1) * P] for n in range(2)] + [zs[:, RING - 1, n * P:(n + 1) * P] for n in range(4)] + [hst[:, n * P:(n + 1) * P] for n in range(6)]
            turn_all([(banks[2 + n // 4][:, n % 4 * P:(n % 4 + 1) * P], e) for n, e in enumerate(end)])
            pe.wait_ge(small_in, 5)
            turn_all([(banks[2][:, n * P:(n + 1) * P], join[:, 8 + n, :]) for n in range(4)])

            def sum_msgs(i, u, warm):
                pe.wait_ge(relued, 4 * i + u + 1)
                if warm:
                    pe.wait_ge(acc_ready, 4 * i + u - 1)
                for w in range(WIN):
                    pe.matmul(banks[u % 2][:, 0:CH], ident[:, :], hmsg[:, u, w, :], start=(w == 0), stop=False)
                pe.wait_ge(carried, 4 * i + u + 1)
                pe.matmul(banks[u % 2][:, 0:CH], ident[:, :], carry[:, u % 2, 0:CH], start=False, stop=True)\
                  .then_inc(sum_ready, 1)

            for u in range(RING):
                sum_msgs(0, u, u > 1)
            with pe.Fori(1, LANE_ROWS // RING) as i:
                for u in range(RING):
                    sum_msgs(i, u, True)
            pe.wait_ge(acc_ready, LANE_ROWS)
            pe.wait_ge(hsa_in, 16)
            end = [acc[:, RING - 1, n * P:(n + 1) * P] for n in range(2)] + [hst[:, n * P:(n + 1) * P] for n in range(2)]
            turn_all([(banks[2][:, n * P:(n + 1) * P], e) for n, e in enumerate(end)])
            pe.wait_ge(small_in, 6)
            turn_all([(banks[2][:, n * P:(n + 1) * P], join[:, 2 + n, :]) for n in range(2)])

            def turn_agg(b, u, warm):
                pe.wait_ge(agg_add, b + 1)
                if warm:
                    pe.wait_ge(agg_cp, b - 1)
                for h in range(2):
                    last = pe.transpose(banks[2 + u][:, h * P:(h + 1) * P], xn[:, u, h * P:(h + 1) * P], ident[:, :])
                last.then_inc(agg_tr, 1)

            turn_agg(0, 0, False)
            turn_agg(1, 1, False)
            with pe.Fori(1, NB // 2) as i:
                for u in range(2):
                    turn_agg(2 * i + u, u, True)

            def dense1(n, u, warm):
                for m in range(4):
                    if warm:
                        pe.wait_ge(y1_ev, 4 * n + m - 7)
                    for h in range(2):
                        last = pe.matmul(banks[4 * u + m][:, 0:CCOLS], w1_sb[:, h, m * P:(m + 1) * P],
                                         hT[:, h, bass.ds(n * CCOLS, CCOLS)], start=(h == 0), stop=(h == 1))
                    last.then_inc(y1_mm, 1)

            pe.wait_ge(agg_cp, NB)
            dense1(0, 0, False)
            dense1(1, 1, False)
            with pe.Fori(1, NCHUNK // 2) as i:
                for u in range(2):
                    dense1(2 * i + u, u, True)

            def dense2(n, u, warm):
                pe.wait_ge(y1_act, n + 1)
                if warm:
                    pe.wait_ge(y2_ev, n - 1)
                for m in range(2):
                    for h in range(4):
                        last = pe.matmul(banks[2 * u + m][:, 0:CCOLS], w2_sb[:, h, m * P:(m + 1) * P],
                                         y1[:, h, bass.ds(n * CCOLS, CCOLS)], start=(h == 0), stop=(h == 3))
                last.then_inc(y2_mm, 1)

            dense2(0, 0, False)
            dense2(1, 1, False)
            with pe.Fori(1, NCHUNK // 2) as i:
                for u in range(2):
                    dense2(2 * i + u, u, True)
            for n in range(2):
                pe.wait_ge(small_in, 7 + n)
                pe.matmul(banks[6][:, 2 * n:2 * n + 2], ones[:, :], gn[:, 3 * n, :], start=True, stop=True)\
                  .then_inc(small_out, 1)

            def turn_out(b, u, warm):
                pe.wait_ge(out_aff, b + 1)
                if warm:
                    pe.wait_ge(out_add, b - 1)
                for h in range(2):
                    last = pe.transpose(banks[u][0:NP, h * P:(h + 1) * P], xT[:, u, h, 0:NP], ident[:, :])
                last.then_inc(out_tr, 1)

            turn_out(0, 0, False)
            turn_out(1, 1, False)
            with pe.Fori(1, NB // 2) as i:
                for u in range(2):
                    turn_out(2 * i + u, u, True)

        @block.vector
        def _(v):
            count = [0]

            def step(ins):
                count[0] += 1
                ins.then_inc(dve, 1)
                v.wait_ge(dve, count[0])

            def bc_last(a, n):
                return a[:, :, None].to_broadcast([P, a.shape[1], n])

            def bc_mid(a, n):
                return a[:, None, :].to_broadcast([P, n, a.shape[1]])

            step(v.memset(eps[:, :], EPS))
            v.wait_ge(dst_in, 16)
            v.tensor_copy(dlast_sb, dst_sb.rearrange("p (b n) -> p b n", n=BLK)[:, :, BLK - 1]).then_inc(dstf_done, 1)
            v.tensor_copy(dstf_sb, dst_sb).then_inc(dstf_done, 1)

            def ln_stats(t, n):
                with v.Fori(0, NB) as b:
                    v.bn_stats(stats[:, b, :], t[:, b, :]).then_inc(bnst, 1)
                v.wait_ge(bnst, n * NB)
                for b in range(NB):
                    last = v.bn_aggr(mv[:, b, :], stats[:, b, :])
                last.then_inc(ln_var, 1)

            def ln_scale(n):
                v.wait_ge(ln_std, n)
                step(v.reciprocal(rstd[:, :], rstd[:, :]))
                v.scalar_tensor_tensor(out=nmr[:, :], in0=mv[:, :, 0], scalar=-1.0, in1=rstd[:, :],
                                       op0=ALU.mult, op1=ALU.mult).then_inc(ln_norm, 1)

            v.wait_ge(x_in, 16)
            ln_stats(xs, 1)
            ln_scale(1)
            v.wait_ge(src_in, 16)
            for d in range(4):
                v.tensor_copy(src4_sb.rearrange("p (w d s) -> p w d s", d=4, s=WIN)[:, :, d, :],
                              src_sb[:, d * WIN:(d + LANE_WIN) * WIN].rearrange("p (w s) -> p w s", s=WIN))\
                 .then_inc(src4_done, 1)
            v.wait_ge(iotas, 3)
            step(v.tensor_copy(nid[:, :], nid_i[:, :]))
            v.wait_ge(blk_in, 16)
            step(v.tensor_tensor(cmp1, bc_mid(blk_sb, NB + 1), bc_last(nid, NBLK), ALU.is_lt))
            step(v.tensor_reduce(cnt[:, :], cmp1, AX.X, ALU.add))
            step(v.tensor_scalar(cnt[:, :], cnt[:, :], float(NBLK - 1), None, ALU.min))
            v.tensor_copy(blk_i[:, :], cnt[:, :]).then_inc(blk_done, 1)
            v.wait_ge(h_ready, NB)
            ln_stats(hs, 2)
            ln_scale(2)
            v.wait_ge(blk_gathered, 16 * (NB + 1))
            step(v.tensor_tensor(dblk, dblk, bc_last(nid, BLK), ALU.is_lt))
            step(v.tensor_reduce(start[:, :], dblk, AX.X, ALU.add))
            step(v.scalar_tensor_tensor(out=start[:, :], in0=cnt[:, :], scalar=float(BLK), in1=start[:, :],
                                        op0=ALU.mult, op1=ALU.add))
            step(v.tensor_copy(n_i[:, 0, :], start[:, :]))
            step(v.tensor_scalar(n_i[:, 1, :], start[:, :], float(WIN - 1), None, ALU.add))
            step(v.tensor_scalar(n_i[:, :, :], n_i[:, :, :], 3, None, ALU.arith_shift_right))
            step(v.tensor_copy(s3[:, :, :], n_i[:, :, :]))
            st, en = start[:, 0:NB], start[:, 1:NB + 1]
            step(v.tensor_tensor(has[:, :], en, st, ALU.is_gt))
            step(v.tensor_tensor(nrow[:, :], s3[:, 1, 1:NB + 1], s3[:, 0, 0:NB], ALU.subtract))
            step(v.tensor_tensor(nrow[:, :], nrow[:, :], has[:, :], ALU.mult))
            v.wait_ge(memsets, 1)
            v.tensor_tensor_scan(incl[:, :], nrow[:, :], zeros[:, 0:NB], 0.0, ALU.add, ALU.add).then_inc(small_in, 1)
            v.wait_ge(small_out, 1)
            step(v.tensor_copy(offs[:, :], banks[6][:, 0:2]))
            step(v.scalar_tensor_tensor(out=rs[:, :], in0=incl[:, :], scalar=offs[:, 0:1], in1=nrow[:, :],
                                        op0=ALU.add, op1=ALU.subtract))
            step(v.tensor_scalar(nt[:, 0, :], has[:, :], -FAR, FAR, ALU.mult, ALU.add))
            step(v.tensor_tensor(nt[:, 0, :], nt[:, 0, :], rs[:, :], ALU.add))
            step(v.tensor_copy(sidx[:, :], nt[:, 0, :]))
            step(v.tensor_copy(mk[:, :, 0], st))
            step(v.tensor_copy(mk[:, :, 1], en))
            v.tensor_tensor(mk[:, :, 2], rs[:, :], s3[:, 0, 0:NB], ALU.subtract).then_inc(node_done, 1)
            last_row, lane_f, lane_l, t = (nt[:, n, :] for n in range(4))
            step(v.scalar_tensor_tensor(out=last_row, in0=rs[:, :], scalar=-1.0, in1=nrow[:, :], op0=ALU.add, op1=ALU.add))
            middle = (LANE_ROWS - 1) / 2
            step(v.tensor_scalar(lane_i[:, 0, :], rs[:, :], -middle, 1.0 / LANE_ROWS, ALU.add, ALU.mult))
            step(v.tensor_scalar(lane_i[:, 1, :], last_row, -middle, 1.0 / LANE_ROWS, ALU.add, ALU.mult))
            step(v.tensor_copy(nt[:, 1:3, :], lane_i[:, :, :]))
            step(v.scalar_tensor_tensor(out=t, in0=lane_l, scalar=float(ROWS), in1=last_row, op0=ALU.add, op1=ALU.subtract))
            step(v.tensor_tensor(lane_f, lane_l, lane_f, ALU.is_gt))
            step(v.tensor_tensor(t, t, lane_f, ALU.mult))
            step(v.tensor_tensor(t, t, last_row, ALU.add))
            step(v.tensor_tensor(t, t, has[:, :], ALU.mult))
            step(v.tensor_copy(fidx[:, :], t))

            v.wait_ge(marks_in, 16)
            for f in range(3):
                step(v.tensor_tensor_scan(fld[:, f, :], mkr[:, :, f], mkr[:, :, f], 0.0, ALU.max, ALU.max))
            v.tensor_copy(l3[:, :], fld[:, :, LANE_ROWS - 1]).then_inc(small_in, 1)
            v.wait_ge(small_out, 2)
            step(v.tensor_copy(l3t[:, 0, :], banks[6][0:3, P:2 * P]))
            step(v.memset(l3t[:, 1, :], 0.0))
            v.tensor_tensor_scan(l3t[:, 1, 1:P], l3t[:, 0, 0:P - 1], l3t[:, 0, 0:P - 1], 0.0, ALU.max, ALU.max)\
             .then_inc(small_in, 1)
            v.wait_ge(small_out, 3)
            step(v.tensor_copy(l3[:, :], banks[6][:, 2 * P:2 * P + 3]))
            for f in range(3):
                step(v.tensor_scalar(fld[:, f, :], fld[:, f, :], l3[:, f:f + 1], None, ALU.max))
            step(v.tensor_copy(row[:, :], row_i[:, :]))
            step(v.tensor_tensor(win, row[:, :], fld[:, 2, :], ALU.subtract))
            step(v.tensor_scalar(t0, win, float(WIN), None, ALU.mult))
            step(v.tensor_scalar(winc, win, float(NWIN - 1), None, ALU.min))
            v.tensor_copy(win_i[:, :], winc).then_inc(win_done, 1)
            step(v.tensor_copy(lane_j[:, 0:1], fld[:, 0, 0:1]))
            step(v.tensor_scalar(lane_j[:, 1:2], fld[:, 1, 0:1], -1.0, None, ALU.add))
            step(v.tensor_scalar(lane_j[:, 0:2], lane_j[:, 0:2], 3, None, ALU.arith_shift_right))
            step(v.tensor_copy(lane[:, 0:2], lane_j[:, 0:2]))
            step(v.tensor_scalar(lane[:, 0:2], lane[:, 0:2], fld[:, 2, 0:1], None, ALU.add))
            step(v.tensor_tensor(lane[:, 1:2], lane[:, 1:2], row[:, LANE_ROWS - 1:LANE_ROWS], ALU.min))
            v.tensor_copy(lane_j[:, 0:2], lane[:, 0:2]).then_inc(win_done, 1)
            step(v.tensor_tensor(kcont[:, :], t0, fld[:, 0, :], ALU.is_gt))
            step(v.tensor_scalar(t1, row[:, :], offs[:, 1:2], None, ALU.is_ge))
            step(v.tensor_scalar(brk[:, :], kcont[:, :], -1.0, 1.0, ALU.mult, ALU.add))
            step(v.tensor_tensor(brk[:, :], brk[:, :], t1, ALU.max))
            step(v.tensor_scalar(acont[:, :], brk[:, :], -1.0, 1.0, ALU.mult, ALU.add))
            step(v.tensor_scalar(mneg[:, :], brk[:, :], NEG, None, ALU.mult))
            step(v.tensor_reduce(lane[:, 2:3], brk[:, :], AX.X, ALU.max))
            step(v.tensor_scalar(lane[:, 3:4], lane[:, 2:3], -1.0, 1.0, ALU.mult, ALU.add))
            v.tensor_scalar(xT[:, 0, 0, :], ident[:, :], lane[:, 3:4], None, ALU.mult).then_inc(small_in, 1)
            v.wait_ge(small_out, 4)
            step(v.tensor_copy(flagb[:, 0, :], banks[7][:, 0:P]))
            step(v.tensor_scalar(flagb[:, 1, :], flagb[:, 0, :], -NEG, NEG, ALU.mult, ALU.add))
            step(v.tensor_copy(wslot[:, :], w_i[:, :]))
            step(v.tensor_tensor(valid, bc_last(t0, WIN), bc_mid(wslot, LANE_ROWS), ALU.add))
            step(v.tensor_tensor(srow, valid, bc_last(fld[:, 0, :], WIN), ALU.is_ge))
            step(v.tensor_tensor(valid, valid, bc_last(fld[:, 1, :], WIN), ALU.is_lt))
            step(v.tensor_tensor(valid, valid, srow, ALU.mult))
            step(v.tensor_scalar(sneg[:, :, :], valid, -NEG, NEG, ALU.mult, ALU.add))
            v.wait_ge(src4_gathered, 16 * GROUPS)
            s4 = src4_row.rearrange("p (g d s) -> p g d s", d=4, s=WIN)
            wg = winc.rearrange("p (g j) -> p g j", j=4)
            sg = srow.rearrange("p (g j) w -> p g j w", j=4)
            step(v.tensor_copy(sg[:, :, 0, :], s4[:, :, 0, :]))
            for j in range(1, 4):
                step(v.tensor_tensor(delta, wg[:, :, j], wg[:, :, 0], ALU.subtract))
                for d in range(j + 1):
                    step(v.scalar_tensor_tensor(out=seltmp if d else sg[:, :, j, :], in0=bc_last(delta, WIN),
                                                scalar=float(d), in1=s4[:, :, d, :], op0=ALU.is_equal, op1=ALU.mult))
                    if d:
                        step(v.tensor_tensor(sg[:, :, j, :], sg[:, :, j, :], seltmp, ALU.add))
            step(v.tensor_tensor(srow, srow, valid, ALU.mult))
            step(v.tensor_reduce(fmx, srow, AX.X, ALU.max))
            step(v.tensor_scalar(valid, valid, -1.0, 1.0, ALU.mult, ALU.add))
            step(v.tensor_tensor(valid, valid, bc_last(fmx, WIN), ALU.mult))
            step(v.tensor_tensor(srow, srow, valid, ALU.add))
            step(v.tensor_copy(pack[:, 0:LANE_ROWS, 0:WIN], srow))
            step(v.tensor_copy(pack[:, 0:LANE_ROWS, WIN], winc))
            v.memset(pack[:, LANE_ROWS:LANE_ROWS + RING, :], 0).then_inc(qidx_done, 1)
            v.wait_ge(k_out, 16 * NB)
            step(v.memset(top[:, RING - 1, :], 0.0))
            step(v.memset(zs[:, RING - 1, :], 0.0))
            v.wait_ge(kinit, 16)

            def logits(i, u, warm):
                t = 32 * i + 8 * u
                h = u % 2
                v.wait_ge(km_in[u], 16 * i + 16)
                if warm:
                    v.wait_ge(a_step, t)
                v.scalar_tensor_tensor(out=kcur, in0=kcur, scalar=kcont[:, bass.ds(4 * i + u, 1)], in1=km[:, u, :],
                                       op0=ALU.mult, op1=ALU.add).then_inc(a_step, 1)
                v.wait_ge(qv_in[u], 16 * WIN * (i + 1))
                v.wait_ge(a_step, t + 1)
                l = qv[:, u, :, 0, :]
                v.tensor_tensor(l, l, bc_mid(kcur, WIN), ALU.mult).then_inc(a_step, 1)
                v.wait_ge(a_step, t + 2)
                v.tensor_tensor(mx1, l[:, 0:4, :], l[:, 4:8, :], ALU.max).then_inc(a_step, 1)
                v.wait_ge(a_step, t + 3)
                v.tensor_tensor(mx2, mx1[:, 0:2, :], mx1[:, 2:4, :], ALU.max).then_inc(a_step, 1)
                v.wait_ge(a_step, t + 4)
                v.tensor_tensor(mx3, mx2[:, 0, :], mx2[:, 1, :], ALU.max).then_inc(a_step, 1)
                v.wait_ge(a_step, t + 5)
                if not (isinstance(i, int) and i == 0):
                    v.wait_ge(hist_out[u], 32 * i)
                before, now = top[:, (u - 1) % RING, :], top[:, u, :]
                reset = mneg[:, bass.ds(4 * i + u, 1)]
                v.scalar_tensor_tensor(out=now, in0=before, scalar=reset, in1=mx3, op0=ALU.add, op1=ALU.max)\
                 .then_inc(a_step, 1)
                v.wait_ge(a_step, t + 6)
                if warm and not (isinstance(i, int) and i == 0 and u < 2):
                    v.wait_ge(weighted, 8 * i + 2 * u - 2)
                v.scalar_tensor_tensor(out=alpha[:, h, :], in0=before, scalar=reset, in1=now,
                                       op0=ALU.add, op1=ALU.subtract).then_inc(a_step, 1)
                v.tensor_tensor(l, l, bc_mid(now, WIN), ALU.subtract).then_inc(a_step, 1)

            def weigh(i, u):
                h = u % 2
                early = isinstance(i, int) and i == 0
                v.wait_ge(exp_ready, 4 * i + u + 1)
                v.tensor_tensor(qv[:, u, :, 1, :], qv[:, u, :, 1, :], qv[:, u, :, 0, :], ALU.mult).then_inc(weighted, 1)
                if not (early and u == 0):
                    v.wait_ge(state_ready, 4 * i + u)
                if not (early and u < 2):
                    v.wait_ge(psum_ready, 4 * i + u - 1)
                v.tensor_tensor(carry[:, h, :].rearrange("p (a c) -> p a c", a=2),
                                zs[:, (u - 1) % RING, :].rearrange("p (a c) -> p a c", a=2),
                                bc_mid(alpha[:, h, :], 2), ALU.mult).then_inc(weighted, 1)

            logits(0, 0, False)
            for u in range(1, RING):
                logits(0, u, True)
                weigh(0, u - 1)
            with v.Fori(1, LANE_ROWS // RING) as i:
                for u in range(RING):
                    logits(i, u, True)
                    weigh(i if u else i - 1, (u - 1) % RING)
            weigh(LANE_ROWS // RING - 1, RING - 1)

            v.wait_ge(small_out, 5)
            for n in range(3):
                step(v.tensor_copy(join[:, 4 * n:4 * n + 4, :].rearrange("p n c -> p (n c)"), banks[2 + n][:, :]))
            J = lambda n: join[:, n, :]

            def shifted(to, of):
                step(v.memset(to[:, 0:1], 0.0))
                step(v.tensor_copy(to[:, 1:P], of[:, 0:P - 1]))

            for h in range(2):
                tm, hm = J(h), J(6 + h)
                step(v.tensor_tensor_scan(J(12), flagb[:, 1, :], tm, 0.0, ALU.add, ALU.max))
                shifted(J(13), J(12))
                step(v.tensor_tensor(J(16), J(13), flagb[:, 1, :], ALU.add))
                step(v.tensor_tensor(J(16), J(16), J(12), ALU.subtract))
                step(v.tensor_tensor(J(17), tm, J(12), ALU.subtract))
                step(v.tensor_tensor(J(14), J(13), hm, ALU.max))
                step(v.tensor_tensor(J(18), J(13), J(14), ALU.subtract))
                v.tensor_tensor(J(19), hm, J(14), ALU.subtract).then_inc(join_arg, 1)
                v.wait_ge(join_exp, h + 1)
                for k in range(2):
                    step(v.tensor_tensor(J(15), J(2 + 2 * k + h), J(17), ALU.mult))
                    step(v.tensor_tensor_scan(J(20), J(16), J(15), 0.0, ALU.mult, ALU.add))
                    shifted(J(21), J(20))
                    step(v.tensor_tensor(J(22), J(21), J(18), ALU.mult))
                    step(v.tensor_tensor(J(23), J(8 + 2 * k + h), J(19), ALU.mult))
                    last = v.tensor_tensor(J(8 + 2 * k + h), J(22), J(23), ALU.add)
                    if (h, k) != (1, 1):
                        step(last)
            last.then_inc(small_in, 1)
            v.wait_ge(small_out, 6)
            v.tensor_copy(carry[:, 0, :], banks[2][:, :]).then_inc(join_done, 1)

            with v.Fori(0, NB // FRING) as i:
                for r in range(FRING):
                    n = 3 * FRING * i + 3 * r
                    v.wait_ge(fin_in[r], 16 * i + 16)
                    z, s = fin[:, r, 0:CH], fin[:, r, CH:2 * CH]
                    v.reciprocal(z, z).then_inc(fin_step, 1)
                    v.wait_ge(fin_step, n + 1)
                    v.tensor_tensor(s, s, z, ALU.mult).then_inc(fin_step, 1)
                    v.wait_ge(fin_step, n + 2)
                    v.scalar_tensor_tensor(out=xs[:, FRING * i + r, :], in0=s, scalar=has[:, bass.ds(FRING * i + r, 1)],
                                           in1=xs[:, FRING * i + r, :], op0=ALU.mult, op1=ALU.add).then_inc(fin_step, 1)
            v.wait_ge(fin_step, 3 * NB)
            ln_stats(xs, 3)
            ln_scale(3)
            step(v.memset(acc[:, RING - 1, :], 0.0))
            v.wait_ge(h_ready, 2 * NB)
            v.tensor_tensor(xs[:, :, :], xs[:, :, :], hs[:, :, :], ALU.add).then_inc(xh_done, 1)

            def add_edges(i, u):
                v.wait_ge(msg_in[u], 16 * (WIN + 1) * (i + 1))
                if not (isinstance(i, int) and i == 0):
                    v.wait_ge(hista_out[u], 16 * i)
                m = hmsg[:, u, :, :].rearrange("p w c -> p (w c)")
                v.tensor_tensor(m, m, eat[:, u, :], ALU.add).then_inc(added, 1)

            def carry_sum(i, u):
                early = isinstance(i, int) and i == 0
                if not (early and u == 0):
                    v.wait_ge(acc_ready, 4 * i + u)
                if not (early and u < 2):
                    v.wait_ge(sum_ready, 4 * i + u - 1)
                v.tensor_scalar(carry[:, u % 2, 0:CH], acc[:, (u - 1) % RING, :], acont[:, bass.ds(4 * i + u, 1)], None,
                                ALU.mult).then_inc(carried, 1)

            v.wait_ge(join_out, 16)
            add_edges(0, 0)
            for u in range(1, RING):
                add_edges(0, u)
                carry_sum(0, u - 1)
            with v.Fori(1, LANE_ROWS // RING) as i:
                for u in range(RING):
                    add_edges(i, u)
                    carry_sum(i if u else i - 1, (u - 1) % RING)
            carry_sum(LANE_ROWS // RING - 1, RING - 1)
            v.wait_ge(small_out, 7)
            step(v.tensor_copy(join[:, 0:4, :].rearrange("p n c -> p (n c)"), banks[2][:, :]))
            for h in range(2):
                step(v.tensor_tensor_scan(J(12), flagb[:, 0, :], J(h), 0.0, ALU.mult, ALU.add))
                shifted(J(13), J(12))
                last = v.tensor_tensor(J(2 + h), J(2 + h), J(13), ALU.add)
                if h == 0:
                    step(last)
            last.then_inc(small_in, 1)
            v.wait_ge(small_out, 8)
            v.tensor_copy(carry[:, 0, 0:CH], banks[2][:, 0:CH]).then_inc(join_done, 1)

            def add_agg(i, b, early):
                v.wait_ge(agg_in[b % FRING], 32 * i + 16 * (b // FRING) + 16)
                if not (early and b < 2):
                    v.wait_ge(agg_tr, 10 * i + b - 1)
                v.scalar_tensor_tensor(out=xn[:, b % 2, :], in0=fin[:, b % FRING, 0:CH], scalar=has[:, bass.ds(10 * i + b, 1)],
                                       in1=hs[:, 10 * i + b, :], op0=ALU.mult, op1=ALU.add).then_inc(agg_add, 1)

            for b in range(10):
                add_agg(0, b, True)
            with v.Fori(1, NB // 10) as i:
                for b in range(10):
                    add_agg(i, b, False)

            with v.Fori(0, NCHUNK) as n:
                for m in range(4):
                    v.wait_ge(y1_ev, 4 * n + m + 1)
                    v.bn_stats(stats[:, n + m * NCHUNK, :], y1[:, m, bass.ds(n * CCOLS, CCOLS)]).then_inc(y1_bn, 1)
            v.wait_ge(y1_bn, 4 * NCHUNK)
            for m in range(4):
                last = v.bn_aggr(mvd[:, m, :], stats[:, m * NCHUNK:(m + 1) * NCHUNK, :].rearrange("p n s -> p (n s)"))
            step(last)
            v.tensor_copy(bn[:, 0, :], mvd[:, :, 1]).then_inc(bn_var, 1)
            v.wait_ge(bn_std, 1)
            step(v.reciprocal(bn[:, 0, :], bn[:, 0, :]))
            step(v.tensor_tensor(bn[:, 1, :], bn[:, 0, :], pvs("bn_g"), ALU.mult))
            step(v.tensor_tensor(bn[:, 2, :], bn[:, 1, :], mvd[:, :, 0], ALU.mult))
            v.tensor_tensor(bn[:, 2, :], pvs("bn_b"), bn[:, 2, :], ALU.subtract).then_inc(bn_ready, 1)

            with v.Fori(0, NCHUNK) as n:
                v.wait_ge(y2_ev, n + 1)
                for m in range(2):
                    v.bn_stats(stats[:, n + m * NCHUNK, :], y2[:, m, bass.ds(n * CCOLS, CCOLS)]).then_inc(y2_bn, 1)
            v.wait_ge(y2_bn, 2 * NCHUNK)
            for m in range(2):
                last = v.bn_aggr(mvd[:, m, :], stats[:, m * NCHUNK:(m + 1) * NCHUNK, :].rearrange("p n s -> p (n s)"))
            step(last)
            G = lambda n: gn[:, n, :]
            mean, var = mvd[:, 0:2, 0], mvd[:, 0:2, 1]
            v.tensor_copy(G(0), mean).then_inc(small_in, 1)
            v.wait_ge(small_out, 9)
            step(v.tensor_reduce(gn[:, 1, 0:1], banks[6][:, 0:2], AX.X, ALU.add))
            step(v.tensor_scalar(gn[:, 1, 0:1], gn[:, 1, 0:1], 1.0 / CH, None, ALU.mult))
            gm = gn[:, 1, 0:1]
            step(v.tensor_scalar(G(2), mean, gm, None, ALU.subtract))
            step(v.tensor_tensor(G(3), G(2), G(2), ALU.mult))
            v.tensor_tensor(G(3), G(3), var, ALU.add).then_inc(small_in, 1)
            v.wait_ge(small_out, 10)
            step(v.tensor_reduce(gn[:, 4, 0:1], banks[6][:, 2:4], AX.X, ALU.add))
            step(v.memset(G(12), 0.0))
            v.tensor_scalar(G(12), G(12), gn[:, 4, 0:1], 1.0 / CH, ALU.add, ALU.mult).then_inc(g_var, 1)
            v.wait_ge(g_std, 1)
            step(v.reciprocal(G(12), G(12)))
            step(v.tensor_tensor(G(5), pvs("ln_w"), G(12), ALU.mult))
            step(v.tensor_scalar(G(6), G(5), gm, None, ALU.mult))
            step(v.tensor_tensor(G(6), pvs("ln_b"), G(6), ALU.subtract))
            step(v.tensor_tensor(G(7), G(5), mean, ALU.mult))
            step(v.tensor_tensor(G(7), G(7), G(6), ALU.add))
            step(v.tensor_tensor(G(8), G(7), pvs("gn_ms"), ALU.mult))
            step(v.tensor_tensor(G(9), G(7), G(8), ALU.subtract))
            step(v.tensor_tensor(G(9), G(9), G(9), ALU.mult))
            step(v.tensor_tensor(G(10), G(5), G(5), ALU.mult))
            step(v.tensor_tensor(G(10), G(10), var, ALU.mult))
            v.tensor_tensor(G(12), G(10), G(9), ALU.add).then_inc(g_var, 1)
            v.wait_ge(g_std, 2)
            step(v.reciprocal(G(12), G(12)))
            step(v.tensor_tensor(G(11), pvs("gn_w"), G(12), ALU.mult))
            step(v.tensor_tensor(G(13), G(5), G(11), ALU.mult))
            step(v.tensor_tensor(G(14), G(6), G(8), ALU.subtract))
            step(v.tensor_tensor(G(14), G(14), G(11), ALU.mult))
            v.tensor_tensor(G(14), G(14), pvs("gn_b"), ALU.add).then_inc(g_ready, 1)

            v.wait_ge(xh_done, 1)
            with v.Fori(0, NB // 2) as i:
                for u in range(2):
                    v.wait_ge(out_tr, 2 * i + u + 1)
                    v.tensor_tensor(xs[0:NP, 2 * i + u, :], banks[u][0:NP, 0:CH], xs[0:NP, 2 * i + u, :], ALU.add)\
                     .then_inc(out_add, 1)


def kernel(x, src, dst, edge_attr_256, L0_gnn_Wqkv, L0_gnn_gamma, L0_gnn_beta, L1_gnn_W1, L1_gnn_b1, L1_gnn_bn_gamma,
           L1_gnn_bn_beta, L1_gnn_W2, L1_gnn_b2, L1_gnn_ln_w, L1_gnn_ln_b, L1_gnn_gn_w, L1_gnn_gn_b, L1_gnn_gn_ms):
    import concourse.bacc as bacc
    from concourse.bass_utils import run_bass_kernel_spmd

    def padded(a, rows):
        return np.concatenate([a, np.zeros((rows - a.shape[0],) + a.shape[1:], a.dtype)])

    a = {}
    a["x"] = padded(np.asarray(x), PAD_NODES)
    flat = padded(np.asarray(src), (P * LANE_WIN + 3) * WIN)
    a["src"] = np.stack([flat[p * LANE_WIN * WIN:(p * LANE_WIN + LANE_WIN + 3) * WIN] for p in range(P)])
    a["dst"] = np.asarray(dst)
    a["edge"] = padded(np.asarray(edge_attr_256), NWIN * WIN).reshape(NWIN, WIN * CH)
    w = np.asarray(L0_gnn_Wqkv).reshape(2, P, 3, CH).transpose(1, 0, 2, 3)
    a["wqkv"] = np.ascontiguousarray(np.stack([w[:, :, 0], w[:, :, 2], w[:, :, 1]], 2).reshape(P, 2, 3 * CH))
    a["w1"] = np.ascontiguousarray(np.asarray(L1_gnn_W1).reshape(2, P, HID).transpose(1, 0, 2))
    a["w2"] = np.ascontiguousarray(np.asarray(L1_gnn_W2).reshape(4, P, CH).transpose(1, 0, 2))
    vectors = [L0_gnn_gamma, L0_gnn_beta, L1_gnn_b1, L1_gnn_bn_gamma, L1_gnn_bn_beta, L1_gnn_b2, L1_gnn_ln_w,
               L1_gnn_ln_b, L1_gnn_gn_w, L1_gnn_gn_b, L1_gnn_gn_ms]
    a["params"] = np.ascontiguousarray(np.concatenate([np.asarray(t).reshape(-1, P).T for t in vectors], 1))

    nc = bacc.Bacc("TRN2", target_bir_lowering=False, num_devices=1)
    args = [nc.dram_tensor(f"in_{n}", t.shape, mybir.dt.from_np(t.dtype), kind="ExternalInput").ap() for n, t in a.items()]
    out = nc.dram_tensor("out_0", (NODES, CH), F32, kind="ExternalOutput").ap()
    build(nc, *args, out)
    r = run_bass_kernel_spmd(nc, [{f"in_{n}": t for n, t in a.items()}], core_ids=[0])
    return r.results[0]["out_0"]
```

```python
from contextlib import ExitStack

import numpy as np
import concourse.bass as bass
from concourse import mybir

F32 = mybir.dt.float32
I32 = mybir.dt.int32
ALU = mybir.AluOpType
ACT = mybir.ActivationFunctionType
AX = mybir.AxisListType

P = 128
NODES, EDGES, CH, HID = 3750, 123750, 256, 512
NB = 30
NP = NODES // NB
PAD_NODES = P * NB
WIN = 8
NWIN = -(-EDGES // WIN)
LANE_WIN = -(-NWIN // P)
LANE_ROWS = -(-(NWIN + NODES) // (4 * P)) * 4
ROWS = P * LANE_ROWS
GROUPS = LANE_ROWS // 4
BLK = 375
NBLK = EDGES // BLK
DPART = 110
NCHUNK = 10
CCOLS = NODES // NCHUNK
FAR = 1.0e6
LN_CHUNK = NB // 3
SCH = 8
PREFIX_AT, FIELDS_AT = 6, 12
NF = 4
NEG = -1.0e30
EPS = 1e-5
SCALE = CH ** -0.5
RING = 4
FRING = 5

PARAMS = [("gamma", 2), ("beta", 2), ("b1", 4), ("bn_g", 4), ("bn_b", 4), ("b2", 2), ("ln_w", 2),
          ("ln_b", 2), ("gn_w", 2), ("gn_b", 2), ("gn_ms", 2)]
NPAR = sum(n for _, n in PARAMS)


def build(nc, x, src, dst, edge, wqkv, w1, w2, params, out):
    assert LANE_ROWS % RING == 0 and NBLK * BLK == EDGES and NP * NB == NODES and NB % 2 == 0
    with ExitStack() as ctx:
        def sb(name, shape, dt=F32):
            return ctx.enter_context(nc.sbuf_tensor(name, shape, dt))

        def sem(name):
            return ctx.enter_context(nc.semaphore(name))

        def dram(name, shape, dt=F32):
            return nc.dram_tensor(name, shape, dt, kind="Internal").ap()

        dst_f = dram("dst_f", (NBLK, BLK))
        blk_last = dram("blk_last", (NBLK,))
        src4 = dram("src4", (P * LANE_WIN, 4 * WIN))
        marks = dram("marks", (ROWS, NF))
        k_tab = dram("k_tab", (PAD_NODES, CH))
        qv_tab = dram("qv_tab", (PAD_NODES, 2 * CH))
        h_tab = dram("h_tab", (PAD_NODES, CH))
        hist_m = dram("hist_m", (ROWS, CH))
        hist_zs = dram("hist_zs", (ROWS + P, 2 * CH))
        hist_a = dram("hist_a", (ROWS + P, CH))

        xs = sb("xs", [P, NB, CH])
        hs = sb("hs", [P, NB, CH])
        ks = sb("ks", [P, NB * CH])
        ring = sb("ring", [P, RING * WIN * 2 * CH])
        ident = sb("ident", [P, P])
        upper = sb("upper", [P, P])
        ones = sb("ones", [P, P])
        zeros = sb("zeros", [P, LANE_ROWS * NF])
        wq_sb = sb("wq_sb", [P, 2, 3 * CH])
        w1_sb = sb("w1_sb", [P, 2, HID])
        w2_sb = sb("w2_sb", [P, 4, CH])
        par = sb("par", [P, NPAR])
        stats = sb("stats", [P, 4 * NCHUNK, 6])
        mv = sb("mv", [P, NB, 2])
        rstd = sb("rstd", [P, NB])
        nmr = sb("nmr", [P, NB])
        eps = sb("eps", [P, 1])
        xn = sb("xn", [P, 2, CH])
        xT = sb("xT", [P, 2, 2, P])
        stage = sb("stage", [P, 2, 2 * CH])

        nid_i = sb("nid_i", [P, NB + 1], I32)
        nid = sb("nid", [P, NB + 1])
        cnt = sb("cnt", [P, NB + 1])
        blk_i = sb("blk_i", [P, NB + 1], I32)
        start = sb("start", [P, NB + 1])
        n_i = sb("n_i", [P, 2, NB + 1], I32)
        s3 = sb("s3", [P, 2, NB + 1])
        has = sb("has", [P, NB])
        nrow = sb("nrow", [P, NB])
        incl = sb("incl", [P, NB])
        rs = sb("rs", [P, NB])
        nt = sb("nt", [P, 4, NB])
        sidx = sb("sidx", [P, NB], I32)
        fidx = sb("fidx", [P, NB], I32)
        lane_i = sb("lane_i", [P, 2, NB], I32)
        mk = sb("mk", [P, NB, NF])
        offs = sb("offs", [P, 2])

        row_i = sb("row_i", [P, LANE_ROWS], I32)
        row = sb("row", [P, LANE_ROWS])
        fld = sb("fld", [P, NF, LANE_ROWS])
        win_i = sb("win_i", [P, LANE_ROWS], I32)
        brk = sb("brk", [P, LANE_ROWS])
        acont = sb("acont", [P, LANE_ROWS])
        mneg = sb("mneg", [P, LANE_ROWS])
        w_i = sb("w_i", [P, WIN], I32)
        wslot = sb("wslot", [P, WIN])
        sneg = sb("sneg", [P, LANE_ROWS, WIN])
        pack = sb("pack", [P, LANE_ROWS + RING, WIN + 2], I32)
        idx = sb("idx", [P, RING, WIN + 2], I32)
        bn = sb("bn", [P, 3, 4])
        mvd = sb("mvd", [P, 4, 2])
        gn = sb("gn", [P, 15, 2])
        l3 = sb("l3", [P, NF])
        l3t = sb("l3t", [NF, 2, P])
        lane = sb("lane", [P, 6])
        lane_j = sb("lane_j", [P, 3], I32)
        flagd = sb("flagd", [P, P])
        flagb = sb("flagb", [P, 2, P])

        banks = [ctx.enter_context(nc.psum_tensor(f"bank{i}", [P, 512], F32)) for i in range(8)]

        cmp1 = ks[:, 0:SCH * NBLK].rearrange("p (b k) -> p b k", b=SCH)
        dblk = ring[:, 0:(NB + 1) * BLK].rearrange("p (b k) -> p b k", b=NB + 1)
        dst_sb = ring[0:DPART, 1024:1024 + EDGES // DPART].bitcast(I32)
        dstf_sb = ring[0:DPART, 4096:4096 + EDGES // DPART]
        dlast_sb = ring[0:DPART, 6144:6144 + NBLK // DPART]
        src4_sb = ring[:, 12000:12000 + LANE_WIN * 4 * WIN]
        blk_sb = ring[:, 15872:15872 + NBLK]
        src_sb = ks[:, 4096:4096 + (LANE_WIN + 3) * WIN].bitcast(I32)
        LW = LANE_ROWS * WIN
        hsf = hs[:, :, :].rearrange("p b c -> p (b c)")
        valid = hsf[:, 0:LW].rearrange("p (r w) -> p r w", w=WIN)
        srow = hsf[:, LW:2 * LW].rearrange("p (r w) -> p r w", w=WIN)
        src4_row = hsf[:, 2 * LW:2 * LW + GROUPS * 4 * WIN]
        seltmp = hsf[:, 3 * LW:3 * LW + GROUPS * WIN].rearrange("p (g w) -> p g w", w=WIN)
        tmp0 = 4 * LW
        mkr = hsf[:, tmp0:tmp0 + NF * LANE_ROWS].rearrange("p (r f) -> p r f", f=NF)
        win, winc, t0, t1, fmx, delta = (hsf[:, tmp0 + (NF + n) * LANE_ROWS:tmp0 + (NF + 1 + n) * LANE_ROWS] for n in range(6))
        delta = delta[:, 0:GROUPS]
        at = [0]

        def carve(*shape):
            n = int(np.prod(shape))
            v = ks[:, at[0]:at[0] + n]
            at[0] += n
            assert at[0] <= NB * CH
            return v if len(shape) == 1 else v.rearrange("p (a b) -> p a b", a=shape[0])

        kk = carve(RING, CH)
        mx1 = carve(4, CH)
        mx2 = carve(2, CH)
        mx3 = carve(CH)
        top = carve(RING, CH)
        zs = carve(RING, 2 * CH)
        alpha = carve(2, CH)
        carry = carve(2, 2 * CH)
        hst = mx1.rearrange("p a b -> p (a b)")
        acc = zs[:, :, 0:CH]
        qv = ring[:, :].rearrange("p (r w h c) -> p r w h c", r=RING, w=WIN, h=2)
        hmsg = ring[:, 0:RING * WIN * CH].rearrange("p (r w c) -> p r w c", r=RING, w=WIN)
        eat = ring[:, RING * WIN * CH:].rearrange("p (r n) -> p r n", r=RING)
        fin = ring[:, 0:FRING * 2 * CH].rearrange("p (r n) -> p r n", r=FRING)
        aggs = ring[:, 15104:15104 + FRING * CH].rearrange("p (r n) -> p r n", r=FRING)
        join = ring[:, 4096:4096 + 24 * P].rearrange("p (n c) -> p n c", c=P)
        y1 = ring[:, 0:4 * NODES].rearrange("p (m n) -> p m n", m=4)
        hT = ks[:, 0:2 * NODES].rearrange("p (m n) -> p m n", m=2)
        y2 = hT

        def pv(name, m):
            first = sum(w for _, w in PARAMS[:[n for n, _ in PARAMS].index(name)])
            return par[:, first + m:first + m + 1]

        def pvs(name):
            n = dict(PARAMS)[name]
            first = sum(w for _, w in PARAMS[:[k for k, _ in PARAMS].index(name)])
            return par[:, first:first + n]

        dst_in, src_in, w_in, par_in = (sem(n) for n in ("dst_in", "src_in", "w_in", "par_in"))
        x_in = [sem(f"x_in{c}") for c in range(3)]
        dstf_out, blk_in, src4_out, zero_m = (sem(n) for n in ("dstf_out", "blk_in", "src4_out", "zero_m"))
        consts0, consts, iotas, memsets = (sem(n) for n in ("consts0", "consts", "iotas", "memsets"))
        dve = sem("dve")
        bnst, aggr = sem("bnst"), sem("aggr")
        dstf_done, src4_done, blk_done, node_done, win_done, qidx_done = (
            sem(n) for n in ("dstf_done", "src4_done", "blk_done", "node_done", "win_done", "qidx_done"))
        blk_gathered = [sem(f"blk_gathered{c}") for c in range(-(-(NB + 1) // SCH))]
        marks_out, marks_in, k_out, src4_gathered = (sem(n) for n in ("marks_out", "marks_in", "k_out", "src4_gathered"))
        ln_var, ln_std, ln_norm = sem("ln_var"), sem("ln_std"), sem("ln_norm")
        h_ready, xn_ready, tr_ready, xT_ready, qkv_ready, qkv_evac = (
            sem(n) for n in ("h_ready", "xn_ready", "tr_ready", "xT_ready", "qkv_ready", "qkv_evac"))
        qv_out = [sem(f"qv_out{i}") for i in range(2)]
        small_in, small_out = sem("small_in"), sem("small_out")
        qv_in = [sem(f"qv_in{i}") for i in range(RING)]
        a_step, exp_ready, weighted, psum_ready, state_ready = (
            sem(n) for n in ("a_step", "exp_ready", "weighted", "psum_ready", "state_ready"))
        hist_out = [sem(f"hist_out{i}") for i in range(RING)]
        hst_in, join_done, join_out = sem("hst_in"), sem("join_done"), sem("join_out")
        join_arg, join_exp, idx_ready, gathering = (sem(n) for n in ("join_arg", "join_exp", "idx_ready", "gathering"))
        g_ready, xh_done = sem("g_ready"), sem("xh_done")
        fin_in, fin_step, fin_used = [sem(f"fin_in{i}") for i in range(FRING)], sem("fin_step"), sem("fin_used")
        h_out = sem("h_out")
        msg_in = [sem(f"msg_in{i}") for i in range(RING)]
        added, relued, carried, sum_ready, acc_ready = (
            sem(n) for n in ("added", "relued", "carried", "sum_ready", "acc_ready"))
        hista_out = [sem(f"hista_out{i}") for i in range(RING)]
        hsa_in, joina_out = sem("hsa_in"), sem("joina_out")
        agg_in, agg_add, agg_tr, agg_cp = [sem(f"agg_in{i}") for i in range(FRING)], sem("agg_add"), sem("agg_tr"), sem("agg_cp")
        y1_mm, y1_ev, y1_bn, bn_var, bn_std, bn_ready, y1_act = (
            sem(n) for n in ("y1_mm", "y1_ev", "y1_bn", "bn_var", "bn_std", "bn_ready", "y1_act"))
        y2_mm, y2_ev, y2_bn = sem("y2_mm"), sem("y2_ev"), sem("y2_bn")
        g_var, g_std, out_aff, out_tr, out_add, out_st = (
            sem(n) for n in ("g_var", "g_std", "out_aff", "out_tr", "out_add", "out_st"))

        spans = [range(b, min(b + SCH, NB + 1)) for b in range(0, NB + 1, SCH)]

        block = ctx.enter_context(nc.Block())
        lanes = lambda t, a: t[0:ROWS, :].rearrange("(p c) f -> p c f", p=P)[:, a, :]

        @block.sync
        def _(sp):
            sp.dma_start(dst_sb, dst.rearrange("(p n) -> p n", p=DPART)).then_inc(dst_in, 16)
            for c in range(3):
                part = slice(c * LN_CHUNK, (c + 1) * LN_CHUNK)
                sp.dma_start(xs[:, part, :], x.rearrange("(p b) c -> p b c", p=P)[:, part, :]).then_inc(x_in[c], 16)
            sp.dma_start(src_sb, src).then_inc(src_in, 16)
            sp.dma_start(par[:, :], params).then_inc(par_in, 16)
            sp.dma_start(wq_sb[:, :, :], wqkv).then_inc(w_in, 16)
            sp.dma_start(w1_sb[:, :, :], w1).then_inc(w_in, 16)
            sp.dma_start(w2_sb[:, :, :], w2).then_inc(w_in, 16)
            sp.wait_ge(dstf_done, 2)
            sp.dma_start(dst_f.rearrange("(p b) n -> p (b n)", p=DPART), dstf_sb).then_inc(dstf_out, 16)
            sp.dma_start(blk_last.rearrange("(p n) -> p n", p=DPART), dlast_sb).then_inc(dstf_out, 16)
            sp.wait_ge(dstf_out, 32)
            sp.dma_start(blk_sb, blk_last.rearrange("(a n) -> a n", a=1).to_broadcast([P, NBLK])).then_inc(blk_in, 16)
            sp.wait_ge(memsets, 1)
            sp.dma_start(marks.rearrange("(p c) f -> p (c f)", p=P), zeros[:, :]).then_inc(zero_m, 16)
            sp.wait_ge(src4_done, 4)
            sp.dma_start(src4.rearrange("(p n) d -> p (n d)", p=P), src4_sb).then_inc(src4_out, 16)

            def store_qv(b, u):
                sp.wait_ge(qkv_evac, b + 1)
                sp.dma_start(qv_tab.rearrange("(p b) c -> p b c", p=P)[:, b, :], stage[:, u, :]).then_inc(qv_out[u], 16)

            with sp.Fori(0, FIELDS_AT - 2) as i:
                for u in range(2):
                    store_qv(2 * i + u, u)
            sp.wait_ge(marks_out, 16 * NB)
            sp.dma_start(mkr.rearrange("p r f -> p (r f)"), marks.rearrange("(p c) f -> p (c f)", p=P)).then_inc(marks_in, 16)
            with sp.Fori(FIELDS_AT - 2, NB // 2) as i:
                for u in range(2):
                    store_qv(2 * i + u, u)
            sp.dma_start(k_tab.rearrange("(p b) c -> p (b c)", p=P), ks[:, :]).then_inc(k_out, 16)

            def store_state(i, u):
                sp.wait_ge(state_ready, 4 * i + u + 1)
                sp.dma_start(lanes(hist_m, 4 * i + u), top[:, u, :]).then_inc(hist_out[u], 16)
                sp.dma_start(lanes(hist_zs, 4 * i + u), zs[:, u, :]).then_inc(hist_out[u], 16)

            with sp.Fori(0, LANE_ROWS // RING) as i:
                for u in range(RING):
                    store_state(i, u)

            sp.wait_ge(join_done, 1)
            sp.dma_start(hist_zs[ROWS:ROWS + P, :], carry[:, 0, :]).then_inc(join_out, 16)
            for c in range(3):
                part = slice(c * LN_CHUNK, (c + 1) * LN_CHUNK)
                sp.wait_ge(h_ready, NB + LN_CHUNK * (c + 1))
                sp.dma_start(h_tab.rearrange("(p b) c -> p b c", p=P)[:, part, :], hs[:, part, :]).then_inc(h_out, 16)

            def store_acc(i, u):
                sp.wait_ge(acc_ready, 4 * i + u + 1)
                sp.dma_start(lanes(hist_a, 4 * i + u), acc[:, u, :]).then_inc(hista_out[u], 16)

            with sp.Fori(0, LANE_ROWS // RING) as i:
                for u in range(RING):
                    store_acc(i, u)
            sp.wait_ge(join_done, 2)
            sp.dma_start(hist_a[ROWS:ROWS + P, :], carry[:, 0, 0:CH]).then_inc(joina_out, 16)
            for g in range(3):
                sp.wait_ge(out_add, (g + 1) * NB // 3)
                sp.dma_start(out.rearrange("(p b) c -> p b c", p=NP)[:, g * NB // 3:(g + 1) * NB // 3, :],
                             xs[0:NP, g * NB // 3:(g + 1) * NB // 3, :]).then_inc(out_st, 16)
            sp.wait_ge(out_st, 48)

        @block.gpsimd
        def _(pool):
            pool.memset(zeros[:, :], 0.0).then_inc(memsets, 1)
            pool.memset(ident[:, :], 0.0).then_inc(consts0, 1)
            pool.memset(ones[:, :], 1.0).then_inc(consts0, 1)
            pool.iota(nid_i[:, :], pattern=[[1, NB + 1]], base=0, channel_multiplier=NB).then_inc(iotas, 1)
            pool.iota(row_i[:, :], pattern=[[1, LANE_ROWS]], base=0, channel_multiplier=LANE_ROWS).then_inc(iotas, 1)
            pool.iota(w_i[:, :], pattern=[[1, WIN]], base=0, channel_multiplier=0).then_inc(iotas, 1)
            pool.wait_ge(consts0, 2)
            pool.affine_select(out=ident[:, :], in_=ident[:, :], compare_op=ALU.not_equal, fill=1.0, base=0,
                               pattern=[[-1, P]], channel_multiplier=1).then_inc(consts, 1)
            pool.affine_select(out=upper[:, :], in_=ones[:, :], compare_op=ALU.is_gt, fill=0.0, base=0,
                               pattern=[[1, P]], channel_multiplier=-1).then_inc(consts, 1)
            for b in range(NB + 1):
                if b % SCH == 0:
                    pool.wait_ge(blk_done, b // SCH + 1)
                pool.indirect_dma_start(dblk[:, b, :], None, dst_f[:, :],
                                        bass.IndirectOffsetOnAxis(ap=blk_i[:, b:b + 1], axis=0),
                                        bounds_check=NBLK - 1, oob_is_err=False).then_inc(blk_gathered[b // SCH], 16)
            pool.wait_ge(node_done, 1)
            pool.wait_ge(zero_m, 16)
            for b in range(NB):
                pool.indirect_dma_start(marks[:, :], bass.IndirectOffsetOnAxis(ap=sidx[:, b:b + 1], axis=0),
                                        mk[:, b, :], None, bounds_check=ROWS - 1, oob_is_err=False).then_inc(marks_out, 16)
            pool.wait_ge(win_done, 1)
            pool.wait_ge(src4_out, 16)
            for g in range(GROUPS):
                pool.indirect_dma_start(src4_row[:, g * 4 * WIN:(g + 1) * 4 * WIN], None, src4[:, :],
                                        bass.IndirectOffsetOnAxis(ap=win_i[:, 4 * g:4 * g + 1], axis=0),
                                        bounds_check=P * LANE_WIN - 1, oob_is_err=False).then_inc(src4_gathered, 16)
            last_node, last_window = pool.to_reg(PAD_NODES - 1), pool.to_reg(NWIN - 1)

            def gather_qv(t, u):
                pool.wait_ge(idx_ready, t + 1)
                pool.sem_inc(gathering, 1)
                pool.indirect_dma_start(kk[:, u, :], None, k_tab[:, :],
                                        bass.IndirectOffsetOnAxis(ap=idx[:, u, WIN + 1:WIN + 2], axis=0),
                                        bounds_check=last_node, oob_is_err=False).then_inc(qv_in[u], 16)
                for w in range(WIN):
                    pool.indirect_dma_start(qv[:, u, w, :, :].rearrange("p h c -> p (h c)"), None, qv_tab[:, :],
                                            bass.IndirectOffsetOnAxis(ap=idx[:, u, w:w + 1], axis=0),
                                            bounds_check=last_node, oob_is_err=False).then_inc(qv_in[u], 16)

            pool.wait_ge(k_out, 16)
            for u in range(2):
                pool.wait_ge(qv_out[u], 16 * (NB // 2))
            for u in range(RING):
                gather_qv(u, u)
            with pool.Fori(1, LANE_ROWS // RING) as i:
                for u in range(RING):
                    gather_qv(4 * i + u, u)

            pool.wait_ge(win_done, 2)
            for u in range(RING):
                pool.wait_ge(hist_out[u], 32 * (LANE_ROWS // RING))
            pool.indirect_dma_start(hst[:, 0:CH], None, hist_m[:, :], bass.IndirectOffsetOnAxis(ap=lane_j[:, 0:1], axis=0),
                                    bounds_check=ROWS - 1, oob_is_err=False).then_inc(hst_in, 16)
            pool.indirect_dma_start(hst[:, CH:3 * CH], None, hist_zs[0:ROWS, :], bass.IndirectOffsetOnAxis(ap=lane_j[:, 0:1], axis=0),
                                    bounds_check=ROWS - 1, oob_is_err=False).then_inc(hst_in, 16)
            pool.wait_ge(join_out, 16)

            for b in range(NB):
                if b >= FRING:
                    pool.wait_ge(fin_step, 3 * (b - FRING + 1))
                pool.indirect_dma_start(fin[:, b % FRING, :], None, hist_zs[:, :],
                                        bass.IndirectOffsetOnAxis(ap=fidx[:, b:b + 1], axis=0),
                                        bounds_check=ROWS + P - 1, oob_is_err=False).then_inc(fin_in[b % FRING], 16)

            def gather_msg(t, u):
                pool.wait_ge(idx_ready, LANE_ROWS + RING + t + 1)
                pool.sem_inc(gathering, 1)
                pool.indirect_dma_start(eat[:, u, :], None, edge[:, :],
                                        bass.IndirectOffsetOnAxis(ap=idx[:, u, WIN:WIN + 1], axis=0),
                                        bounds_check=last_window, oob_is_err=False).then_inc(msg_in[u], 16)
                for w in range(WIN):
                    pool.indirect_dma_start(hmsg[:, u, w, :], None, h_tab[:, :],
                                            bass.IndirectOffsetOnAxis(ap=idx[:, u, w:w + 1], axis=0),
                                            bounds_check=last_node, oob_is_err=False).then_inc(msg_in[u], 16)

            pool.wait_ge(fin_step, 3 * NB)
            pool.wait_ge(h_out, 48)
            for u in range(RING):
                gather_msg(u, u)
            with pool.Fori(1, LANE_ROWS // RING) as i:
                for u in range(RING):
                    gather_msg(4 * i + u, u)
            for u in range(RING):
                pool.wait_ge(hista_out[u], 16 * (LANE_ROWS // RING))
            pool.indirect_dma_start(hst[:, 0:CH], None, hist_a[0:ROWS, :], bass.IndirectOffsetOnAxis(ap=lane_j[:, 0:1], axis=0),
                                    bounds_check=ROWS - 1, oob_is_err=False).then_inc(hsa_in, 16)
            pool.wait_ge(joina_out, 16)
            for b in range(NB):
                if b >= FRING:
                    pool.wait_ge(agg_add, b - FRING + 1)
                pool.indirect_dma_start(aggs[:, b % FRING, :], None, hist_a[:, :],
                                        bass.IndirectOffsetOnAxis(ap=fidx[:, b:b + 1], axis=0),
                                        bounds_check=ROWS + P - 1, oob_is_err=False).then_inc(agg_in[b % FRING], 16)

        @block.scalar
        def _(act):
            def relu_ln(n, c):
                std_of_var(n, c)
                act.wait_ge(ln_norm, n)
                for b in range(c * LN_CHUNK, (c + 1) * LN_CHUNK):
                    act.activation(hs[:, b, :], xs[:, b, :], ACT.Relu, bias=nmr[:, b:b + 1],
                                   scale=rstd[:, b:b + 1]).then_inc(h_ready, 1)

            def std_of_var(n, c):
                part = slice(c * LN_CHUNK, (c + 1) * LN_CHUNK)
                act.wait_ge(ln_var, n)
                act.activation(rstd[:, part], mv[:, part, 1], ACT.Sqrt, bias=eps[:, 0:1]).then_inc(ln_std, 1)

            for c in range(3):
                relu_ln(c + 1, c)
            for c in range(3):
                std_of_var(c + 4, c)
            act.wait_ge(ln_norm, 6)
            act.wait_ge(par_in, 16)

            def normalise(b, u, warm):
                if warm:
                    act.wait_ge(tr_ready, b - 1)
                act.activation(xn[:, u, :], hs[:, b, :], ACT.Identity, bias=nmr[:, bass.ds(b, 1)],
                               scale=rstd[:, bass.ds(b, 1)]).then_inc(xn_ready, 1)

            def scale_T(b, u, warm):
                act.wait_ge(tr_ready, b + 1)
                if warm:
                    act.wait_ge(qkv_ready, b - 1)
                for h in range(2):
                    last = act.activation(xT[:, u, h, :], banks[u][:, h * P:(h + 1) * P], ACT.Identity,
                                          bias=pv("beta", h), scale=pv("gamma", h))
                last.then_inc(xT_ready, 1)

            def evac_qkv(b, u, warm):
                act.wait_ge(qkv_ready, b + 1)
                if warm:
                    act.wait_ge(qv_out[u], 8 * b - 8 * u)
                act.activation(stage[:, u, :], banks[2 + u][:, :], ACT.Copy)
                act.activation(ks[:, bass.ds(b * CH, CH)], banks[4 + u][:, 0:CH], ACT.Copy).then_inc(qkv_evac, 1)

            normalise(0, 0, False)
            normalise(1, 1, False)
            scale_T(0, 0, False)
            for b in (2, 3):
                normalise(b, b % 2, True)
                scale_T(b - 1, (b - 1) % 2, b > 2)
                evac_qkv(b - 2, b % 2, False)
            with act.Fori(2, NB // 2) as i:
                for u in range(2):
                    normalise(2 * i + u, u, True)
                    scale_T(2 * i + u - 1, 1 - u, True)
                    evac_qkv(2 * i + u - 2, u, True)
            scale_T(NB - 1, 1, True)
            evac_qkv(NB - 2, 0, True)
            evac_qkv(NB - 1, 1, True)

            def next_idx(i, u):
                act.activation(idx[:, u, :], pack[:, 4 * i + u + RING, :], ACT.Copy).then_inc(idx_ready, 1)

            def first_idx():
                for u in range(RING):
                    act.activation(idx[:, u, :], pack[:, u, :], ACT.Copy).then_inc(idx_ready, 1)

            def exps(i, u):
                act.wait_ge(a_step, 28 * i + 7 * u + 6)
                for w in range(WIN):
                    last = act.activation(qv[:, u, w, 0, :], qv[:, u, w, 0, :], ACT.Exp,
                                          bias=sneg[:, 4 * i + u, w:w + 1], scale=SCALE)
                    if w == WIN // 2 - 1:
                        last.then_inc(exp_ready, 1)
                last.then_inc(exp_ready, 1)
                act.wait_ge(a_step, 28 * i + 7 * u + 7)
                act.activation(alpha[:, u % 2, :], alpha[:, u % 2, :], ACT.Exp, scale=SCALE).then_inc(exp_ready, 1)

            def evac_state(i, u):
                act.wait_ge(psum_ready, 4 * i + u + 1)
                act.activation(zs[:, u, :], banks[u % 2][:, :], ACT.Copy).then_inc(state_ready, 1)
                next_idx(i, u)

            act.wait_ge(qidx_done, 1)
            first_idx()
            exps(0, 0)
            for u in range(1, RING):
                exps(0, u)
                evac_state(0, u - 1)
            with act.Fori(1, LANE_ROWS // RING) as i:
                for u in range(RING):
                    exps(i, u)
                    evac_state(i if u else i - 1, (u - 1) % RING)
            evac_state(LANE_ROWS // RING - 1, RING - 1)

            for h in range(2):
                act.wait_ge(join_arg, h + 1)
                act.activation(join[:, 16:20, :], join[:, 16:20, :], ACT.Exp, scale=SCALE).then_inc(join_exp, 1)

            for c in range(3):
                relu_ln(c + 7, c)

            def relus(i, u):
                act.wait_ge(added, 4 * i + u + 1)
                for w in range(WIN):
                    last = act.activation(hmsg[:, u, w, :], hmsg[:, u, w, :], ACT.Relu,
                                          bias=sneg[:, 4 * i + u, w:w + 1])
                last.then_inc(relued, 1)

            def evac_acc(i, u):
                act.wait_ge(sum_ready, 4 * i + u + 1)
                act.activation(acc[:, u, :], banks[u % 2][:, 0:CH], ACT.Copy).then_inc(acc_ready, 1)
                next_idx(i, u)

            first_idx()
            relus(0, 0)
            for u in range(1, RING):
                relus(0, u)
                evac_acc(0, u - 1)
            with act.Fori(1, LANE_ROWS // RING) as i:
                for u in range(RING):
                    relus(i, u)
                    evac_acc(i if u else i - 1, (u - 1) % RING)
            evac_acc(LANE_ROWS // RING - 1, RING - 1)

            def columns(b, u):
                act.wait_ge(agg_tr, b + 1)
                act.activation(hT[:, :, bass.ds(b * NP, NP)],
                               banks[2 + u][:, 0:2 * P].rearrange("p (m n) -> p m n", m=2)[:, :, 0:NP],
                               ACT.Copy).then_inc(agg_cp, 1)

            def bias1(n, u):
                for m in range(4):
                    act.wait_ge(y1_mm, 4 * n + m + 1)
                    act.activation(y1[:, m, bass.ds(n * CCOLS, CCOLS)], banks[4 + m][:, 0:CCOLS], ACT.Identity,
                                   bias=pv("b1", m)).then_inc(y1_ev, 1)

            for b in range(6):
                columns(b, b % 2)
            for n in range(2):
                for b in range(3 * n + 6, 3 * n + 9):
                    columns(b, b % 2)
                bias1(n, 0)
            with act.Fori(2, NCHUNK // 2) as i:
                for c in range(2):
                    for b in range(3 * c, 3 * c + 3):
                        columns(6 * i + b, b % 2)
                    bias1(2 * i - 2 + c, 0)
            for n in range(NCHUNK - 2, NCHUNK):
                bias1(n, 0)
            act.wait_ge(bn_var, 1)
            act.activation(bn[:, 0, :], bn[:, 0, :], ACT.Sqrt, bias=eps[:, 0:1]).then_inc(bn_std, 1)
            act.wait_ge(bn_ready, 1)

            def relu1(n):
                for m in range(4):
                    last = act.activation(y1[:, m, bass.ds(n * CCOLS, CCOLS)], y1[:, m, bass.ds(n * CCOLS, CCOLS)],
                                          ACT.Relu, bias=bn[:, 2, m:m + 1], scale=bn[:, 1, m:m + 1])
                last.then_inc(y1_act, 1)

            def bias2(n, u):
                act.wait_ge(y2_mm, n + 1)
                for m in range(2):
                    last = act.activation(y2[:, m, bass.ds(n * CCOLS, CCOLS)], banks[2 * u + m][:, 0:CCOLS],
                                          ACT.Identity, bias=pv("b2", m))
                last.then_inc(y2_ev, 1)

            relu1(0)
            relu1(1)
            bias2(0, 0)
            with act.Fori(1, NCHUNK // 2) as i:
                for u in range(2):
                    relu1(2 * i + u)
                    bias2(2 * i + u - 1, 1 - u)
            bias2(NCHUNK - 1, 1)
            for n in range(2):
                act.wait_ge(g_var, n + 1)
                act.activation(gn[:, 12, :], gn[:, 12, :], ACT.Sqrt, bias=eps[:, 0:1]).then_inc(g_std, 1)
            act.wait_ge(g_ready, 1)

            def affine(b, u, warm):
                if warm:
                    act.wait_ge(out_tr, b - 1)
                for m in range(2):
                    last = act.activation(xT[:, u, m, 0:NP], y2[:, m, bass.ds(b * NP, NP)], ACT.Relu,
                                          bias=gn[:, 14, m:m + 1], scale=gn[:, 13, m:m + 1])
                last.then_inc(out_aff, 1)

            affine(0, 0, False)
            affine(1, 1, False)
            with act.Fori(1, NB // 2) as i:
                for u in range(2):
                    affine(2 * i + u, u, True)

        @block.tensor
        def _(pe):
            pe.wait_ge(consts, 2)
            pe.wait_ge(w_in, 48)

            def turn(b, u, warm):
                pe.wait_ge(xn_ready, b + 1)
                if warm:
                    pe.wait_ge(xT_ready, b - 1)
                for h in range(2):
                    last = pe.transpose(banks[u][:, h * P:(h + 1) * P], xn[:, u, h * P:(h + 1) * P], ident[:, :])
                last.then_inc(tr_ready, 1)

            def project(b, u, warm):
                pe.wait_ge(xT_ready, b + 1)
                if warm:
                    pe.wait_ge(qkv_evac, b - 1)
                for h in range(2):
                    pe.matmul(banks[2 + u][:, :], xT[:, u, h, :], wq_sb[:, h, 0:2 * CH], start=(h == 0), stop=(h == 1))
                for h in range(2):
                    last = pe.matmul(banks[4 + u][:, 0:CH], xT[:, u, h, :], wq_sb[:, h, 2 * CH:3 * CH],
                                     start=(h == 0), stop=(h == 1))
                last.then_inc(qkv_ready, 1)

            turn(0, 0, False)
            turn(1, 1, False)
            project(0, 0, False)
            turn(2, 0, True)
            project(1, 1, False)
            turn(3, 1, True)
            project(2, 0, True)
            def tiles(first, behind):
                with pe.Fori(first, behind) as i:
                    for u in range(2):
                        turn(2 * i + u, u, True)
                        project(2 * i + u - 1, 1 - u, True)

            tiles(2, PREFIX_AT)
            pe.wait_ge(small_in, 1)
            pe.matmul(banks[6][:, 0:1], upper[:, :], incl[:, NB - 1:NB], start=True, stop=True)
            pe.matmul(banks[6][:, 1:2], ones[:, :], incl[:, NB - 1:NB], start=True, stop=True).then_inc(small_out, 1)
            tiles(PREFIX_AT, FIELDS_AT)
            pe.wait_ge(small_in, 2)
            pe.transpose(banks[6][0:NF, P:2 * P], l3[:, :], ident[:, :]).then_inc(small_out, 1)
            pe.wait_ge(small_in, 3)
            pe.transpose(banks[6][:, 2 * P:2 * P + NF], l3t[:, 1, :], ident[0:NF, 0:NF]).then_inc(small_out, 1)
            tiles(FIELDS_AT, NB // 2)
            project(NB - 1, 1, True)
            pe.wait_ge(small_in, 4)
            pe.matmul(banks[7][:, 0:P], ones[:, :], flagd[:, :], start=True, stop=True).then_inc(small_out, 1)

            def sum_slots(i, u, warm):
                if warm:
                    pe.wait_ge(state_ready, 4 * i + u - 1)
                for w in range(WIN):
                    if w % (WIN // 2) == 0:
                        pe.wait_ge(weighted, 12 * i + 3 * u + 1 + w // (WIN // 2))
                    pe.matmul(banks[u % 2][:, :], ident[:, :], qv[:, u, w, :, :].rearrange("p h c -> p (h c)"),
                              start=(w == 0), stop=False)
                pe.wait_ge(weighted, 12 * i + 3 * u + 3)
                pe.matmul(banks[u % 2][:, :], ident[:, :], carry[:, u % 2, :], start=False, stop=True)\
                  .then_inc(psum_ready, 1)

            for u in range(RING):
                sum_slots(0, u, u > 1)
            with pe.Fori(1, LANE_ROWS // RING) as i:
                for u in range(RING):
                    sum_slots(i, u, True)

            def turn_all(pairs):
                for to, of in pairs:
                    last = pe.transpose(to, of, ident[:, :])
                last.then_inc(small_out, 1)

            pe.wait_ge(state_ready, LANE_ROWS)
            pe.wait_ge(hst_in, 32)
            end = [top[:, RING - 1, n * P:(n + 1) * P] for n in range(2)] + [zs[:, RING - 1, n * P:(n + 1) * P] for n in range(4)] + [hst[:, n * P:(n + 1) * P] for n in range(6)]
            turn_all([(banks[2 + n // 4][:, n % 4 * P:(n % 4 + 1) * P], e) for n, e in enumerate(end)])
            pe.wait_ge(small_in, 5)
            turn_all([(banks[2][:, n * P:(n + 1) * P], join[:, 8 + n, :]) for n in range(4)])

            def sum_msgs(i, u, warm):
                pe.wait_ge(relued, 4 * i + u + 1)
                if warm:
                    pe.wait_ge(acc_ready, 4 * i + u - 1)
                for w in range(WIN):
                    pe.matmul(banks[u % 2][:, 0:CH], ident[:, :], hmsg[:, u, w, :], start=(w == 0), stop=False)
                pe.wait_ge(carried, 4 * i + u + 1)
                pe.matmul(banks[u % 2][:, 0:CH], ident[:, :], carry[:, u % 2, 0:CH], start=False, stop=True)\
                  .then_inc(sum_ready, 1)

            for u in range(RING):
                sum_msgs(0, u, u > 1)
            with pe.Fori(1, LANE_ROWS // RING) as i:
                for u in range(RING):
                    sum_msgs(i, u, True)
            pe.wait_ge(acc_ready, LANE_ROWS)
            pe.wait_ge(hsa_in, 16)
            end = [acc[:, RING - 1, n * P:(n + 1) * P] for n in range(2)] + [hst[:, n * P:(n + 1) * P] for n in range(2)]
            turn_all([(banks[2][:, n * P:(n + 1) * P], e) for n, e in enumerate(end)])
            pe.wait_ge(small_in, 6)
            turn_all([(banks[2][:, n * P:(n + 1) * P], join[:, 2 + n, :]) for n in range(2)])

            def turn_agg(b, u, warm):
                pe.wait_ge(agg_add, b + 1)
                if warm:
                    pe.wait_ge(agg_cp, b - 1)
                for h in range(2):
                    last = pe.transpose(banks[2 + u][:, h * P:(h + 1) * P], xn[:, u, h * P:(h + 1) * P], ident[:, :])
                last.then_inc(agg_tr, 1)

            def dense1(n, u, warm):
                pe.wait_ge(agg_cp, 3 * n + 3)
                for m in range(4):
                    if warm:
                        pe.wait_ge(y1_ev, 4 * n + m - 3)
                    for h in range(2):
                        last = pe.matmul(banks[4 + m][:, 0:CCOLS], w1_sb[:, h, m * P:(m + 1) * P],
                                         hT[:, h, bass.ds(n * CCOLS, CCOLS)], start=(h == 0), stop=(h == 1))
                    last.then_inc(y1_mm, 1)

            turn_agg(0, 0, False)
            turn_agg(1, 1, False)
            for b in range(2, 6):
                turn_agg(b, b % 2, True)
            dense1(0, 0, False)
            for b in range(6, 9):
                turn_agg(b, b % 2, True)
            dense1(1, 1, True)
            for b in range(9, 12):
                turn_agg(b, b % 2, True)
            dense1(2, 0, True)
            with pe.Fori(2, NCHUNK // 2) as i:
                for c in range(2):
                    for b in range(3 * c, 3 * c + 3):
                        turn_agg(6 * i + b, b % 2, True)
                    dense1(2 * i - 1 + c, 0, True)
            dense1(NCHUNK - 1, 0, True)

            def dense2(n, u, warm):
                pe.wait_ge(y1_act, n + 1)
                if warm:
                    pe.wait_ge(y2_ev, n - 1)
                for m in range(2):
                    for h in range(4):
                        last = pe.matmul(banks[2 * u + m][:, 0:CCOLS], w2_sb[:, h, m * P:(m + 1) * P],
                                         y1[:, h, bass.ds(n * CCOLS, CCOLS)], start=(h == 0), stop=(h == 3))
                last.then_inc(y2_mm, 1)

            dense2(0, 0, False)
            dense2(1, 1, False)
            with pe.Fori(1, NCHUNK // 2) as i:
                for u in range(2):
                    dense2(2 * i + u, u, True)
            for n in range(2):
                pe.wait_ge(small_in, 7 + n)
                pe.matmul(banks[6][:, 2 * n:2 * n + 2], ones[:, :], gn[:, 3 * n, :], start=True, stop=True)\
                  .then_inc(small_out, 1)

            def turn_out(b, u, warm):
                pe.wait_ge(out_aff, b + 1)
                if warm:
                    pe.wait_ge(out_add, b - 1)
                for h in range(2):
                    last = pe.transpose(banks[u][0:NP, h * P:(h + 1) * P], xT[:, u, h, 0:NP], ident[:, :])
                last.then_inc(out_tr, 1)

            turn_out(0, 0, False)
            turn_out(1, 1, False)
            with pe.Fori(1, NB // 2) as i:
                for u in range(2):
                    turn_out(2 * i + u, u, True)

        @block.vector
        def _(v):
            count = [0]

            def step(ins):
                count[0] += 1
                ins.then_inc(dve, 1)
                v.wait_ge(dve, count[0])

            def bc_last(a, n):
                return a[:, :, None].to_broadcast([P, a.shape[1], n])

            def bc_mid(a, n):
                return a[:, None, :].to_broadcast([P, n, a.shape[1]])

            step(v.memset(eps[:, :], EPS))
            v.wait_ge(dst_in, 16)
            v.tensor_copy(dlast_sb, dst_sb.rearrange("p (b n) -> p b n", n=BLK)[:, :, BLK - 1]).then_inc(dstf_done, 1)
            v.tensor_copy(dstf_sb, dst_sb).then_inc(dstf_done, 1)

            def ln_stats(t, n, c):
                for b in range(c * LN_CHUNK, (c + 1) * LN_CHUNK):
                    v.bn_stats(stats[:, b, :], t[:, b, :]).then_inc(bnst, 1)
                v.wait_ge(bnst, n * LN_CHUNK)
                for b in range(c * LN_CHUNK, (c + 1) * LN_CHUNK):
                    last = v.bn_aggr(mv[:, b, :], stats[:, b, :])
                last.then_inc(ln_var, 1)

            def ln_scale(n, c):
                part = slice(c * LN_CHUNK, (c + 1) * LN_CHUNK)
                v.wait_ge(ln_std, n)
                step(v.reciprocal(rstd[:, part], rstd[:, part]))
                v.scalar_tensor_tensor(out=nmr[:, part], in0=mv[:, part, 0], scalar=-1.0, in1=rstd[:, part],
                                       op0=ALU.mult, op1=ALU.mult).then_inc(ln_norm, 1)

            v.wait_ge(iotas, 3)
            step(v.tensor_copy(nid[:, :], nid_i[:, :]))
            v.wait_ge(blk_in, 16)
            for c, part in enumerate(spans):
                for b in part:
                    last = v.tensor_scalar(cmp1[:, b % SCH, :], blk_sb, nid[:, b:b + 1], None, ALU.is_lt, ALU.add,
                                           accum_out=cnt[:, b:b + 1])
                step(last)
                cols = slice(part[0], part[-1] + 1)
                step(v.tensor_scalar(cnt[:, cols], cnt[:, cols], float(NBLK - 1), None, ALU.min))
                v.tensor_copy(blk_i[:, cols], cnt[:, cols]).then_inc(blk_done, 1)
            for c in range(3):
                v.wait_ge(x_in[c], 16)
                ln_stats(xs, c + 1, c)
                if c:
                    ln_scale(c, c - 1)
            v.wait_ge(src_in, 16)
            for d in range(4):
                v.tensor_copy(src4_sb.rearrange("p (w d s) -> p w d s", d=4, s=WIN)[:, :, d, :],
                              src_sb[:, d * WIN:(d + LANE_WIN) * WIN].rearrange("p (w s) -> p w s", s=WIN))\
                 .then_inc(src4_done, 1)
            ln_scale(3, 2)
            for c in range(3):
                v.wait_ge(h_ready, LN_CHUNK * (c + 1))
                ln_stats(hs, c + 4, c)
                if c:
                    ln_scale(c + 3, c - 1)
            for c, part in enumerate(spans):
                v.wait_ge(blk_gathered[c], 16 * len(part))
                for b in part:
                    last = v.tensor_scalar(dblk[:, b, :], dblk[:, b, :], nid[:, b:b + 1], None, ALU.is_lt, ALU.add,
                                           accum_out=start[:, b:b + 1])
                if c == 0:
                    ln_scale(6, 2)
            step(last)
            step(v.scalar_tensor_tensor(out=start[:, :], in0=cnt[:, :], scalar=float(BLK), in1=start[:, :],
                                        op0=ALU.mult, op1=ALU.add))
            step(v.tensor_copy(n_i[:, 0, :], start[:, :]))
            step(v.tensor_scalar(n_i[:, 1, :], start[:, :], float(WIN - 1), None, ALU.add))
            step(v.tensor_scalar(n_i[:, :, :], n_i[:, :, :], 3, None, ALU.arith_shift_right))
            step(v.tensor_copy(s3[:, :, :], n_i[:, :, :]))
            st, en = start[:, 0:NB], start[:, 1:NB + 1]
            step(v.tensor_tensor(has[:, :], en, st, ALU.is_gt))
            step(v.tensor_tensor(nrow[:, :], s3[:, 1, 1:NB + 1], s3[:, 0, 0:NB], ALU.subtract))
            step(v.tensor_tensor(nrow[:, :], nrow[:, :], has[:, :], ALU.mult))
            v.wait_ge(memsets, 1)
            v.tensor_tensor_scan(incl[:, :], nrow[:, :], zeros[:, 0:NB], 0.0, ALU.add, ALU.add).then_inc(small_in, 1)
            v.wait_ge(small_out, 1)
            step(v.tensor_copy(offs[:, :], banks[6][:, 0:2]))
            step(v.scalar_tensor_tensor(out=rs[:, :], in0=incl[:, :], scalar=offs[:, 0:1], in1=nrow[:, :],
                                        op0=ALU.add, op1=ALU.subtract))
            step(v.tensor_scalar(nt[:, 0, :], has[:, :], -FAR, FAR, ALU.mult, ALU.add))
            step(v.tensor_tensor(nt[:, 0, :], nt[:, 0, :], rs[:, :], ALU.add))
            step(v.tensor_copy(sidx[:, :], nt[:, 0, :]))
            step(v.tensor_copy(mk[:, :, 0], st))
            step(v.tensor_copy(mk[:, :, 1], en))
            step(v.tensor_copy(mk[:, :, 3], nid[:, 0:NB]))
            v.tensor_tensor(mk[:, :, 2], rs[:, :], s3[:, 0, 0:NB], ALU.subtract).then_inc(node_done, 1)
            last_row, lane_f, lane_l, t = (nt[:, n, :] for n in range(4))
            step(v.scalar_tensor_tensor(out=last_row, in0=rs[:, :], scalar=-1.0, in1=nrow[:, :], op0=ALU.add, op1=ALU.add))
            middle = (LANE_ROWS - 1) / 2
            step(v.tensor_scalar(lane_i[:, 0, :], rs[:, :], -middle, 1.0 / LANE_ROWS, ALU.add, ALU.mult))
            step(v.tensor_scalar(lane_i[:, 1, :], last_row, -middle, 1.0 / LANE_ROWS, ALU.add, ALU.mult))
            step(v.tensor_copy(nt[:, 1:3, :], lane_i[:, :, :]))
            step(v.scalar_tensor_tensor(out=t, in0=lane_l, scalar=float(ROWS), in1=last_row, op0=ALU.add, op1=ALU.subtract))
            step(v.tensor_tensor(lane_f, lane_l, lane_f, ALU.is_gt))
            step(v.tensor_tensor(t, t, lane_f, ALU.mult))
            step(v.tensor_tensor(t, t, last_row, ALU.add))
            step(v.tensor_tensor(t, t, has[:, :], ALU.mult))
            step(v.tensor_copy(fidx[:, :], t))

            v.wait_ge(marks_in, 16)
            for f in range(NF):
                step(v.tensor_tensor_scan(fld[:, f, :], mkr[:, :, f], mkr[:, :, f], 0.0, ALU.max, ALU.max))
            v.tensor_copy(l3[:, :], fld[:, :, LANE_ROWS - 1]).then_inc(small_in, 1)
            v.wait_ge(small_out, 2)
            step(v.tensor_copy(l3t[:, 0, :], banks[6][0:NF, P:2 * P]))
            step(v.memset(l3t[:, 1, :], 0.0))
            v.tensor_tensor_scan(l3t[:, 1, 1:P], l3t[:, 0, 0:P - 1], l3t[:, 0, 0:P - 1], 0.0, ALU.max, ALU.max)\
             .then_inc(small_in, 1)
            v.wait_ge(small_out, 3)
            step(v.tensor_copy(l3[:, :], banks[6][:, 2 * P:2 * P + NF]))
            for f in range(NF):
                step(v.tensor_scalar(fld[:, f, :], fld[:, f, :], l3[:, f:f + 1], None, ALU.max))
            step(v.tensor_copy(row[:, :], row_i[:, :]))
            step(v.tensor_tensor(win, row[:, :], fld[:, 2, :], ALU.subtract))
            step(v.tensor_scalar(t0, win, float(WIN), None, ALU.mult))
            step(v.tensor_scalar(winc, win, float(NWIN - 1), None, ALU.min))
            v.tensor_copy(win_i[:, :], winc).then_inc(win_done, 1)
            step(v.tensor_scalar(lane_j[:, 0:1], fld[:, 1, 0:1], -1.0, None, ALU.add))
            step(v.tensor_scalar(lane_j[:, 0:1], lane_j[:, 0:1], 3, None, ALU.arith_shift_right))
            step(v.tensor_copy(lane[:, 0:1], lane_j[:, 0:1]))
            step(v.tensor_tensor(lane[:, 0:1], lane[:, 0:1], fld[:, 2, 0:1], ALU.add))
            step(v.tensor_tensor(lane[:, 0:1], lane[:, 0:1], row[:, LANE_ROWS - 1:LANE_ROWS], ALU.min))
            v.tensor_copy(lane_j[:, 0:1], lane[:, 0:1]).then_inc(win_done, 1)
            step(v.tensor_tensor(brk[:, :], t0, fld[:, 0, :], ALU.is_le))
            step(v.tensor_scalar(t1, row[:, :], offs[:, 1:2], None, ALU.is_ge))
            step(v.tensor_tensor(brk[:, :], brk[:, :], t1, ALU.max))
            step(v.tensor_scalar(acont[:, :], brk[:, :], -1.0, 1.0, ALU.mult, ALU.add))
            step(v.tensor_scalar(mneg[:, :], brk[:, :], NEG, None, ALU.mult))
            step(v.tensor_reduce(lane[:, 2:3], brk[:, :], AX.X, ALU.max))
            step(v.tensor_scalar(lane[:, 3:4], lane[:, 2:3], -1.0, 1.0, ALU.mult, ALU.add))
            v.tensor_scalar(flagd[:, :], ident[:, :], lane[:, 3:4], None, ALU.mult).then_inc(small_in, 1)
            v.wait_ge(small_out, 4)
            step(v.tensor_copy(flagb[:, 0, :], banks[7][:, 0:P]))
            step(v.tensor_scalar(flagb[:, 1, :], flagb[:, 0, :], -NEG, NEG, ALU.mult, ALU.add))
            step(v.tensor_copy(wslot[:, :], w_i[:, :]))
            step(v.tensor_tensor(valid, bc_last(t0, WIN), bc_mid(wslot, LANE_ROWS), ALU.add))
            step(v.tensor_tensor(srow, valid, bc_last(fld[:, 0, :], WIN), ALU.is_ge))
            step(v.tensor_tensor(valid, valid, bc_last(fld[:, 1, :], WIN), ALU.is_lt))
            step(v.tensor_tensor(valid, valid, srow, ALU.mult))
            step(v.tensor_scalar(sneg[:, :, :], valid, -NEG, NEG, ALU.mult, ALU.add))
            v.wait_ge(src4_gathered, 16 * GROUPS)
            s4 = src4_row.rearrange("p (g d s) -> p g d s", d=4, s=WIN)
            wg = winc.rearrange("p (g j) -> p g j", j=4)
            sg = srow.rearrange("p (g j) w -> p g j w", j=4)
            step(v.tensor_copy(sg[:, :, 0, :], s4[:, :, 0, :]))
            for j in range(1, 4):
                step(v.tensor_tensor(delta, wg[:, :, j], wg[:, :, 0], ALU.subtract))
                for d in range(j + 1):
                    step(v.scalar_tensor_tensor(out=seltmp if d else sg[:, :, j, :], in0=bc_last(delta, WIN),
                                                scalar=float(d), in1=s4[:, :, d, :], op0=ALU.is_equal, op1=ALU.mult))
                    if d:
                        step(v.tensor_tensor(sg[:, :, j, :], sg[:, :, j, :], seltmp, ALU.add))
            step(v.tensor_tensor(srow, srow, valid, ALU.mult))
            step(v.tensor_reduce(fmx, srow, AX.X, ALU.max))
            step(v.tensor_scalar(valid, valid, -1.0, 1.0, ALU.mult, ALU.add))
            step(v.tensor_tensor(valid, valid, bc_last(fmx, WIN), ALU.mult))
            step(v.tensor_tensor(srow, srow, valid, ALU.add))
            step(v.tensor_copy(pack[:, 0:LANE_ROWS, 0:WIN], srow))
            step(v.tensor_copy(pack[:, 0:LANE_ROWS, WIN], winc))
            step(v.tensor_copy(pack[:, 0:LANE_ROWS, WIN + 1], fld[:, 3, :]))
            v.memset(pack[:, LANE_ROWS:LANE_ROWS + RING, :], 0).then_inc(qidx_done, 1)
            v.wait_ge(k_out, 16)
            step(v.memset(top[:, RING - 1, :], 0.0))
            step(v.memset(zs[:, RING - 1, :], 0.0))

            def walk(i, u, weigh_before=True, logits_now=True):
                cold = isinstance(i, int) and i == 0
                n, h = 28 * i + 7 * u, u % 2
                j, o = (i, u - 1) if u else (i - 1, RING - 1)
                cold_o = isinstance(j, int) and j == 0 and o < 2
                l = qv[:, u, :, 0, :]
                e, val = qv[:, o, :, 0, :], qv[:, o, :, 1, :]
                before, now = top[:, (u - 1) % RING, :], top[:, u, :]
                half = WIN // 2
                if logits_now:
                    v.wait_ge(qv_in[u], 16 * (WIN + 1) * (i + 1))
                    v.tensor_tensor(l, l, bc_mid(kk[:, u, :], WIN), ALU.mult).then_inc(a_step, 1)
                if weigh_before:
                    v.wait_ge(exp_ready, 12 * j + 3 * o + 1)
                    v.tensor_tensor(val[:, 0:half, :], val[:, 0:half, :], e[:, 0:half, :], ALU.mult).then_inc(weighted, 1)
                if logits_now:
                    v.wait_ge(a_step, n + 1)
                    v.tensor_tensor(mx1, l[:, 0:half, :], l[:, half:WIN, :], ALU.max).then_inc(a_step, 1)
                if weigh_before:
                    v.wait_ge(exp_ready, 12 * j + 3 * o + 2)
                    v.tensor_tensor(val[:, half:WIN, :], val[:, half:WIN, :], e[:, half:WIN, :], ALU.mult).then_inc(weighted, 1)
                if logits_now:
                    v.wait_ge(a_step, n + 2)
                    v.tensor_tensor(mx2, mx1[:, 0:2, :], mx1[:, 2:4, :], ALU.max).then_inc(a_step, 1)
                    v.wait_ge(a_step, n + 3)
                    v.tensor_tensor(mx3, mx2[:, 0, :], mx2[:, 1, :], ALU.max).then_inc(a_step, 1)
                if weigh_before:
                    v.wait_ge(exp_ready, 12 * j + 3 * o + 3)
                    if not (cold_o and o == 0):
                        v.wait_ge(state_ready, 4 * j + o)
                    if not cold_o:
                        v.wait_ge(psum_ready, 4 * j + o - 1)
                    v.tensor_tensor(carry[:, o % 2, :].rearrange("p (a c) -> p a c", a=2),
                                    zs[:, (o - 1) % RING, :].rearrange("p (a c) -> p a c", a=2),
                                    bc_mid(alpha[:, o % 2, :], 2), ALU.mult).then_inc(weighted, 1)
                if logits_now:
                    v.wait_ge(a_step, n + 4)
                    if not cold:
                        v.wait_ge(hist_out[u], 32 * i)
                    reset = mneg[:, bass.ds(4 * i + u, 1)]
                    v.scalar_tensor_tensor(out=now, in0=before, scalar=reset, in1=mx3, op0=ALU.add, op1=ALU.max)\
                     .then_inc(a_step, 1)
                    v.wait_ge(a_step, n + 5)
                    v.tensor_tensor(l, l, bc_mid(now, WIN), ALU.subtract).then_inc(a_step, 1)
                    if not (cold and u < 2):
                        v.wait_ge(weighted, 12 * i + 3 * u - 3)
                    v.scalar_tensor_tensor(out=alpha[:, h, :], in0=before, scalar=reset, in1=now,
                                           op0=ALU.add, op1=ALU.subtract).then_inc(a_step, 1)

            walk(0, 0, weigh_before=False)
            for u in range(1, RING):
                walk(0, u)
            with v.Fori(1, LANE_ROWS // RING) as i:
                for u in range(RING):
                    walk(i, u)
            walk(LANE_ROWS // RING, 0, logits_now=False)

            v.wait_ge(small_out, 5)
            for n in range(3):
                step(v.tensor_copy(join[:, 4 * n:4 * n + 4, :].rearrange("p n c -> p (n c)"), banks[2 + n][:, :]))
            J = lambda n: join[:, n, :]

            def shifted(to, of):
                step(v.memset(to[:, 0:1], 0.0))
                step(v.tensor_copy(to[:, 1:P], of[:, 0:P - 1]))

            for h in range(2):
                tm, hm = J(h), J(6 + h)
                step(v.tensor_tensor_scan(J(12), flagb[:, 1, :], tm, 0.0, ALU.add, ALU.max))
                shifted(J(13), J(12))
                step(v.tensor_tensor(J(16), J(13), flagb[:, 1, :], ALU.add))
                step(v.tensor_tensor(J(16), J(16), J(12), ALU.subtract))
                step(v.tensor_tensor(J(17), tm, J(12), ALU.subtract))
                step(v.tensor_tensor(J(14), J(13), hm, ALU.max))
                step(v.tensor_tensor(J(18), J(13), J(14), ALU.subtract))
                v.tensor_tensor(J(19), hm, J(14), ALU.subtract).then_inc(join_arg, 1)
                v.wait_ge(join_exp, h + 1)
                for k in range(2):
                    step(v.tensor_tensor(J(15), J(2 + 2 * k + h), J(17), ALU.mult))
                    step(v.tensor_tensor_scan(J(20), J(16), J(15), 0.0, ALU.mult, ALU.add))
                    shifted(J(21), J(20))
                    step(v.tensor_tensor(J(22), J(21), J(18), ALU.mult))
                    step(v.tensor_tensor(J(23), J(8 + 2 * k + h), J(19), ALU.mult))
                    last = v.tensor_tensor(J(8 + 2 * k + h), J(22), J(23), ALU.add)
                    if (h, k) != (1, 1):
                        step(last)
            last.then_inc(small_in, 1)
            v.wait_ge(small_out, 6)
            v.tensor_copy(carry[:, 0, :], banks[2][:, :]).then_inc(join_done, 1)

            for c in range(3):
                for b in range(c * LN_CHUNK, (c + 1) * LN_CHUNK):
                    r = b % FRING
                    v.wait_ge(fin_in[r], 16 * (b // FRING + 1))
                    z, s = fin[:, r, 0:CH], fin[:, r, CH:2 * CH]
                    v.reciprocal(z, z).then_inc(fin_step, 1)
                    v.wait_ge(fin_step, 3 * b + 1)
                    v.tensor_tensor(s, s, z, ALU.mult).then_inc(fin_step, 1)
                    v.wait_ge(fin_step, 3 * b + 2)
                    v.scalar_tensor_tensor(out=xs[:, b, :], in0=s, scalar=has[:, b:b + 1], in1=xs[:, b, :],
                                           op0=ALU.mult, op1=ALU.add).then_inc(fin_step, 1)
                v.wait_ge(fin_step, 3 * LN_CHUNK * (c + 1))
                ln_stats(xs, c + 7, c)
                ln_scale(c + 7, c)
            step(v.memset(acc[:, RING - 1, :], 0.0))
            v.wait_ge(h_ready, 2 * NB)
            v.tensor_tensor(xs[:, :, :], xs[:, :, :], hs[:, :, :], ALU.add).then_inc(xh_done, 1)

            def add_edges(i, u):
                v.wait_ge(msg_in[u], 16 * (WIN + 1) * (i + 1))
                if not (isinstance(i, int) and i == 0):
                    v.wait_ge(hista_out[u], 16 * i)
                m = hmsg[:, u, :, :].rearrange("p w c -> p (w c)")
                v.tensor_tensor(m, m, eat[:, u, :], ALU.add).then_inc(added, 1)

            def carry_sum(i, u):
                early = isinstance(i, int) and i == 0
                if not (early and u == 0):
                    v.wait_ge(acc_ready, 4 * i + u)
                if not (early and u < 2):
                    v.wait_ge(sum_ready, 4 * i + u - 1)
                v.tensor_scalar(carry[:, u % 2, 0:CH], acc[:, (u - 1) % RING, :], acont[:, bass.ds(4 * i + u, 1)], None,
                                ALU.mult).then_inc(carried, 1)

            v.wait_ge(join_out, 16)
            add_edges(0, 0)
            for u in range(1, RING):
                add_edges(0, u)
                carry_sum(0, u - 1)
            with v.Fori(1, LANE_ROWS // RING) as i:
                for u in range(RING):
                    add_edges(i, u)
                    carry_sum(i if u else i - 1, (u - 1) % RING)
            carry_sum(LANE_ROWS // RING - 1, RING - 1)
            v.wait_ge(small_out, 7)
            step(v.tensor_copy(join[:, 0:4, :].rearrange("p n c -> p (n c)"), banks[2][:, :]))
            for h in range(2):
                step(v.tensor_tensor_scan(J(12), flagb[:, 0, :], J(h), 0.0, ALU.mult, ALU.add))
                shifted(J(13), J(12))
                last = v.tensor_tensor(J(2 + h), J(2 + h), J(13), ALU.add)
                if h == 0:
                    step(last)
            last.then_inc(small_in, 1)
            v.wait_ge(small_out, 8)
            v.tensor_copy(carry[:, 0, 0:CH], banks[2][:, 0:CH]).then_inc(join_done, 1)

            def add_agg(i, b, early):
                v.wait_ge(agg_in[b % FRING], 32 * i + 16 * (b // FRING) + 16)
                if not (early and b < 2):
                    v.wait_ge(agg_tr, 10 * i + b - 1)
                v.scalar_tensor_tensor(out=xn[:, b % 2, :], in0=aggs[:, b % FRING, :], scalar=has[:, bass.ds(10 * i + b, 1)],
                                       in1=hs[:, 10 * i + b, :], op0=ALU.mult, op1=ALU.add).then_inc(agg_add, 1)

            for b in range(10):
                add_agg(0, b, True)
            with v.Fori(1, NB // 10) as i:
                for b in range(10):
                    add_agg(i, b, False)

            with v.Fori(0, NCHUNK) as n:
                for m in range(4):
                    v.wait_ge(y1_ev, 4 * n + m + 1)
                    v.bn_stats(stats[:, n + m * NCHUNK, :], y1[:, m, bass.ds(n * CCOLS, CCOLS)]).then_inc(y1_bn, 1)
            v.wait_ge(y1_bn, 4 * NCHUNK)
            for m in range(4):
                last = v.bn_aggr(mvd[:, m, :], stats[:, m * NCHUNK:(m + 1) * NCHUNK, :].rearrange("p n s -> p (n s)"))
            step(last)
            v.tensor_copy(bn[:, 0, :], mvd[:, :, 1]).then_inc(bn_var, 1)
            v.wait_ge(bn_std, 1)
            step(v.reciprocal(bn[:, 0, :], bn[:, 0, :]))
            step(v.tensor_tensor(bn[:, 1, :], bn[:, 0, :], pvs("bn_g"), ALU.mult))
            step(v.tensor_tensor(bn[:, 2, :], bn[:, 1, :], mvd[:, :, 0], ALU.mult))
            v.tensor_tensor(bn[:, 2, :], pvs("bn_b"), bn[:, 2, :], ALU.subtract).then_inc(bn_ready, 1)

            with v.Fori(0, NCHUNK) as n:
                v.wait_ge(y2_ev, n + 1)
                for m in range(2):
                    v.bn_stats(stats[:, n + m * NCHUNK, :], y2[:, m, bass.ds(n * CCOLS, CCOLS)]).then_inc(y2_bn, 1)
            v.wait_ge(y2_bn, 2 * NCHUNK)
            for m in range(2):
                last = v.bn_aggr(mvd[:, m, :], stats[:, m * NCHUNK:(m + 1) * NCHUNK, :].rearrange("p n s -> p (n s)"))
            step(last)
            G = lambda n: gn[:, n, :]
            mean, var = mvd[:, 0:2, 0], mvd[:, 0:2, 1]
            v.tensor_copy(G(0), mean).then_inc(small_in, 1)
            v.wait_ge(small_out, 9)
            step(v.tensor_reduce(gn[:, 1, 0:1], banks[6][:, 0:2], AX.X, ALU.add))
            step(v.tensor_scalar(gn[:, 1, 0:1], gn[:, 1, 0:1], 1.0 / CH, None, ALU.mult))
            gm = gn[:, 1, 0:1]
            step(v.tensor_scalar(G(2), mean, gm, None, ALU.subtract))
            step(v.tensor_tensor(G(3), G(2), G(2), ALU.mult))
            v.tensor_tensor(G(3), G(3), var, ALU.add).then_inc(small_in, 1)
            v.wait_ge(small_out, 10)
            step(v.tensor_reduce(gn[:, 4, 0:1], banks[6][:, 2:4], AX.X, ALU.add))
            step(v.memset(G(12), 0.0))
            v.tensor_scalar(G(12), G(12), gn[:, 4, 0:1], 1.0 / CH, ALU.add, ALU.mult).then_inc(g_var, 1)
            v.wait_ge(g_std, 1)
            step(v.reciprocal(G(12), G(12)))
            step(v.tensor_tensor(G(5), pvs("ln_w"), G(12), ALU.mult))
            step(v.tensor_scalar(G(6), G(5), gm, None, ALU.mult))
            step(v.tensor_tensor(G(6), pvs("ln_b"), G(6), ALU.subtract))
            step(v.tensor_tensor(G(7), G(5), mean, ALU.mult))
            step(v.tensor_tensor(G(7), G(7), G(6), ALU.add))
            step(v.tensor_tensor(G(8), G(7), pvs("gn_ms"), ALU.mult))
            step(v.tensor_tensor(G(9), G(7), G(8), ALU.subtract))
            step(v.tensor_tensor(G(9), G(9), G(9), ALU.mult))
            step(v.tensor_tensor(G(10), G(5), G(5), ALU.mult))
            step(v.tensor_tensor(G(10), G(10), var, ALU.mult))
            v.tensor_tensor(G(12), G(10), G(9), ALU.add).then_inc(g_var, 1)
            v.wait_ge(g_std, 2)
            step(v.reciprocal(G(12), G(12)))
            step(v.tensor_tensor(G(11), pvs("gn_w"), G(12), ALU.mult))
            step(v.tensor_tensor(G(13), G(5), G(11), ALU.mult))
            step(v.tensor_tensor(G(14), G(6), G(8), ALU.subtract))
            step(v.tensor_tensor(G(14), G(14), G(11), ALU.mult))
            v.tensor_tensor(G(14), G(14), pvs("gn_b"), ALU.add).then_inc(g_ready, 1)

            v.wait_ge(xh_done, 1)
            with v.Fori(0, NB // 2) as i:
                for u in range(2):
                    v.wait_ge(out_tr, 2 * i + u + 1)
                    v.tensor_tensor(xs[0:NP, 2 * i + u, :], banks[u][0:NP, 0:CH], xs[0:NP, 2 * i + u, :], ALU.add)\
                     .then_inc(out_add, 1)


def kernel(x, src, dst, edge_attr_256, L0_gnn_Wqkv, L0_gnn_gamma, L0_gnn_beta, L1_gnn_W1, L1_gnn_b1, L1_gnn_bn_gamma,
           L1_gnn_bn_beta, L1_gnn_W2, L1_gnn_b2, L1_gnn_ln_w, L1_gnn_ln_b, L1_gnn_gn_w, L1_gnn_gn_b, L1_gnn_gn_ms):
    import concourse.bacc as bacc
    from concourse.bass_utils import run_bass_kernel_spmd

    def padded(a, rows):
        return np.concatenate([a, np.zeros((rows - a.shape[0],) + a.shape[1:], a.dtype)])

    a = {}
    a["x"] = padded(np.asarray(x), PAD_NODES)
    flat = padded(np.asarray(src), (P * LANE_WIN + 3) * WIN)
    a["src"] = np.stack([flat[p * LANE_WIN * WIN:(p * LANE_WIN + LANE_WIN + 3) * WIN] for p in range(P)])
    a["dst"] = np.asarray(dst)
    a["edge"] = padded(np.asarray(edge_attr_256), NWIN * WIN).reshape(NWIN, WIN * CH)
    w = np.asarray(L0_gnn_Wqkv).reshape(2, P, 3, CH).transpose(1, 0, 2, 3)
    a["wqkv"] = np.ascontiguousarray(np.stack([w[:, :, 0], w[:, :, 2], w[:, :, 1]], 2).reshape(P, 2, 3 * CH))
    a["w1"] = np.ascontiguousarray(np.asarray(L1_gnn_W1).reshape(2, P, HID).transpose(1, 0, 2))
    a["w2"] = np.ascontiguousarray(np.asarray(L1_gnn_W2).reshape(4, P, CH).transpose(1, 0, 2))
    vectors = [L0_gnn_gamma, L0_gnn_beta, L1_gnn_b1, L1_gnn_bn_gamma, L1_gnn_bn_beta, L1_gnn_b2, L1_gnn_ln_w,
               L1_gnn_ln_b, L1_gnn_gn_w, L1_gnn_gn_b, L1_gnn_gn_ms]
    a["params"] = np.ascontiguousarray(np.concatenate([np.asarray(t).reshape(-1, P).T for t in vectors], 1))

    nc = bacc.Bacc("TRN2", target_bir_lowering=False, num_devices=1)
    args = [nc.dram_tensor(f"in_{n}", t.shape, mybir.dt.from_np(t.dtype), kind="ExternalInput").ap() for n, t in a.items()]
    out = nc.dram_tensor("out_0", (NODES, CH), F32, kind="ExternalOutput").ap()
    build(nc, *args, out)
    r = run_bass_kernel_spmd(nc, [{f"in_{n}": t for n, t in a.items()}], core_ids=[0])
    return r.results[0]["out_0"]
```

```python
from contextlib import ExitStack

import numpy as np
import concourse.bass as bass
from concourse import mybir

F32 = mybir.dt.float32
I32 = mybir.dt.int32
ALU = mybir.AluOpType
ACT = mybir.ActivationFunctionType
AX = mybir.AxisListType

P = 128
NODES, EDGES, CH, HID = 3750, 123750, 256, 512
NB = 30
NP = NODES // NB
PAD_NODES = P * NB
WIN = 8
NWIN = -(-EDGES // WIN)
LANE_WIN = -(-NWIN // P)
LANE_EDGES = LANE_WIN * WIN
LANE_STATES = 2 * P * LANE_WIN
LANE_ROWS = -(-(NWIN + NODES) // (4 * P)) * 4
ROWS = P * LANE_ROWS
GROUPS = LANE_ROWS // 4
BLK = 375
NBLK = EDGES // BLK
DPART = 110
NCHUNK = 10
CCOLS = NODES // NCHUNK
FAR = 1.0e6
LN_CHUNK = NB // 3
SCH = 8
FIELDS_AT = 9
NF = 4
NEG = -1.0e30
EPS = 1e-5
SCALE = CH ** -0.5
RING = 4
PE_SLOTS = 2
FRING = 5

PARAMS = [("gamma", 2), ("beta", 2), ("b1", 4), ("bn_g", 4), ("bn_b", 4), ("b2", 2), ("ln_w", 2),
          ("ln_b", 2), ("gn_w", 2), ("gn_b", 2), ("gn_ms", 2)]
NPAR = sum(n for _, n in PARAMS)


def build(nc, x, src, dst_lanes, edge, wqkv, w1, w2, params, out):
    assert LANE_ROWS % RING == 0 and PE_SLOTS == 2 and GROUPS % 2 == 0 and LANE_WIN % RING == 1 and WIN == 8 and NBLK * BLK == EDGES and NP * NB == NODES and NB % 2 == 0
    with ExitStack() as ctx:
        def sb(name, shape, dt=F32):
            return ctx.enter_context(nc.sbuf_tensor(name, shape, dt))

        def sem(name):
            return ctx.enter_context(nc.semaphore(name))

        def dram(name, shape, dt=F32):
            return nc.dram_tensor(name, shape, dt, kind="Internal").ap()

        dst_f = dram("dst_f", (NBLK, BLK))
        blk_last = dram("blk_last", (NBLK,))
        src4 = dram("src4", (P * LANE_WIN, 4 * WIN))
        marks = dram("marks", (ROWS, NF))
        k_tab = dram("k_tab", (PAD_NODES, CH))
        qv_tab = dram("qv_tab", (PAD_NODES, 2 * CH))
        h_tab = dram("h_tab", (PAD_NODES, CH))
        hist_m = dram("hist_m", (ROWS, CH))
        hist_zs = dram("hist_zs", (ROWS + P, 2 * CH))
        hist_a = dram("hist_a", (LANE_STATES + P, CH))

        xs = sb("xs", [P, NB, CH])
        hs = sb("hs", [P, NB, CH])
        ks = sb("ks", [P, NB * CH])
        ring = sb("ring", [P, RING * WIN * 2 * CH])
        ident = sb("ident", [P, P])
        upper = sb("upper", [P, P])
        ones = sb("ones", [P, P])
        zeros = sb("zeros", [P, LANE_ROWS * NF])
        wq_sb = sb("wq_sb", [P, 2, 3 * CH])
        w1_sb = sb("w1_sb", [P, 2, HID])
        w2_sb = sb("w2_sb", [P, 4, CH])
        par = sb("par", [P, NPAR])
        stats = sb("stats", [P, 4 * NCHUNK, 6])
        mv = sb("mv", [P, NB, 2])
        rstd = sb("rstd", [P, NB])
        nmr = sb("nmr", [P, NB])
        eps = sb("eps", [P, 1])
        xn = sb("xn", [P, 2, CH])
        xT = sb("xT", [P, 2, 2, P])
        stage = sb("stage", [P, 2, 2 * CH])

        nid_i = sb("nid_i", [P, NB + 1], I32)
        nid = sb("nid", [P, NB + 1])
        cnt = sb("cnt", [P, NB + 1])
        blk_i = sb("blk_i", [P, NB + 1], I32)
        start = sb("start", [P, NB + 1])
        n_i = sb("n_i", [P, 2, NB + 1], I32)
        s3 = sb("s3", [P, 2, NB + 1])
        has = sb("has", [P, NB])
        nrow = sb("nrow", [P, NB])
        incl = sb("incl", [P, NB])
        rs = sb("rs", [P, NB])
        nt = sb("nt", [P, 4, NB])
        sidx = sb("sidx", [P, NB], I32)
        fidx = sb("fidx", [P, NB], I32)
        lane_i = sb("lane_i", [P, 2, NB], I32)
        mk = sb("mk", [P, NB, NF])
        offs = sb("offs", [P, 2])

        row_i = sb("row_i", [P, LANE_ROWS], I32)
        row = sb("row", [P, LANE_ROWS])
        fld = sb("fld", [P, NF, LANE_ROWS])
        win_i = sb("win_i", [P, LANE_ROWS], I32)
        brk = sb("brk", [P, LANE_ROWS])
        acont = sb("acont", [P, LANE_ROWS])
        mneg = sb("mneg", [P, LANE_ROWS])
        w_i = sb("w_i", [P, WIN], I32)
        wslot = sb("wslot", [P, WIN])
        sneg = sb("sneg", [P, LANE_ROWS, WIN])
        pack = sb("pack", [P, LANE_ROWS + RING, WIN + 2], I32)
        idx = sb("idx", [P, RING, WIN + 2], I32)
        bn = sb("bn", [P, 3, 4])
        mvd = sb("mvd", [P, 4, 2])
        gn = sb("gn", [P, 15, 2])
        l3 = sb("l3", [P, NF])
        l3t = sb("l3t", [NF, 2, P])
        lane = sb("lane", [P, 6])
        lane_j = sb("lane_j", [P, 3], I32)
        neg_ident = zeros[:, P:2 * P]
        flagd = upper
        wq_flat = wq_sb[:, :, :].rearrange("p a b -> p (a b)")
        src_l = wq_flat[:, 0:(LANE_WIN + 3) * WIN].bitcast(I32)
        first_neg = sb("first_neg", [P, LANE_WIN, WIN])
        later_neg = stage[:, :, :].rearrange("p a b -> p (a b)")[:, 0:LANE_EDGES].rearrange("p (t w) -> p t w", w=WIN)
        joins = wq_flat[:, 1000:1000 + LANE_WIN]
        whole = wq_flat[:, 1128:1128 + LANE_WIN]
        flagl = wq_flat[:, 1256:1256 + P]
        small = cnt[:, 0:NB]
        small_any = sb("small_any", [P, 1])
        small_i = sb("small_i", [P, 1], I32)
        flagb = sb("flagb", [P, 2, P])

        banks = [ctx.enter_context(nc.psum_tensor(f"bank{i}", [P, 512], F32)) for i in range(8)]

        cmp1 = ks[:, 0:SCH * NBLK].rearrange("p (b k) -> p b k", b=SCH)
        dblk = ring[:, 0:(NB + 1) * BLK].rearrange("p (b k) -> p b k", b=NB + 1)
        dst_sb = ring[0:DPART, 1024:1024 + EDGES // DPART].bitcast(I32)
        dstf_sb = ring[0:DPART, 4096:4096 + EDGES // DPART]
        dlast_sb = ring[0:DPART, 6144:6144 + NBLK // DPART]
        src4_sb = ring[:, 12000:12000 + LANE_WIN * 4 * WIN]
        blk_sb = ring[:, 15872:15872 + NBLK]
        src_sb = ks[:, 4096:4096 + (LANE_WIN + 3) * WIN].bitcast(I32)
        LW = LANE_ROWS * WIN
        at = [RING // 2 * WIN * 2 * CH, RING * WIN * 2 * CH]

        def carve(*shape, of=ring):
            n = int(np.prod(shape))
            v = of[:, at[0]:at[0] + n]
            at[0] += n
            assert at[0] <= at[1]
            return v if len(shape) == 1 else v.rearrange("p (a b) -> p a b", a=shape[0])

        mkr = carve(LANE_ROWS, NF)
        valid = carve(LANE_ROWS, WIN)
        srow = carve(LANE_ROWS, WIN)
        src4_row = carve(GROUPS * 4 * WIN)
        seltmp = carve(GROUPS, WIN)
        win, winc, t0, t1, fmx, delta = (carve(LANE_ROWS) for _ in range(6))
        delta = delta[:, 0:GROUPS]
        dst_l = hs[:, :, :].rearrange("p b c -> p (b c)")[:, 0:LANE_EDGES].rearrange("p (t w) -> p t w", w=WIN)
        at[:] = 0, NB * CH

        kk = carve(RING, CH, of=ks)
        mx1 = carve(4, CH, of=ks)
        mx2 = carve(2, CH, of=ks)
        mx3 = carve(CH, of=ks)
        top = carve(RING, CH, of=ks)
        zs = carve(RING, 2 * CH, of=ks)
        alpha = carve(2, CH, of=ks)
        carry = carve(2, 2 * CH, of=ks)
        hst = mx1.rearrange("p a b -> p (a b)")
        acc = zs[:, :, 0:CH]
        qv = ring[:, :].rearrange("p (s e h c) -> p s e h c", s=RING, e=WIN, h=2)
        hmsg = ring[:, 0:RING * WIN * CH].rearrange("p (s e c) -> p s e c", s=RING, e=WIN)
        eat = ring[:, RING * WIN * CH:].rearrange("p (s n) -> p s n", s=RING)
        parts = ring[:, :].rearrange("p (s h e c) -> p s h e c", s=RING, h=2, e=WIN)
        fin = ring[:, 0:NB * 2 * CH].rearrange("p (b k c) -> p b k c", b=NB, k=2)
        aggs = ring[:, 15104:15104 + FRING * CH].rearrange("p (s n) -> p s n", s=FRING)
        join = ring[:, 4096:4096 + 38 * P].rearrange("p (n c) -> p n c", c=P)
        turning = [xn[:, 0, :], xn[:, 1, :], xT[:, 0, :, :].rearrange("p h n -> p (h n)")]
        y1 = ring[:, 0:4 * NODES].rearrange("p (m n) -> p m n", m=4)
        hT = ks[:, 0:2 * NODES].rearrange("p (m n) -> p m n", m=2)
        y2 = hT

        def pv(name, m):
            first = sum(w for _, w in PARAMS[:[n for n, _ in PARAMS].index(name)])
            return par[:, first + m:first + m + 1]

        def pvs(name):
            n = dict(PARAMS)[name]
            first = sum(w for _, w in PARAMS[:[k for k, _ in PARAMS].index(name)])
            return par[:, first:first + n]

        dst_in, src_in, w_in, par_in = (sem(n) for n in ("dst_in", "src_in", "w_in", "par_in"))
        x_in = [sem(f"x_in{c}") for c in range(3)]
        dstf_out, blk_in, src4_out, zero_m = (sem(n) for n in ("dstf_out", "blk_in", "src4_out", "zero_m"))
        consts0, consts, iotas, memsets = (sem(n) for n in ("consts0", "consts", "iotas", "memsets"))
        dve = sem("dve")
        bnst = sem("bnst")
        dstf_done, src4_done, blk_done, node_done, win_done, qidx_done = (
            sem(n) for n in ("dstf_done", "src4_done", "blk_done", "node_done", "win_done", "qidx_done"))
        blk_gathered = [sem(f"blk_gathered{c}") for c in range(-(-(NB + 1) // SCH))]
        marks_out, marks_in, k_out = (sem(n) for n in ("marks_out", "marks_in", "k_out"))
        src4_gathered = [sem(f"src4_gathered{h}") for h in range(2)]
        ln_var, ln_std, ln_norm = sem("ln_var"), sem("ln_std"), sem("ln_norm")
        h_ready, xn_ready, tr_ready, xT_ready, qkv_ready, qkv_evac = (
            sem(n) for n in ("h_ready", "xn_ready", "tr_ready", "xT_ready", "qkv_ready", "qkv_evac"))
        qv_out = [sem(f"qv_out{i}") for i in range(2)]
        small_in, small_out = sem("small_in"), sem("small_out")
        qv_in = [sem(f"qv_in{i}") for i in range(RING)]
        diff_ready = sem("diff_ready")
        a_step, exp_ready, weighted, psum_ready, state_ready = (
            sem(n) for n in ("a_step", "exp_ready", "weighted", "psum_ready", "state_ready"))
        hist_out = [sem(f"hist_out{i}") for i in range(RING)]
        hst_in, join_done, join_out = sem("hst_in"), sem("join_done"), sem("join_out")
        join_arg, join_exp, idx_ready, gathering = (sem(n) for n in ("join_arg", "join_exp", "idx_ready", "gathering"))
        g_ready, xh_done = sem("g_ready"), sem("xh_done")
        fin_group = lambda b: b // 2 if b < LN_CHUNK else LN_CHUNK // 2 + b // LN_CHUNK - 1
        fin_in, fin_step, z_guess = [sem(f"fin_in{i}") for i in range(LN_CHUNK // 2 + 2)], sem("fin_step"), sem("z_guess")
        fin_used = sem("fin_used")
        h_out = sem("h_out")
        msg_in = [sem(f"msg_in{i}") for i in range(RING)]
        added, relued, carried, sum_ready, acc_ready = (
            sem(n) for n in ("added", "relued", "carried", "sum_ready", "acc_ready"))
        hista_out = [sem(f"hista_out{i}") for i in range(RING)]
        hsa_in, joina_out = sem("hsa_in"), sem("joina_out")
        lanes_in, path_known, flag_in, flag_out = (sem(n) for n in ("lanes_in", "path_known", "flag_in", "flag_out"))
        edges_in, later_relued, first_sum = [sem(f"edges_in{i}") for i in range(RING)], sem("later_relued"), sem("first_sum")
        agg_in, agg_add, agg_tr, agg_cp = [sem(f"agg_in{i}") for i in range(FRING)], sem("agg_add"), sem("agg_tr"), sem("agg_cp")
        y1_mm, y1_ev, y1_bn, bn_var, bn_std, bn_ready, y1_act = (
            sem(n) for n in ("y1_mm", "y1_ev", "y1_bn", "bn_var", "bn_std", "bn_ready", "y1_act"))
        y2_mm, y2_ev, y2_bn = sem("y2_mm"), sem("y2_ev"), sem("y2_bn")
        g_var, g_std, out_aff, out_tr, out_add, out_st = (
            sem(n) for n in ("g_var", "g_std", "out_aff", "out_tr", "out_add", "out_st"))

        spans = [range(b, min(b + SCH, NB + 1)) for b in range(0, NB + 1, SCH)]

        block = ctx.enter_context(nc.Block())
        lanes = lambda t, a: t[0:ROWS, :].rearrange("(p c) f -> p c f", p=P)[:, a, :]

        @block.sync
        def _(sp):
            sp.dma_start(dst_sb, dst_lanes[0:EDGES].rearrange("(p n) -> p n", p=DPART)).then_inc(dst_in, 16)
            sp.dma_start(src_sb, src).then_inc(src_in, 16)
            sp.wait_ge(dstf_done, 2)
            sp.dma_start(dst_f.rearrange("(p b) n -> p (b n)", p=DPART), dstf_sb).then_inc(dstf_out, 16)
            sp.dma_start(blk_last.rearrange("(p n) -> p n", p=DPART), dlast_sb).then_inc(dstf_out, 16)
            sp.wait_ge(dstf_out, 32)
            sp.dma_start(blk_sb, blk_last.rearrange("(a n) -> a n", a=1).to_broadcast([P, NBLK])).then_inc(blk_in, 16)
            for c in range(3):
                part = slice(c * LN_CHUNK, (c + 1) * LN_CHUNK)
                sp.dma_start(xs[:, part, :], x.rearrange("(p b) c -> p b c", p=P)[:, part, :]).then_inc(x_in[c], 16)
            sp.dma_start(par[:, :], params).then_inc(par_in, 16)
            sp.dma_start(wq_sb[:, :, :], wqkv).then_inc(w_in, 16)
            sp.dma_start(w1_sb[:, :, :], w1).then_inc(w_in, 16)
            sp.dma_start(w2_sb[:, :, :], w2).then_inc(w_in, 16)
            sp.wait_ge(memsets, 1)
            sp.dma_start(marks.rearrange("(p c) f -> p (c f)", p=P), zeros[:, :]).then_inc(zero_m, 16)
            sp.wait_ge(src4_done, 4)
            sp.dma_start(src4.rearrange("(p n) d -> p (n d)", p=P), src4_sb).then_inc(src4_out, 16)

            def store_qv(b, u):
                sp.wait_ge(qkv_evac, b + 1)
                sp.dma_start(qv_tab.rearrange("(p b) c -> p b c", p=P)[:, b, :], stage[:, u, :]).then_inc(qv_out[u], 16)

            def store_k(b0, b1):
                sp.dma_start(k_tab.rearrange("(p b) c -> p (b c)", p=P)[:, b0 * CH:b1 * CH], ks[:, b0 * CH:b1 * CH])\
                  .then_inc(k_out, 16)

            with sp.Fori(0, FIELDS_AT - 2) as i:
                for u in range(2):
                    store_qv(2 * i + u, u)
            sp.wait_ge(marks_out, 16 * NB)
            sp.dma_start(mkr.rearrange("p r f -> p (r f)"), marks.rearrange("(p c) f -> p (c f)", p=P)).then_inc(marks_in, 16)
            cuts = [FIELDS_AT - 2, (NB // 2 + FIELDS_AT - 2) // 2, NB // 2]
            store_k(0, 2 * cuts[0])
            for c0, c1 in zip(cuts, cuts[1:]):
                with sp.Fori(c0, c1) as i:
                    for u in range(2):
                        store_qv(2 * i + u, u)
                store_k(2 * c0, 2 * c1)
            sp.dma_start(dst_l.rearrange("p t w -> p (t w)").bitcast(I32), dst_lanes.rearrange("(p n) -> p n", p=P))\
              .then_inc(lanes_in, 16)
            sp.dma_start(src_l, src).then_inc(lanes_in, 16)

            def store_state(i, u):
                sp.wait_ge(state_ready, 4 * i + u + 1)
                sp.dma_start(lanes(hist_m, 4 * i + u), top[:, u, :]).then_inc(hist_out[u], 16)
                sp.dma_start(lanes(hist_zs, 4 * i + u), zs[:, u, :]).then_inc(hist_out[u], 16)

            with sp.Fori(0, LANE_ROWS // RING) as i:
                for u in range(RING):
                    store_state(i, u)

            sp.wait_ge(join_done, 1)
            sp.dma_start(hist_zs[ROWS:ROWS + P, :], carry[:, 0, :]).then_inc(join_out, 16)
            for c in range(3):
                part = slice(c * LN_CHUNK, (c + 1) * LN_CHUNK)
                sp.wait_ge(h_ready, NB + LN_CHUNK * (c + 1))
                sp.dma_start(h_tab.rearrange("(p b) c -> p b c", p=P)[:, part, :], hs[:, part, :]).then_inc(h_out, 16)

            def store_acc(i, u):
                sp.wait_ge(acc_ready, 4 * i + u + 1)
                sp.dma_start(lanes(hist_a, 4 * i + u), acc[:, u, :]).then_inc(hista_out[u], 16)

            by_window = edge.rearrange("(p t) n -> p t n", p=P)
            states = hist_a[0:LANE_STATES, :].rearrange("(p t h) c -> p t (h c)", p=P, h=2)

            def load_edges(i, u, warm):
                if warm:
                    sp.wait_ge(sum_ready, 4 * i + u - 3)
                sp.dma_start(parts[:, u, 1, :, :].rearrange("p w c -> p (w c)"), by_window[:, 4 * i + u, :])\
                  .then_inc(edges_in[u], 16)

            def store_states(i, u):
                sp.wait_ge(acc_ready, 4 * i + u + 1)
                sp.dma_start(states[:, 4 * i + u, :], zs[:, u, :]).then_inc(hista_out[u], 16)

            sp.wait_ge(path_known, 1)
            rows_needed = sp.value_load(small_i[0:1, 0:1], min_val=0, max_val=1)
            with sp.If(rows_needed == 0):
                sp.wait_ge(fin_used, 3)
                for u in range(RING):
                    load_edges(0, u, False)
                with sp.Fori(1, LANE_WIN // RING) as i:
                    for u in range(RING):
                        load_edges(i, u, True)
                        store_states(i - 1, u)
                load_edges(LANE_WIN // RING, 0, True)
                for u in range(RING):
                    store_states(LANE_WIN // RING - 1, u)
                store_states(LANE_WIN // RING, 0)
                sp.wait_ge(join_done, 2)
                sp.dma_start(hist_a[LANE_STATES:LANE_STATES + P, :], carry[:, 0, 0:CH]).then_inc(joina_out, 16)
            with sp.Else():
                with sp.Fori(0, LANE_ROWS // RING) as i:
                    for u in range(RING):
                        store_acc(i, u)
                sp.wait_ge(join_done, 2)
                sp.dma_start(hist_a[ROWS:ROWS + P, :], carry[:, 0, 0:CH]).then_inc(joina_out, 16)
            for g in range(3):
                sp.wait_ge(out_add, (g + 1) * NB // 6)
                sp.dma_start(out.rearrange("(p b) c -> p b c", p=NP)[:, g * NB // 3:(g + 1) * NB // 3, :],
                             xs[0:NP, g * NB // 3:(g + 1) * NB // 3, :]).then_inc(out_st, 16)
            sp.wait_ge(out_st, 48)

        @block.gpsimd
        def _(pool):
            pool.memset(zeros[:, :], 0.0).then_inc(memsets, 1)
            pool.memset(ident[:, :], 0.0).then_inc(consts0, 1)
            pool.memset(ones[:, :], 1.0).then_inc(consts0, 1)
            pool.iota(nid_i[:, :], pattern=[[1, NB + 1]], base=0, channel_multiplier=NB).then_inc(iotas, 1)
            pool.iota(row_i[:, :], pattern=[[1, LANE_ROWS]], base=0, channel_multiplier=LANE_ROWS).then_inc(iotas, 1)
            pool.iota(w_i[:, :], pattern=[[1, WIN]], base=0, channel_multiplier=0).then_inc(iotas, 1)
            pool.wait_ge(consts0, 2)
            pool.affine_select(out=ident[:, :], in_=ident[:, :], compare_op=ALU.not_equal, fill=1.0, base=0,
                               pattern=[[-1, P]], channel_multiplier=1).then_inc(consts, 1)
            pool.affine_select(out=upper[:, :], in_=ones[:, :], compare_op=ALU.is_gt, fill=0.0, base=0,
                               pattern=[[1, P]], channel_multiplier=-1).then_inc(consts, 1)
            for b in range(NB + 1):
                if b % SCH == 0:
                    pool.wait_ge(blk_done, b // SCH + 1)
                pool.indirect_dma_start(dblk[:, b, :], None, dst_f[:, :],
                                        bass.IndirectOffsetOnAxis(ap=blk_i[:, b:b + 1], axis=0),
                                        bounds_check=NBLK - 1, oob_is_err=False).then_inc(blk_gathered[b // SCH], 16)
            pool.wait_ge(node_done, 1)
            pool.wait_ge(zero_m, 16)
            for b in range(NB):
                pool.indirect_dma_start(marks[:, :], bass.IndirectOffsetOnAxis(ap=sidx[:, b:b + 1], axis=0),
                                        mk[:, b, :], None, bounds_check=ROWS - 1, oob_is_err=False).then_inc(marks_out, 16)
            pool.wait_ge(win_done, 1)
            pool.wait_ge(src4_out, 16)
            for g in range(GROUPS):
                pool.indirect_dma_start(src4_row[:, g * 4 * WIN:(g + 1) * 4 * WIN], None, src4[:, :],
                                        bass.IndirectOffsetOnAxis(ap=win_i[:, 4 * g:4 * g + 1], axis=0),
                                        bounds_check=P * LANE_WIN - 1, oob_is_err=False).then_inc(src4_gathered[2 * g // GROUPS], 16)
            last_node, last_window = pool.to_reg(PAD_NODES - 1), pool.to_reg(NWIN - 1)

            def gather_qv(t, u):
                pool.wait_ge(idx_ready, t + 1)
                pool.sem_inc(gathering, 1)
                pool.indirect_dma_start(kk[:, u, :], None, k_tab[:, :],
                                        bass.IndirectOffsetOnAxis(ap=idx[:, u, WIN + 1:WIN + 2], axis=0),
                                        bounds_check=last_node, oob_is_err=False).then_inc(qv_in[u], 16)
                for w in range(WIN):
                    pool.indirect_dma_start(qv[:, u, w, :, :].rearrange("p h c -> p (h c)"), None, qv_tab[:, :],
                                            bass.IndirectOffsetOnAxis(ap=idx[:, u, w:w + 1], axis=0),
                                            bounds_check=last_node, oob_is_err=False).then_inc(qv_in[u], 16)

            pool.wait_ge(k_out, 48)
            for u in range(2):
                pool.wait_ge(qv_out[u], 16 * (NB // 2))
            for u in range(RING):
                gather_qv(u, u)
            with pool.Fori(1, LANE_ROWS // RING) as i:
                for u in range(RING):
                    gather_qv(4 * i + u, u)

            pool.wait_ge(win_done, 2)
            for u in range(RING):
                pool.wait_ge(hist_out[u], 32 * (LANE_ROWS // RING))
            pool.indirect_dma_start(hst[:, 0:CH], None, hist_m[:, :], bass.IndirectOffsetOnAxis(ap=lane_j[:, 0:1], axis=0),
                                    bounds_check=ROWS - 1, oob_is_err=False).then_inc(hst_in, 16)
            pool.indirect_dma_start(hst[:, CH:3 * CH], None, hist_zs[0:ROWS, :], bass.IndirectOffsetOnAxis(ap=lane_j[:, 0:1], axis=0),
                                    bounds_check=ROWS - 1, oob_is_err=False).then_inc(hst_in, 16)
            pool.wait_ge(join_out, 16)

            for b in range(NB):
                pool.indirect_dma_start(fin[:, b, :, :].rearrange("p k c -> p (k c)"), None, hist_zs[:, :],
                                        bass.IndirectOffsetOnAxis(ap=fidx[:, b:b + 1], axis=0),
                                        bounds_check=ROWS + P - 1, oob_is_err=False).then_inc(fin_in[fin_group(b)], 16)

            def gather_msg(t, u):
                pool.wait_ge(idx_ready, LANE_ROWS + RING + t + 1)
                pool.sem_inc(gathering, 1)
                pool.indirect_dma_start(eat[:, u, :], None, edge[:, :],
                                        bass.IndirectOffsetOnAxis(ap=idx[:, u, WIN:WIN + 1], axis=0),
                                        bounds_check=last_window, oob_is_err=False).then_inc(msg_in[u], 16)
                for w in range(WIN):
                    pool.indirect_dma_start(hmsg[:, u, w, :], None, h_tab[:, :],
                                            bass.IndirectOffsetOnAxis(ap=idx[:, u, w:w + 1], axis=0),
                                            bounds_check=last_node, oob_is_err=False).then_inc(msg_in[u], 16)

            pool.wait_ge(fin_used, 3)
            pool.wait_ge(h_out, 48)
            def gather_h(t, u):
                pool.wait_ge(idx_ready, LANE_ROWS + RING + t + 1)
                pool.sem_inc(gathering, 1)
                for w in range(WIN):
                    pool.indirect_dma_start(parts[:, u, 0, w, :], None, h_tab[:, :],
                                            bass.IndirectOffsetOnAxis(ap=idx[:, u, w:w + 1], axis=0),
                                            bounds_check=last_node, oob_is_err=False).then_inc(msg_in[u], 16)

            def gather_agg(states):
                pool.wait_ge(joina_out, 16)
                for b in range(NB):
                    if b >= FRING:
                        pool.wait_ge(agg_add, b - FRING + 1)
                    pool.indirect_dma_start(aggs[:, b % FRING, :], None, hist_a[0:states, :],
                                            bass.IndirectOffsetOnAxis(ap=fidx[:, b:b + 1], axis=0),
                                            bounds_check=states - 1, oob_is_err=False).then_inc(agg_in[b % FRING], 16)

            pool.wait_ge(path_known, 1)
            rows_needed = pool.value_load(small_i[0:1, 0:1], min_val=0, max_val=1)
            with pool.If(rows_needed == 0):
                for u in range(RING):
                    gather_h(u, u)
                with pool.Fori(1, LANE_WIN // RING) as i:
                    for u in range(RING):
                        gather_h(4 * i + u, u)
                gather_h(LANE_WIN - 1, 0)
                for u in range(RING):
                    pool.wait_ge(hista_out[u], 16 * (LANE_WIN // RING + (u == 0)))
                pool.wait_ge(flag_in, 1)
                pool.indirect_dma_start(hst[:, 0:CH], None, hist_a[0:LANE_STATES, :], bass.IndirectOffsetOnAxis(ap=lane_j[:, 2:3], axis=0),
                                        bounds_check=LANE_STATES - 1, oob_is_err=False).then_inc(hsa_in, 16)
                gather_agg(LANE_STATES + P)
            with pool.Else():
                for u in range(RING):
                    gather_msg(u, u)
                with pool.Fori(1, LANE_ROWS // RING) as i:
                    for u in range(RING):
                        gather_msg(4 * i + u, u)
                for u in range(RING):
                    pool.wait_ge(hista_out[u], 16 * (LANE_ROWS // RING))
                pool.indirect_dma_start(hst[:, 0:CH], None, hist_a[0:ROWS, :], bass.IndirectOffsetOnAxis(ap=lane_j[:, 0:1], axis=0),
                                        bounds_check=ROWS - 1, oob_is_err=False).then_inc(hsa_in, 16)
                gather_agg(ROWS + P)

        @block.scalar
        def _(act):
            def relu_ln(n, c):
                std_of_var(n, c)
                act.wait_ge(ln_norm, n)
                for b in range(c * LN_CHUNK, (c + 1) * LN_CHUNK):
                    act.activation(hs[:, b, :], xs[:, b, :], ACT.Relu, bias=nmr[:, b:b + 1],
                                   scale=rstd[:, b:b + 1]).then_inc(h_ready, 1)

            def std_of_var(n, c):
                part = slice(c * LN_CHUNK, (c + 1) * LN_CHUNK)
                act.wait_ge(ln_var, n)
                act.activation(rstd[:, part], mv[:, part, 1], ACT.Sqrt, bias=eps[:, 0:1]).then_inc(ln_std, 1)

            act.wait_ge(src_in, 16)
            for d in range(4):
                act.activation(src4_sb.rearrange("p (w d s) -> p w d s", d=4, s=WIN)[:, :, d, :],
                               src_sb[:, d * WIN:(d + LANE_WIN) * WIN].rearrange("p (w s) -> p w s", s=WIN), ACT.Copy)\
                   .then_inc(src4_done, 1)
            for c in range(3):
                relu_ln(c + 1, c)
            for c in range(3):
                std_of_var(c + 4, c)
            act.wait_ge(ln_norm, 6)
            act.wait_ge(par_in, 16)

            def normalise(b, u, warm):
                if warm:
                    act.wait_ge(tr_ready, b - 1)
                act.activation(xn[:, u, :], hs[:, b, :], ACT.Identity, bias=nmr[:, bass.ds(b, 1)],
                               scale=rstd[:, bass.ds(b, 1)]).then_inc(xn_ready, 1)

            def scale_T(b, u, warm):
                act.wait_ge(tr_ready, b + 1)
                if warm:
                    act.wait_ge(qkv_ready, b - 1)
                for h in range(2):
                    last = act.activation(xT[:, u, h, :], banks[u][:, h * P:(h + 1) * P], ACT.Identity,
                                          bias=pv("beta", h), scale=pv("gamma", h))
                last.then_inc(xT_ready, 1)

            def evac_qkv(b, u, warm):
                act.wait_ge(qkv_ready, b + 1)
                if warm:
                    act.wait_ge(qv_out[u], 8 * b - 8 * u)
                act.activation(stage[:, u, :], banks[2 + u][:, :], ACT.Copy)
                act.activation(ks[:, bass.ds(b * CH, CH)], banks[4 + u][:, 0:CH], ACT.Copy).then_inc(qkv_evac, 1)

            normalise(0, 0, False)
            normalise(1, 1, False)
            scale_T(0, 0, False)
            for b in (2, 3):
                normalise(b, b % 2, True)
                scale_T(b - 1, (b - 1) % 2, b > 2)
                evac_qkv(b - 2, b % 2, False)
            with act.Fori(2, NB // 2) as i:
                for u in range(2):
                    normalise(2 * i + u, u, True)
                    scale_T(2 * i + u - 1, 1 - u, True)
                    evac_qkv(2 * i + u - 2, u, True)
            scale_T(NB - 1, 1, True)
            evac_qkv(NB - 2, 0, True)
            evac_qkv(NB - 1, 1, True)

            def next_idx(i, u):
                act.activation(idx[:, u, :], pack[:, 4 * i + u + RING, :], ACT.Copy).then_inc(idx_ready, 1)

            def first_idx(slots=range(RING)):
                for u in slots:
                    act.activation(idx[:, u, :], pack[:, u, :], ACT.Copy).then_inc(idx_ready, 1)

            def exps(i, u):
                act.wait_ge(a_step, 28 * i + 7 * u + 6)
                for w in range(WIN - PE_SLOTS):
                    last = act.activation(qv[:, u, w, 0, :], qv[:, u, w, 0, :], ACT.Exp,
                                          bias=sneg[:, 4 * i + u, w:w + 1], scale=SCALE)
                    if w == WIN // 2 - 1:
                        last.then_inc(exp_ready, 1)
                act.wait_ge(a_step, 28 * i + 7 * u + 7)
                act.activation(alpha[:, u % 2, :], alpha[:, u % 2, :], ACT.Exp, scale=SCALE).then_inc(exp_ready, 1)
                act.wait_ge(diff_ready, 4 * i + u + 1)
                for k in range(PE_SLOTS):
                    w = WIN - PE_SLOTS + k
                    last = act.activation(qv[:, u, w, 0, :], banks[2 + u % 2][:, k * CH:(k + 1) * CH], ACT.Exp,
                                          bias=sneg[:, 4 * i + u, w:w + 1], scale=SCALE)
                last.then_inc(exp_ready, 1)

            def evac_state(i, u):
                act.wait_ge(psum_ready, 4 * i + u + 1)
                act.activation(zs[:, u, :], banks[u % 2][:, :], ACT.Copy).then_inc(state_ready, 1)
                next_idx(i, u)

            act.wait_ge(qidx_done, 1)
            first_idx(range(RING // 2))
            act.wait_ge(qidx_done, 2)
            first_idx(range(RING // 2, RING))
            exps(0, 0)
            for u in range(1, RING):
                exps(0, u)
                evac_state(0, u - 1)
            with act.Fori(1, LANE_ROWS // RING) as i:
                for u in range(RING):
                    exps(i, u)
                    evac_state(i if u else i - 1, (u - 1) % RING)
            evac_state(LANE_ROWS // RING - 1, RING - 1)

            act.wait_ge(join_arg, 1)
            act.activation(join[:, 18:26, :], join[:, 18:26, :], ACT.Exp, scale=SCALE).then_inc(join_exp, 1)

            def guess(c):
                part = slice(c * LN_CHUNK, (c + 1) * LN_CHUNK)
                act.wait_ge(fin_in[fin_group(c * LN_CHUNK)], 16 * LN_CHUNK)
                act.activation(hs[:, part, :], fin[:, part, 0, :], ACT.Ln).then_inc(z_guess, 1)
                act.wait_ge(z_guess, 2 * c - 1)
                act.activation(hs[:, part, :], hs[:, part, :], ACT.Exp, scale=-1.0).then_inc(z_guess, 1)

            guess(1)
            relu_ln(7, 0)
            guess(2)
            relu_ln(8, 1)
            relu_ln(9, 2)

            def relus(i, u):
                act.wait_ge(added, 4 * i + u + 1)
                for w in range(WIN):
                    last = act.activation(hmsg[:, u, w, :], hmsg[:, u, w, :], ACT.Relu,
                                          bias=sneg[:, 4 * i + u, w:w + 1])
                last.then_inc(relued, 1)

            def evac_acc(i, u):
                act.wait_ge(sum_ready, 4 * i + u + 1)
                act.activation(acc[:, u, :], banks[u % 2][:, 0:CH], ACT.Copy).then_inc(acc_ready, 1)
                next_idx(i, u)

            def relus_parts(i, u, idx_for_next=True):
                act.wait_ge(added, 4 * i + u + 1)
                half = WIN // 2
                t = bass.ds(4 * i + u, 1)
                for k in range(2):
                    slots = range(k * half, (k + 1) * half)
                    for w in slots:
                        last = act.activation(parts[:, u, 1, w, :], parts[:, u, 0, w, :], ACT.Relu,
                                              bias=later_neg[:, t, w:w + 1].rearrange("p a b -> p (a b)"))
                    last.then_inc(later_relued, 1)
                    act.wait_ge(later_relued, 8 * i + 2 * u + k + 1)
                    for w in slots:
                        last = act.activation(parts[:, u, 0, w, :], parts[:, u, 0, w, :], ACT.Relu,
                                              bias=first_neg[:, t, w:w + 1].rearrange("p a b -> p (a b)"))
                    last.then_inc(relued, 1)
                if idx_for_next:
                    act.wait_ge(sum_ready, 4 * i + u)
                    act.activation(idx[:, (u - 1) % RING, 0:WIN], src_l[:, bass.ds((4 * i + u + RING - 1) * WIN, WIN)],
                                   ACT.Copy).then_inc(idx_ready, 1)

            act.wait_ge(path_known, 1)
            rows_needed = act.value_load(small_i[0:1, 0:1], min_val=0, max_val=1)
            with act.If(rows_needed == 0):
                act.wait_ge(lanes_in, 32)
                for u in range(RING):
                    act.activation(idx[:, u, 0:WIN], src_l[:, u * WIN:(u + 1) * WIN], ACT.Copy).then_inc(idx_ready, 1)
                for u in range(RING):
                    relus_parts(0, u, u > 0)
                with act.Fori(1, LANE_WIN // RING) as i:
                    for u in range(RING):
                        relus_parts(i, u)
                relus_parts(LANE_WIN // RING, 0, False)
            with act.Else():
                first_idx()
                relus(0, 0)
                for u in range(1, RING):
                    relus(0, u)
                    evac_acc(0, u - 1)
                with act.Fori(1, LANE_ROWS // RING) as i:
                    for u in range(RING):
                        relus(i, u)
                        evac_acc(i if u else i - 1, (u - 1) % RING)
                evac_acc(LANE_ROWS // RING - 1, RING - 1)

            def columns(b, u):
                act.wait_ge(agg_tr, b + 1)
                act.activation(hT[:, :, bass.ds(b * NP, NP)],
                               banks[1 + u][:, 0:2 * P].rearrange("p (m n) -> p m n", m=2)[:, :, 0:NP],
                               ACT.Copy).then_inc(agg_cp, 1)

            def bias1(n, u):
                for m in range(4):
                    act.wait_ge(y1_mm, 4 * n + m + 1)
                    act.activation(y1[:, m, bass.ds(n * CCOLS, CCOLS)], banks[4 + m][:, 0:CCOLS], ACT.Identity,
                                   bias=pv("b1", m)).then_inc(y1_ev, 1)

            for b in range(6):
                columns(b, b % 3)
            for n in range(2):
                for b in range(3 * n + 6, 3 * n + 9):
                    columns(b, b % 3)
                bias1(n, 0)
            with act.Fori(2, NCHUNK // 2) as i:
                for c in range(2):
                    for b in range(3 * c, 3 * c + 3):
                        columns(6 * i + b, b % 3)
                    bias1(2 * i - 2 + c, 0)
            for n in range(NCHUNK - 2, NCHUNK):
                bias1(n, 0)
            act.wait_ge(bn_var, 1)
            act.activation(bn[:, 0, :], bn[:, 0, :], ACT.Sqrt, bias=eps[:, 0:1]).then_inc(bn_std, 1)
            act.wait_ge(bn_ready, 1)

            def relu1(n):
                for m in range(4):
                    last = act.activation(y1[:, m, bass.ds(n * CCOLS, CCOLS)], y1[:, m, bass.ds(n * CCOLS, CCOLS)],
                                          ACT.Relu, bias=bn[:, 2, m:m + 1], scale=bn[:, 1, m:m + 1])
                last.then_inc(y1_act, 1)

            def bias2(n, u):
                act.wait_ge(y2_mm, n + 1)
                for m in range(2):
                    last = act.activation(y2[:, m, bass.ds(n * CCOLS, CCOLS)], banks[2 * u + m][:, 0:CCOLS],
                                          ACT.Identity, bias=pv("b2", m))
                last.then_inc(y2_ev, 1)

            relu1(0)
            relu1(1)
            bias2(0, 0)
            with act.Fori(1, NCHUNK // 2) as i:
                for u in range(2):
                    relu1(2 * i + u)
                    bias2(2 * i + u - 1, 1 - u)
            bias2(NCHUNK - 1, 1)
            for n in range(2):
                act.wait_ge(g_var, n + 1)
                act.activation(gn[:, 12, :], gn[:, 12, :], ACT.Sqrt, bias=eps[:, 0:1]).then_inc(g_std, 1)
            act.wait_ge(g_ready, 1)

            for n in range(NCHUNK):
                for m in range(2):
                    last = act.activation(y2[:, m, n * CCOLS:(n + 1) * CCOLS], y2[:, m, n * CCOLS:(n + 1) * CCOLS],
                                          ACT.Relu, bias=gn[:, 14, m:m + 1], scale=gn[:, 13, m:m + 1])
                last.then_inc(out_aff, 1)

        @block.tensor
        def _(pe):
            pe.wait_ge(consts, 2)
            pe.wait_ge(w_in, 48)

            def turn(b, u, warm):
                pe.wait_ge(xn_ready, b + 1)
                if warm:
                    pe.wait_ge(xT_ready, b - 1)
                for h in range(2):
                    last = pe.transpose(banks[u][:, h * P:(h + 1) * P], xn[:, u, h * P:(h + 1) * P], ident[:, :])
                last.then_inc(tr_ready, 1)

            def project(b, u, warm):
                pe.wait_ge(xT_ready, b + 1)
                if warm:
                    pe.wait_ge(qkv_evac, b - 1)
                for h in range(2):
                    pe.matmul(banks[2 + u][:, :], xT[:, u, h, :], wq_sb[:, h, 0:2 * CH], start=(h == 0), stop=(h == 1))
                for h in range(2):
                    last = pe.matmul(banks[4 + u][:, 0:CH], xT[:, u, h, :], wq_sb[:, h, 2 * CH:3 * CH],
                                     start=(h == 0), stop=(h == 1))
                last.then_inc(qkv_ready, 1)

            turn(0, 0, False)
            turn(1, 1, False)
            project(0, 0, False)
            turn(2, 0, True)
            project(1, 1, False)
            turn(3, 1, True)
            project(2, 0, True)
            def tiles(first, behind):
                with pe.Fori(first, behind) as i:
                    for u in range(2):
                        turn(2 * i + u, u, True)
                        project(2 * i + u - 1, 1 - u, True)

            pe.wait_ge(small_in, 1)
            pe.matmul(banks[6][:, 0:1], upper[:, :], incl[:, NB - 1:NB], start=True, stop=True)
            pe.matmul(banks[6][:, 1:2], ones[:, :], incl[:, NB - 1:NB], start=True, stop=True).then_inc(small_out, 1)
            tiles(2, FIELDS_AT)
            pe.wait_ge(small_in, 2)
            pe.transpose(banks[6][0:NF, P:2 * P], l3[:, :], ident[:, :]).then_inc(small_out, 1)
            pe.wait_ge(small_in, 3)
            pe.transpose(banks[6][:, 2 * P:2 * P + NF], l3t[:, 1, :], ident[0:NF, 0:NF]).then_inc(small_out, 1)
            tiles(FIELDS_AT, NB // 2)
            project(NB - 1, 1, True)
            pe.wait_ge(small_in, 4)
            pe.matmul(banks[7][:, 0:P], ones[:, :], flagd[:, :], start=True, stop=True)
            pe.matmul(banks[7][:, P:P + 1], ones[:, :], small_any[:, :], start=True, stop=True).then_inc(small_out, 1)

            def take_logits(i, u, warm):
                pe.wait_ge(a_step, 28 * i + 7 * u + 1)
                if warm:
                    pe.wait_ge(exp_ready, 12 * i + 3 * u - 3)
                pe.matmul(banks[2 + u % 2][:, :].rearrange("p (e c) -> p e c", c=CH), ident[:, :],
                          qv[:, u, WIN - PE_SLOTS:, 0, :], start=True, stop=False)

            def take_maximum(i, u):
                pe.wait_ge(a_step, 28 * i + 7 * u + 5)
                pe.matmul(banks[2 + u % 2][:, :].rearrange("p (e c) -> p e c", c=CH), neg_ident,
                          top[:, u, :][:, None, :].to_broadcast([P, PE_SLOTS, CH]), start=False, stop=True)\
                  .then_inc(diff_ready, 1)

            def sum_slots(i, u, warm, further=True):
                if warm:
                    pe.wait_ge(state_ready, 4 * i + u - 1)
                nxt = (i, u + 1) if u + 1 < RING else (i + 1, 0)
                for w in range(WIN):
                    if w == WIN // 2 and further:
                        take_logits(*nxt, not (isinstance(i, int) and (i, u) == (0, 0)))
                    if w % (WIN // 2) == 0:
                        pe.wait_ge(weighted, 12 * i + 3 * u + 1 + w // (WIN // 2))
                    pe.matmul(banks[u % 2][:, :], ident[:, :], qv[:, u, w, :, :].rearrange("p h c -> p (h c)"),
                              start=(w == 0), stop=False)
                if further:
                    take_maximum(*nxt)
                pe.wait_ge(weighted, 12 * i + 3 * u + 3)
                pe.matmul(banks[u % 2][:, :], ident[:, :], carry[:, u % 2, :], start=False, stop=True)\
                  .then_inc(psum_ready, 1)

            take_logits(0, 0, False)
            take_maximum(0, 0)
            for u in range(RING):
                sum_slots(0, u, u > 1)
            with pe.Fori(1, LANE_ROWS // RING - 1) as i:
                for u in range(RING):
                    sum_slots(i, u, True)
            for u in range(RING):
                sum_slots(LANE_ROWS // RING - 1, u, True, u + 1 < RING)

            def turn_all(pairs):
                for to, of in pairs:
                    last = pe.transpose(to, of, ident[:, :])
                last.then_inc(small_out, 1)

            pe.wait_ge(state_ready, LANE_ROWS)
            pe.wait_ge(hst_in, 32)
            end = [top[:, RING - 1, n * P:(n + 1) * P] for n in range(2)] + [zs[:, RING - 1, n * P:(n + 1) * P] for n in range(4)] + [hst[:, n * P:(n + 1) * P] for n in range(6)]
            turn_all([(banks[2 + n // 4][:, n % 4 * P:(n % 4 + 1) * P], e) for n, e in enumerate(end)])
            pe.wait_ge(small_in, 5)
            turn_all([(banks[2][:, n * P:(n + 1) * P], join[:, 8 + n, :]) for n in range(4)])

            def sum_msgs(i, u, warm):
                pe.wait_ge(relued, 4 * i + u + 1)
                if warm:
                    pe.wait_ge(acc_ready, 4 * i + u - 1)
                for w in range(WIN):
                    pe.matmul(banks[u % 2][:, 0:CH], ident[:, :], hmsg[:, u, w, :], start=(w == 0), stop=False)
                pe.wait_ge(carried, 4 * i + u + 1)
                pe.matmul(banks[u % 2][:, 0:CH], ident[:, :], carry[:, u % 2, 0:CH], start=False, stop=True)\
                  .then_inc(sum_ready, 1)

            def sum_parts(i, u, warm):
                if warm:
                    pe.wait_ge(acc_ready, 4 * i + u - 1)
                half = WIN // 2
                for w in range(WIN):
                    if w % half == 0:
                        pe.wait_ge(relued, 8 * i + 2 * u + 1 + w // half)
                    last = pe.matmul(banks[u % 2][:, :].rearrange("p (h c) -> p h c", h=2), ident[:, :],
                                     parts[:, u, :, w, :], start=(w == 0), stop=(w == WIN - 1))
                last.then_inc(sum_ready, 1)

            def turn_ends(state):
                end = [state[:, n * P:(n + 1) * P] for n in range(2)] + [hst[:, n * P:(n + 1) * P] for n in range(2)]
                turn_all([(banks[2][:, n * P:(n + 1) * P], e) for n, e in enumerate(end)])

            pe.wait_ge(path_known, 1)
            rows_needed = pe.value_load(small_i[0:1, 0:1], min_val=0, max_val=1)
            with pe.If(rows_needed == 0):
                pe.wait_ge(flag_in, 1)
                pe.matmul(banks[7][:, 0:P], ones[:, :], flagd[:, :], start=True, stop=True).then_inc(flag_out, 1)
                for u in range(RING):
                    sum_parts(0, u, u > 1)
                with pe.Fori(1, LANE_WIN // RING) as i:
                    for u in range(RING):
                        sum_parts(i, u, True)
                sum_parts(LANE_WIN // RING, 0, True)
                pe.wait_ge(acc_ready, LANE_WIN)
                pe.wait_ge(hsa_in, 16)
                turn_ends(zs[:, (LANE_WIN - 1) % RING, CH:2 * CH])
            with pe.Else():
                for u in range(RING):
                    sum_msgs(0, u, u > 1)
                with pe.Fori(1, LANE_ROWS // RING) as i:
                    for u in range(RING):
                        sum_msgs(i, u, True)
                pe.wait_ge(acc_ready, LANE_ROWS)
                pe.wait_ge(hsa_in, 16)
                turn_ends(acc[:, RING - 1, :])
            pe.wait_ge(small_in, 6)
            turn_all([(banks[2][:, n * P:(n + 1) * P], join[:, 2 + n, :]) for n in range(2)])

            def turn_agg(b, u, warm):
                pe.wait_ge(agg_add, b + 1)
                if warm:
                    pe.wait_ge(agg_cp, b - 2)
                for h in range(2):
                    last = pe.transpose(banks[1 + u][:, h * P:(h + 1) * P], turning[u][:, h * P:(h + 1) * P], ident[:, :])
                last.then_inc(agg_tr, 1)

            def dense1(n, u, warm):
                pe.wait_ge(agg_cp, 3 * n + 3)
                for m in range(4):
                    if warm:
                        pe.wait_ge(y1_ev, 4 * n + m - 3)
                    for h in range(2):
                        last = pe.matmul(banks[4 + m][:, 0:CCOLS], w1_sb[:, h, m * P:(m + 1) * P],
                                         hT[:, h, bass.ds(n * CCOLS, CCOLS)], start=(h == 0), stop=(h == 1))
                    last.then_inc(y1_mm, 1)

            for b in range(6):
                turn_agg(b, b % 3, b > 2)
            dense1(0, 0, False)
            for b in range(6, 9):
                turn_agg(b, b % 3, True)
            dense1(1, 1, True)
            for b in range(9, 12):
                turn_agg(b, b % 3, True)
            dense1(2, 0, True)
            with pe.Fori(2, NCHUNK // 2) as i:
                for c in range(2):
                    for b in range(3 * c, 3 * c + 3):
                        turn_agg(6 * i + b, b % 3, True)
                    dense1(2 * i - 1 + c, 0, True)
            dense1(NCHUNK - 1, 0, True)

            def dense2(n, u, warm):
                pe.wait_ge(y1_act, n + 1)
                if warm:
                    pe.wait_ge(y2_ev, n - 1)
                for m in range(2):
                    for h in range(4):
                        last = pe.matmul(banks[2 * u + m][:, 0:CCOLS], w2_sb[:, h, m * P:(m + 1) * P],
                                         y1[:, h, bass.ds(n * CCOLS, CCOLS)], start=(h == 0), stop=(h == 3))
                last.then_inc(y2_mm, 1)

            dense2(0, 0, False)
            dense2(1, 1, False)
            with pe.Fori(1, NCHUNK // 2) as i:
                for u in range(2):
                    dense2(2 * i + u, u, True)
            for n in range(2):
                pe.wait_ge(small_in, 7 + n)
                pe.matmul(banks[6][:, 2 * n:2 * n + 2], ones[:, :], gn[:, 3 * n, :], start=True, stop=True)\
                  .then_inc(small_out, 1)

            for q in range(NB // 2):
                pe.wait_ge(out_aff, (2 * q + 1) // 3 + 1)
                if q >= 3:
                    pe.wait_ge(out_add, q - 2)
                for k in range(2):
                    for h in range(2):
                        last = pe.transpose(banks[q % 3][0:NP, (2 * k + h) * P:(2 * k + h + 1) * P],
                                            y2[:, h, (2 * q + k) * NP:(2 * q + k + 1) * NP], ident[:, :])
                last.then_inc(out_tr, 1)

        @block.vector
        def _(v):
            count = [0]

            def step(ins):
                count[0] += 1
                ins.then_inc(dve, 1)
                v.wait_ge(dve, count[0])

            def bc_last(a, n):
                return a[:, :, None].to_broadcast([P, a.shape[1], n])

            def bc_mid(a, n):
                return a[:, None, :].to_broadcast([P, n, a.shape[1]])

            step(v.memset(eps[:, :], EPS))
            v.wait_ge(dst_in, 16)
            v.tensor_copy(dlast_sb, dst_sb.rearrange("p (b n) -> p b n", n=BLK)[:, :, BLK - 1]).then_inc(dstf_done, 1)
            v.tensor_copy(dstf_sb, dst_sb).then_inc(dstf_done, 1)

            def ln_stats(t, n, c):
                for b in range(c * LN_CHUNK, (c + 1) * LN_CHUNK):
                    v.bn_stats(stats[:, b, :], t[:, b, :]).then_inc(bnst, 1)
                v.wait_ge(bnst, n * LN_CHUNK)
                for b in range(c * LN_CHUNK, (c + 1) * LN_CHUNK):
                    last = v.bn_aggr(mv[:, b, :], stats[:, b, :])
                last.then_inc(ln_var, 1)

            def ln_scale(n, c):
                part = slice(c * LN_CHUNK, (c + 1) * LN_CHUNK)
                v.wait_ge(ln_std, n)
                step(v.reciprocal(rstd[:, part], rstd[:, part]))
                v.scalar_tensor_tensor(out=nmr[:, part], in0=mv[:, part, 0], scalar=-1.0, in1=rstd[:, part],
                                       op0=ALU.mult, op1=ALU.mult).then_inc(ln_norm, 1)

            v.wait_ge(iotas, 3)
            step(v.tensor_copy(nid[:, :], nid_i[:, :]))
            v.wait_ge(blk_in, 16)
            for c, part in enumerate(spans):
                for b in part:
                    last = v.tensor_scalar(cmp1[:, b % SCH, :], blk_sb, nid[:, b:b + 1], None, ALU.is_lt, ALU.add,
                                           accum_out=cnt[:, b:b + 1])
                step(last)
                cols = slice(part[0], part[-1] + 1)
                step(v.tensor_scalar(cnt[:, cols], cnt[:, cols], float(NBLK - 1), None, ALU.min))
                v.tensor_copy(blk_i[:, cols], cnt[:, cols]).then_inc(blk_done, 1)
            for c in range(3):
                v.wait_ge(x_in[c], 16)
                ln_stats(xs, c + 1, c)
                if c:
                    ln_scale(c, c - 1)
            def search_fine(c):
                v.wait_ge(blk_gathered[c], 16 * len(spans[c]))
                for b in spans[c]:
                    last = v.tensor_scalar(dblk[:, b, :], dblk[:, b, :], nid[:, b:b + 1], None, ALU.is_lt, ALU.add,
                                           accum_out=start[:, b:b + 1])
                return last

            for c in range(len(spans) // 2):
                search_fine(c)
            ln_scale(3, 2)
            for c in range(3):
                v.wait_ge(h_ready, LN_CHUNK * (c + 1))
                ln_stats(hs, c + 4, c)
                if c:
                    ln_scale(c + 3, c - 1)
            ln_scale(6, 2)
            for c in range(len(spans) // 2, len(spans)):
                last = search_fine(c)
            step(last)
            step(v.scalar_tensor_tensor(out=start[:, :], in0=cnt[:, :], scalar=float(BLK), in1=start[:, :],
                                        op0=ALU.mult, op1=ALU.add))
            step(v.tensor_copy(n_i[:, 0, :], start[:, :]))
            step(v.tensor_scalar(n_i[:, 1, :], start[:, :], float(WIN - 1), None, ALU.add))
            step(v.tensor_scalar(n_i[:, :, :], n_i[:, :, :], 3, None, ALU.arith_shift_right))
            step(v.tensor_copy(s3[:, :, :], n_i[:, :, :]))
            st, en = start[:, 0:NB], start[:, 1:NB + 1]
            step(v.tensor_tensor(has[:, :], en, st, ALU.is_gt))
            step(v.tensor_tensor(nrow[:, :], s3[:, 1, 1:NB + 1], s3[:, 0, 0:NB], ALU.subtract))
            step(v.tensor_tensor(nrow[:, :], nrow[:, :], has[:, :], ALU.mult))
            v.wait_ge(memsets, 1)
            v.tensor_tensor_scan(incl[:, :], nrow[:, :], zeros[:, 0:NB], 0.0, ALU.add, ALU.add).then_inc(small_in, 1)
            v.wait_ge(small_out, 1)
            step(v.tensor_copy(offs[:, :], banks[6][:, 0:2]))
            step(v.scalar_tensor_tensor(out=rs[:, :], in0=incl[:, :], scalar=offs[:, 0:1], in1=nrow[:, :],
                                        op0=ALU.add, op1=ALU.subtract))
            step(v.tensor_scalar(nt[:, 0, :], has[:, :], -FAR, FAR, ALU.mult, ALU.add))
            step(v.tensor_tensor(nt[:, 0, :], nt[:, 0, :], rs[:, :], ALU.add))
            step(v.tensor_copy(sidx[:, :], nt[:, 0, :]))
            step(v.tensor_copy(mk[:, :, 0], st))
            step(v.tensor_copy(mk[:, :, 1], en))
            step(v.tensor_copy(mk[:, :, 3], nid[:, 0:NB]))
            v.tensor_tensor(mk[:, :, 2], rs[:, :], s3[:, 0, 0:NB], ALU.subtract).then_inc(node_done, 1)
            last_row, lane_f, lane_l, t = (nt[:, n, :] for n in range(4))
            step(v.scalar_tensor_tensor(out=last_row, in0=rs[:, :], scalar=-1.0, in1=nrow[:, :], op0=ALU.add, op1=ALU.add))
            middle = (LANE_ROWS - 1) / 2
            step(v.tensor_scalar(lane_i[:, 0, :], rs[:, :], -middle, 1.0 / LANE_ROWS, ALU.add, ALU.mult))
            step(v.tensor_scalar(lane_i[:, 1, :], last_row, -middle, 1.0 / LANE_ROWS, ALU.add, ALU.mult))
            step(v.tensor_copy(nt[:, 1:3, :], lane_i[:, :, :]))
            step(v.scalar_tensor_tensor(out=t, in0=lane_l, scalar=float(ROWS), in1=last_row, op0=ALU.add, op1=ALU.subtract))
            step(v.tensor_tensor(lane_f, lane_l, lane_f, ALU.is_gt))
            step(v.tensor_tensor(t, t, lane_f, ALU.mult))
            step(v.tensor_tensor(t, t, last_row, ALU.add))
            step(v.tensor_tensor(t, t, has[:, :], ALU.mult))
            step(v.tensor_copy(fidx[:, :], t))

            v.wait_ge(marks_in, 16)
            v.wait_ge(src4_out, 16)
            for f in range(NF):
                step(v.tensor_tensor_scan(fld[:, f, :], mkr[:, :, f], mkr[:, :, f], 0.0, ALU.max, ALU.max))
            v.tensor_copy(l3[:, :], fld[:, :, LANE_ROWS - 1]).then_inc(small_in, 1)
            v.wait_ge(small_out, 2)
            step(v.tensor_copy(l3t[:, 0, :], banks[6][0:NF, P:2 * P]))
            step(v.memset(l3t[:, 1, :], 0.0))
            v.tensor_tensor_scan(l3t[:, 1, 1:P], l3t[:, 0, 0:P - 1], l3t[:, 0, 0:P - 1], 0.0, ALU.max, ALU.max)\
             .then_inc(small_in, 1)
            v.wait_ge(small_out, 3)
            step(v.tensor_copy(l3[:, :], banks[6][:, 2 * P:2 * P + NF]))
            for f in range(NF):
                step(v.tensor_scalar(fld[:, f, :], fld[:, f, :], l3[:, f:f + 1], None, ALU.max))
            step(v.tensor_copy(row[:, :], row_i[:, :]))
            step(v.tensor_tensor(win, row[:, :], fld[:, 2, :], ALU.subtract))
            step(v.tensor_scalar(t0, win, float(WIN), None, ALU.mult))
            step(v.tensor_scalar(winc, win, float(NWIN - 1), None, ALU.min))
            v.tensor_copy(win_i[:, :], winc).then_inc(win_done, 1)
            step(v.tensor_scalar(lane_j[:, 0:1], fld[:, 1, 0:1], -1.0, None, ALU.add))
            step(v.tensor_scalar(lane_j[:, 0:1], lane_j[:, 0:1], 3, None, ALU.arith_shift_right))
            step(v.tensor_copy(lane[:, 0:1], lane_j[:, 0:1]))
            step(v.tensor_tensor(lane[:, 0:1], lane[:, 0:1], fld[:, 2, 0:1], ALU.add))
            step(v.tensor_tensor(lane[:, 0:1], lane[:, 0:1], row[:, LANE_ROWS - 1:LANE_ROWS], ALU.min))
            v.tensor_copy(lane_j[:, 0:1], lane[:, 0:1]).then_inc(win_done, 1)
            step(v.tensor_tensor(brk[:, :], t0, fld[:, 0, :], ALU.is_le))
            step(v.tensor_scalar(t1, row[:, :], offs[:, 1:2], None, ALU.is_ge))
            step(v.tensor_tensor(brk[:, :], brk[:, :], t1, ALU.max))
            step(v.tensor_scalar(acont[:, :], brk[:, :], -1.0, 1.0, ALU.mult, ALU.add))
            step(v.tensor_scalar(mneg[:, :], brk[:, :], NEG, None, ALU.mult))
            step(v.tensor_reduce(lane[:, 2:3], brk[:, :], AX.X, ALU.max))
            step(v.tensor_scalar(lane[:, 3:4], lane[:, 2:3], -1.0, 1.0, ALU.mult, ALU.add))
            step(v.tensor_tensor(small[:, :], en, st, ALU.subtract))
            step(v.tensor_scalar(small[:, :], small[:, :], WIN - 1.5, None, ALU.is_lt))
            step(v.tensor_tensor(small[:, :], small[:, :], has[:, :], ALU.mult))
            step(v.tensor_reduce(small_any[:, :], small[:, :], AX.X, ALU.max))
            v.tensor_scalar(flagd[:, :], ident[:, :], lane[:, 3:4], None, ALU.mult).then_inc(small_in, 1)
            step(v.tensor_copy(wslot[:, :], w_i[:, :]))
            step(v.tensor_tensor(valid, bc_last(t0, WIN), bc_mid(wslot, LANE_ROWS), ALU.add))
            step(v.tensor_tensor(srow, valid, bc_last(fld[:, 0, :], WIN), ALU.is_ge))
            step(v.tensor_tensor(valid, valid, bc_last(fld[:, 1, :], WIN), ALU.is_lt))
            step(v.tensor_tensor(valid, valid, srow, ALU.mult))
            step(v.tensor_scalar(sneg[:, :, :], valid, -NEG, NEG, ALU.mult, ALU.add))
            def select_src(half):
                g0, g1 = half * GROUPS // 2, (half + 1) * GROUPS // 2
                v.wait_ge(src4_gathered[half], 16 * (g1 - g0))
                rows, n = slice(4 * g0, 4 * g1), g1 - g0
                s4 = src4_row.rearrange("p (g d s) -> p g d s", d=4, s=WIN)[:, g0:g1]
                wg = winc[:, rows].rearrange("p (g j) -> p g j", j=4)
                own, other = srow[:, rows, :], valid[:, rows, :]
                sg = own.rearrange("p (g j) w -> p g j w", j=4)
                step(v.tensor_copy(sg[:, :, 0, :], s4[:, :, 0, :]))
                for j in range(1, 4):
                    step(v.tensor_tensor(delta[:, 0:n], wg[:, :, j], wg[:, :, 0], ALU.subtract))
                    for d in range(j + 1):
                        step(v.scalar_tensor_tensor(out=seltmp[:, 0:n, :] if d else sg[:, :, j, :],
                                                    in0=bc_last(delta[:, 0:n], WIN), scalar=float(d), in1=s4[:, :, d, :],
                                                    op0=ALU.is_equal, op1=ALU.mult))
                        if d:
                            step(v.tensor_tensor(sg[:, :, j, :], sg[:, :, j, :], seltmp[:, 0:n, :], ALU.add))
                step(v.tensor_tensor(own, own, other, ALU.mult))
                step(v.tensor_reduce(fmx[:, rows], own, AX.X, ALU.max))
                step(v.tensor_scalar(other, other, -1.0, 1.0, ALU.mult, ALU.add))
                step(v.tensor_tensor(other, other, bc_last(fmx[:, rows], WIN), ALU.mult))
                step(v.tensor_tensor(pack[:, rows, 0:WIN], own, other, ALU.add))

            step(v.tensor_copy(pack[:, 0:LANE_ROWS, WIN], winc))
            step(v.tensor_copy(pack[:, 0:LANE_ROWS, WIN + 1], fld[:, 3, :]))
            step(v.memset(pack[:, LANE_ROWS:LANE_ROWS + RING, :], 0))
            v.wait_ge(zero_m, 16)
            step(v.tensor_scalar(neg_ident, ident[:, :], -1.0, None, ALU.mult))
            select_src(0)
            v.wait_ge(k_out, 48)
            v.memset(top[:, RING - 1, :], 0.0).then_inc(qidx_done, 1)
            select_src(1)
            v.memset(zs[:, RING - 1, :], 0.0).then_inc(qidx_done, 1)
            v.wait_ge(qidx_done, 2)

            def walk(i, u, weigh_before=True, logits_now=True):
                cold = isinstance(i, int) and i == 0
                n, h = 28 * i + 7 * u, u % 2
                j, o = (i, u - 1) if u else (i - 1, RING - 1)
                cold_o = isinstance(j, int) and j == 0 and o < 2
                l = qv[:, u, :, 0, :]
                e, val = qv[:, o, :, 0, :], qv[:, o, :, 1, :]
                before, now = top[:, (u - 1) % RING, :], top[:, u, :]
                half = WIN // 2
                if logits_now:
                    v.wait_ge(qv_in[u], 16 * (WIN + 1) * (i + 1))
                    v.tensor_tensor(l, l, bc_mid(kk[:, u, :], WIN), ALU.mult).then_inc(a_step, 1)
                if weigh_before:
                    v.wait_ge(exp_ready, 12 * j + 3 * o + 1)
                    v.tensor_tensor(val[:, 0:half, :], val[:, 0:half, :], e[:, 0:half, :], ALU.mult).then_inc(weighted, 1)
                if logits_now:
                    v.wait_ge(a_step, n + 1)
                    v.tensor_tensor(mx1, l[:, 0:half, :], l[:, half:WIN, :], ALU.max).then_inc(a_step, 1)
                if weigh_before:
                    v.wait_ge(exp_ready, 12 * j + 3 * o + 3)
                    v.tensor_tensor(val[:, half:WIN, :], val[:, half:WIN, :], e[:, half:WIN, :], ALU.mult).then_inc(weighted, 1)
                if logits_now:
                    v.wait_ge(a_step, n + 2)
                    v.tensor_tensor(mx2, mx1[:, 0:2, :], mx1[:, 2:4, :], ALU.max).then_inc(a_step, 1)
                    v.wait_ge(a_step, n + 3)
                    v.tensor_tensor(mx3, mx2[:, 0, :], mx2[:, 1, :], ALU.max).then_inc(a_step, 1)
                if weigh_before:
                    if not (cold_o and o == 0):
                        v.wait_ge(state_ready, 4 * j + o)
                    if not cold_o:
                        v.wait_ge(psum_ready, 4 * j + o - 1)
                    v.tensor_tensor(carry[:, o % 2, :].rearrange("p (a c) -> p a c", a=2),
                                    zs[:, (o - 1) % RING, :].rearrange("p (a c) -> p a c", a=2),
                                    bc_mid(alpha[:, o % 2, :], 2), ALU.mult).then_inc(weighted, 1)
                if logits_now:
                    v.wait_ge(a_step, n + 4)
                    if not cold:
                        v.wait_ge(hist_out[u], 32 * i)
                    reset = mneg[:, bass.ds(4 * i + u, 1)]
                    v.scalar_tensor_tensor(out=now, in0=before, scalar=reset, in1=mx3, op0=ALU.add, op1=ALU.max)\
                     .then_inc(a_step, 1)
                    v.wait_ge(a_step, n + 5)
                    mine = WIN - PE_SLOTS
                    v.tensor_tensor(l[:, 0:mine, :], l[:, 0:mine, :], bc_mid(now, mine), ALU.subtract).then_inc(a_step, 1)
                    if not (cold and u < 2):
                        v.wait_ge(weighted, 12 * i + 3 * u - 3)
                    v.scalar_tensor_tensor(out=alpha[:, h, :], in0=before, scalar=reset, in1=now,
                                           op0=ALU.add, op1=ALU.subtract).then_inc(a_step, 1)

            walk(0, 0, weigh_before=False)
            for u in range(1, RING):
                walk(0, u)
            with v.Fori(1, LANE_ROWS // RING) as i:
                for u in range(RING):
                    walk(i, u)
            walk(LANE_ROWS // RING, 0, logits_now=False)

            v.wait_ge(lanes_in, 32)
            for u in range(2):
                v.wait_ge(qv_out[u], 16 * (NB // 2))
            step(v.tensor_copy(dst_l, dst_l.bitcast(I32)))
            first, last_d = dst_l[:, :, 0], dst_l[:, :, WIN - 1]
            step(v.tensor_tensor(first_neg[:, :, :], dst_l, bc_last(first, WIN), ALU.is_equal))
            step(v.tensor_tensor(later_neg[:, :, :], dst_l, bc_last(last_d, WIN), ALU.is_equal))
            step(v.tensor_tensor(later_neg[:, :, :], later_neg[:, :, :], first_neg[:, :, :], ALU.is_gt))
            step(v.tensor_scalar(later_neg[:, :, :], later_neg[:, :, :], -NEG, NEG, ALU.mult, ALU.add))
            step(v.tensor_scalar(first_neg[:, :, :], first_neg[:, :, :], -NEG, NEG, ALU.mult, ALU.add))
            step(v.tensor_tensor(whole[:, :], first, last_d, ALU.is_equal))
            step(v.memset(joins[:, 0:1], 0.0))
            step(v.tensor_tensor(joins[:, 1:LANE_WIN], first[:, 1:LANE_WIN], last_d[:, 0:LANE_WIN - 1], ALU.is_equal))
            step(v.tensor_scalar(dst_l.rearrange("p t w -> p (t w)"), dst_l.rearrange("p t w -> p (t w)"), dst_l[:, 0, 0:1],
                                 None, ALU.is_equal, ALU.add, accum_out=lane[:, 4:5]))
            v.wait_ge(small_out, 4)
            step(v.tensor_scalar(small_any[:, :], banks[7][:, P:P + 1], 1.0, None, ALU.min))
            v.tensor_copy(small_i[:, :], small_any[:, :]).then_inc(path_known, 1)
            step(v.tensor_copy(flagb[:, 0, :], banks[7][:, 0:P]))
            step(v.tensor_scalar(flagb[:, 1, :], flagb[:, 0, :], -NEG, NEG, ALU.mult, ALU.add))

            v.wait_ge(small_out, 5)
            for n in range(3):
                step(v.tensor_copy(join[:, 4 * n:4 * n + 4, :].rearrange("p n c -> p (n c)"), banks[2 + n][:, :]))
            J = lambda n, m=None: join[:, n, :] if m is None else join[:, n:m, :]
            over_k = lambda t: t[:, None, :, :].to_broadcast([P, 2, 2, P])
            by_k = lambda t: t.rearrange("p (k h) c -> p k h c", k=2)

            def together(*instructions):
                for ins in instructions:
                    ins.then_inc(dve, 1)
                count[0] += len(instructions)
                v.wait_ge(dve, count[0])

            def shifted(to, of):
                together(v.memset(to[:, :, 0:1], 0.0), v.tensor_copy(to[:, :, 1:P], of[:, :, 0:P - 1]))

            first_max = J(6, 8)
            run_max, in_max, new_max = J(12, 14), J(14, 16), J(16, 18)
            decay, own, arriving, here = (J(18 + 2 * n, 20 + 2 * n) for n in range(4))
            terms, sums, arrived = J(26, 30), J(30, 34), J(34, 38)
            together(*(v.tensor_tensor_scan(J(12 + h), flagb[:, 1, :], J(h), NEG, ALU.add, ALU.max) for h in range(2)))
            shifted(in_max, run_max)
            together(v.tensor_tensor(decay, in_max, flagb[:, 1:2, :].to_broadcast([P, 2, P]), ALU.add),
                     v.tensor_tensor(own, J(0, 2), run_max, ALU.subtract),
                     v.tensor_tensor(new_max, in_max, first_max, ALU.max))
            ins = [v.tensor_tensor(decay, decay, run_max, ALU.subtract),
                   v.tensor_tensor(arriving, in_max, new_max, ALU.subtract),
                   v.tensor_tensor(here, first_max, new_max, ALU.subtract)]
            together(*ins[0:2])
            ins[2].then_inc(join_arg, 1)
            v.wait_ge(join_exp, 1)
            step(v.tensor_tensor(by_k(terms), by_k(J(2, 6)), over_k(own), ALU.mult))
            together(*(v.tensor_tensor_scan(J(30 + n), J(18 + n % 2), J(26 + n), 0.0, ALU.mult, ALU.add) for n in range(4)))
            shifted(arrived, sums)
            together(v.tensor_tensor(by_k(arrived), by_k(arrived), over_k(arriving), ALU.mult),
                     v.tensor_tensor(by_k(terms), by_k(J(8, 12)), over_k(here), ALU.mult))
            v.tensor_tensor(J(8, 12), arrived, terms, ALU.add).then_inc(small_in, 1)
            v.wait_ge(small_out, 6)
            v.tensor_copy(carry[:, 0, :], banks[2][:, :]).then_inc(join_done, 1)

            step(v.tensor_scalar(nt[:, 0, :], has[:, :], -1.0, None, ALU.mult))
            for c in range(3):
                part = slice(c * LN_CHUNK, (c + 1) * LN_CHUNK)
                z, s = fin[:, part, 0, :], fin[:, part, 1, :]
                if c == 0:
                    for b in range(0, LN_CHUNK, 2):
                        v.wait_ge(fin_in[fin_group(b)], 32)
                        v.reciprocal(z[:, b:b + 2, :], z[:, b:b + 2, :]).then_inc(fin_step, 1)
                        v.wait_ge(fin_step, b // 2 + 1)
                        v.tensor_tensor(s[:, b:b + 2, :], s[:, b:b + 2, :], z[:, b:b + 2, :], ALU.mult).then_inc(dve, 1)
                        count[0] += 1
                    v.wait_ge(dve, count[0])
                else:
                    v.wait_ge(z_guess, 2 * c)
                    guessed = hs[:, part, :]
                    step(v.tensor_tensor(z, z, guessed, ALU.mult))
                    step(v.scalar_tensor_tensor(out=s, in0=z, scalar=-2.0, in1=s, op0=ALU.add, op1=ALU.mult))
                    step(v.tensor_tensor(s, s, guessed, ALU.mult))
                for b in range(c * LN_CHUNK, (c + 1) * LN_CHUNK):
                    last = v.scalar_tensor_tensor(out=xs[:, b, :], in0=fin[:, b, 1, :],
                                                  scalar=nt[:, 0, b:b + 1] if c else has[:, b:b + 1],
                                                  in1=xs[:, b, :], op0=ALU.mult, op1=ALU.add)
                last.then_inc(fin_used, 1)
                v.wait_ge(fin_used, c + 1)
                ln_stats(xs, c + 7, c)
                ln_scale(c + 7, c)
            step(v.memset(acc[:, RING - 1, :], 0.0))
            v.wait_ge(h_ready, 2 * NB)
            v.tensor_tensor(xs[:, :, :], xs[:, :, :], hs[:, :, :], ALU.add).then_inc(xh_done, 1)

            def add_edges(i, u):
                v.wait_ge(msg_in[u], 16 * (WIN + 1) * (i + 1))
                if not (isinstance(i, int) and i == 0):
                    v.wait_ge(hista_out[u], 16 * i)
                m = hmsg[:, u, :, :].rearrange("p w c -> p (w c)")
                v.tensor_tensor(m, m, eat[:, u, :], ALU.add).then_inc(added, 1)

            def carry_sum(i, u):
                early = isinstance(i, int) and i == 0
                if not (early and u == 0):
                    v.wait_ge(acc_ready, 4 * i + u)
                if not (early and u < 2):
                    v.wait_ge(sum_ready, 4 * i + u - 1)
                v.tensor_scalar(carry[:, u % 2, 0:CH], acc[:, (u - 1) % RING, :], acont[:, bass.ds(4 * i + u, 1)], None,
                                ALU.mult).then_inc(carried, 1)

            def join_sums(flag):
                v.wait_ge(small_out, 7)
                step(v.tensor_copy(join[:, 0:4, :].rearrange("p n c -> p (n c)"), banks[2][:, :]))
                together(*(v.tensor_tensor_scan(J(12 + h), flag, J(h), 0.0, ALU.mult, ALU.add) for h in range(2)))
                shifted(J(14, 16), J(12, 14))
                v.tensor_tensor(J(2, 4), J(2, 4), J(14, 16), ALU.add).then_inc(small_in, 1)
                v.wait_ge(small_out, 8)
                v.tensor_copy(carry[:, 0, 0:CH], banks[2][:, 0:CH]).then_inc(join_done, 1)

            def add_parts(i, u):
                v.wait_ge(msg_in[u], 16 * WIN * (i + 1))
                v.wait_ge(edges_in[u], 16 * (i + 1))
                v.tensor_tensor(parts[:, u, 0, :, :], parts[:, u, 0, :, :], parts[:, u, 1, :, :], ALU.add).then_inc(added, 1)

            def carry_parts(i, u):
                early = isinstance(i, int) and i == 0
                before = zs[:, (u - 1) % RING, CH:2 * CH]
                t = bass.ds(4 * i + u, 1)
                v.wait_ge(sum_ready, 4 * i + u + 1)
                if not early:
                    v.wait_ge(hista_out[u], 16 * i)
                if not (early and u == 0):
                    v.wait_ge(acc_ready, 4 * i + u)
                v.scalar_tensor_tensor(out=zs[:, u, 0:CH], in0=before, scalar=joins[:, t], in1=banks[u % 2][:, 0:CH],
                                       op0=ALU.mult, op1=ALU.add).then_inc(first_sum, 1)
                v.wait_ge(first_sum, 4 * i + u + 1)
                v.scalar_tensor_tensor(out=zs[:, u, CH:2 * CH], in0=zs[:, u, 0:CH], scalar=whole[:, t],
                                       in1=banks[u % 2][:, CH:2 * CH], op0=ALU.mult, op1=ALU.add).then_inc(acc_ready, 1)

            v.wait_ge(join_out, 16)
            rows_needed = v.value_load(small_i[0:1, 0:1], min_val=0, max_val=1)
            straight = count[0]
            with v.If(rows_needed == 0):
                step(v.tensor_scalar(lane[:, 5:6], lane[:, 4:5], LANE_EDGES - 0.5, None, ALU.is_ge))
                step(v.tensor_scalar(flagd[:, :], ident[:, :], lane[:, 5:6], None, ALU.mult))
                step(v.tensor_scalar(lane_j[:, 1:2], lane[:, 4:5], -1.0, None, ALU.add))
                step(v.tensor_scalar(lane_j[:, 1:2], lane_j[:, 1:2], 3, None, ALU.arith_shift_right))
                step(v.tensor_copy(lane[:, 1:2], lane_j[:, 1:2]))
                step(v.tensor_scalar(lane[:, 0:1], row[:, 0:1], float(LANE_WIN) / LANE_ROWS, None, ALU.mult))
                step(v.tensor_tensor(lane[:, 0:1], lane[:, 0:1], lane[:, 1:2], ALU.add))
                step(v.tensor_scalar(lane[:, 0:1], lane[:, 0:1], 2.0, None, ALU.mult))
                v.tensor_copy(lane_j[:, 2:3], lane[:, 0:1]).then_inc(flag_in, 1)
                t, lane_f, lane_l, wl = (nt[:, n, :] for n in range(4))
                step(v.tensor_scalar(n_i[:, 0, 0:NB], en, -1.0, None, ALU.add))
                step(v.tensor_scalar(n_i[:, 0, 0:NB], n_i[:, 0, 0:NB], 3, None, ALU.arith_shift_right))
                step(v.tensor_copy(wl, n_i[:, 0, 0:NB]))
                step(v.tensor_scalar(t, wl, float(WIN), None, ALU.mult))
                step(v.tensor_tensor(t, t, st, ALU.is_lt))
                step(v.scalar_tensor_tensor(out=t, in0=wl, scalar=2.0, in1=t, op0=ALU.mult, op1=ALU.add))
                middle = (LANE_EDGES - 1) / 2
                step(v.tensor_scalar(lane_i[:, 0, :], st, -middle, 1.0 / LANE_EDGES, ALU.add, ALU.mult))
                step(v.tensor_scalar(lane_i[:, 1, :], en, -middle - 1.0, 1.0 / LANE_EDGES, ALU.add, ALU.mult))
                step(v.tensor_copy(nt[:, 1:3, :], lane_i[:, :, :]))
                step(v.tensor_tensor(lane_f, lane_l, lane_f, ALU.is_gt))
                step(v.scalar_tensor_tensor(out=lane_l, in0=lane_l, scalar=float(LANE_STATES), in1=t, op0=ALU.add, op1=ALU.subtract))
                step(v.tensor_tensor(lane_l, lane_l, lane_f, ALU.mult))
                step(v.tensor_tensor(t, t, lane_l, ALU.add))
                step(v.tensor_tensor(t, t, has[:, :], ALU.mult))
                step(v.tensor_copy(fidx[:, :], t))
                v.wait_ge(flag_out, 1)
                step(v.tensor_copy(flagl[:, :], banks[7][:, 0:P]))
                step(v.memset(zs[:, RING - 1, :], 0.0))
                add_parts(0, 0)
                for u in range(1, RING):
                    add_parts(0, u)
                    carry_parts(0, u - 1)
                with v.Fori(1, LANE_WIN // RING) as i:
                    for u in range(RING):
                        add_parts(i, u)
                        carry_parts(i if u else i - 1, (u - 1) % RING)
                add_parts(LANE_WIN // RING, 0)
                carry_parts(LANE_WIN // RING - 1, RING - 1)
                carry_parts(LANE_WIN // RING, 0)
                join_sums(flagl[:, :])
            taken, count[0] = count[0], straight
            with v.Else():
                add_edges(0, 0)
                for u in range(1, RING):
                    add_edges(0, u)
                    carry_sum(0, u - 1)
                with v.Fori(1, LANE_ROWS // RING) as i:
                    for u in range(RING):
                        add_edges(i, u)
                        carry_sum(i if u else i - 1, (u - 1) % RING)
                carry_sum(LANE_ROWS // RING - 1, RING - 1)
                join_sums(flagb[:, 0, :])
                assert count[0] <= taken
                while count[0] < taken:
                    step(v.memset(small_any[:, :], 0.0))

            def add_agg(b):
                v.wait_ge(agg_in[b % FRING], 16 * (b // FRING) + 16)
                if b >= 3:
                    v.wait_ge(agg_tr, b - 2)
                v.scalar_tensor_tensor(out=turning[b % 3], in0=aggs[:, b % FRING, :], scalar=has[:, b:b + 1],
                                       in1=hs[:, b, :], op0=ALU.mult, op1=ALU.add).then_inc(agg_add, 1)

            def y1_stats(n):
                for m in range(4):
                    v.wait_ge(y1_ev, 4 * n + m + 1)
                    v.bn_stats(stats[:, n + m * NCHUNK, :], y1[:, m, n * CCOLS:(n + 1) * CCOLS]).then_inc(y1_bn, 1)

            for b in range(NB):
                add_agg(b)
                if b % 3 == 2 and b >= 11:
                    y1_stats((b - 11) // 3)
            for n in range((NB - 9) // 3, NCHUNK):
                y1_stats(n)
            v.wait_ge(y1_bn, 4 * NCHUNK)
            for m in range(4):
                last = v.bn_aggr(mvd[:, m, :], stats[:, m * NCHUNK:(m + 1) * NCHUNK, :].rearrange("p n s -> p (n s)"))
            step(last)
            v.tensor_copy(bn[:, 0, :], mvd[:, :, 1]).then_inc(bn_var, 1)
            v.wait_ge(bn_std, 1)
            step(v.reciprocal(bn[:, 0, :], bn[:, 0, :]))
            step(v.tensor_tensor(bn[:, 1, :], bn[:, 0, :], pvs("bn_g"), ALU.mult))
            step(v.tensor_tensor(bn[:, 2, :], bn[:, 1, :], mvd[:, :, 0], ALU.mult))
            v.tensor_tensor(bn[:, 2, :], pvs("bn_b"), bn[:, 2, :], ALU.subtract).then_inc(bn_ready, 1)

            with v.Fori(0, NCHUNK) as n:
                v.wait_ge(y2_ev, n + 1)
                for m in range(2):
                    v.bn_stats(stats[:, n + m * NCHUNK, :], y2[:, m, bass.ds(n * CCOLS, CCOLS)]).then_inc(y2_bn, 1)
            v.wait_ge(y2_bn, 2 * NCHUNK)
            for m in range(2):
                last = v.bn_aggr(mvd[:, m, :], stats[:, m * NCHUNK:(m + 1) * NCHUNK, :].rearrange("p n s -> p (n s)"))
            step(last)
            G = lambda n: gn[:, n, :]
            mean, var = mvd[:, 0:2, 0], mvd[:, 0:2, 1]
            v.tensor_copy(G(0), mean).then_inc(small_in, 1)
            v.wait_ge(small_out, 9)
            step(v.tensor_reduce(gn[:, 1, 0:1], banks[6][:, 0:2], AX.X, ALU.add))
            step(v.tensor_scalar(gn[:, 1, 0:1], gn[:, 1, 0:1], 1.0 / CH, None, ALU.mult))
            gm = gn[:, 1, 0:1]
            step(v.tensor_scalar(G(2), mean, gm, None, ALU.subtract))
            step(v.tensor_tensor(G(3), G(2), G(2), ALU.mult))
            v.tensor_tensor(G(3), G(3), var, ALU.add).then_inc(small_in, 1)
            v.wait_ge(small_out, 10)
            step(v.tensor_reduce(gn[:, 4, 0:1], banks[6][:, 2:4], AX.X, ALU.add))
            step(v.memset(G(12), 0.0))
            v.tensor_scalar(G(12), G(12), gn[:, 4, 0:1], 1.0 / CH, ALU.add, ALU.mult).then_inc(g_var, 1)
            v.wait_ge(g_std, 1)
            step(v.reciprocal(G(12), G(12)))
            step(v.tensor_tensor(G(5), pvs("ln_w"), G(12), ALU.mult))
            step(v.tensor_scalar(G(6), G(5), gm, None, ALU.mult))
            step(v.tensor_tensor(G(6), pvs("ln_b"), G(6), ALU.subtract))
            step(v.tensor_tensor(G(7), G(5), mean, ALU.mult))
            step(v.tensor_tensor(G(7), G(7), G(6), ALU.add))
            step(v.tensor_tensor(G(8), G(7), pvs("gn_ms"), ALU.mult))
            step(v.tensor_tensor(G(9), G(7), G(8), ALU.subtract))
            step(v.tensor_tensor(G(9), G(9), G(9), ALU.mult))
            step(v.tensor_tensor(G(10), G(5), G(5), ALU.mult))
            step(v.tensor_tensor(G(10), G(10), var, ALU.mult))
            v.tensor_tensor(G(12), G(10), G(9), ALU.add).then_inc(g_var, 1)
            v.wait_ge(g_std, 2)
            step(v.reciprocal(G(12), G(12)))
            step(v.tensor_tensor(G(11), pvs("gn_w"), G(12), ALU.mult))
            step(v.tensor_tensor(G(13), G(5), G(11), ALU.mult))
            step(v.tensor_tensor(G(14), G(6), G(8), ALU.subtract))
            step(v.tensor_tensor(G(14), G(14), G(11), ALU.mult))
            v.tensor_tensor(G(14), G(14), pvs("gn_b"), ALU.add).then_inc(g_ready, 1)

            v.wait_ge(xh_done, 1)
            for q in range(NB // 2):
                v.wait_ge(out_tr, q + 1)
                two = xs[0:NP, 2 * q:2 * q + 2, :].rearrange("p b c -> p (b c)")
                v.tensor_tensor(two, banks[q % 3][0:NP, :], two, ALU.add).then_inc(out_add, 1)


def kernel(x, src, dst, edge_attr_256, L0_gnn_Wqkv, L0_gnn_gamma, L0_gnn_beta, L1_gnn_W1, L1_gnn_b1, L1_gnn_bn_gamma,
           L1_gnn_bn_beta, L1_gnn_W2, L1_gnn_b2, L1_gnn_ln_w, L1_gnn_ln_b, L1_gnn_gn_w, L1_gnn_gn_b, L1_gnn_gn_ms):
    import concourse.bacc as bacc
    from concourse.bass_utils import run_bass_kernel_spmd

    def padded(a, rows):
        return np.concatenate([a, np.zeros((rows - a.shape[0],) + a.shape[1:], a.dtype)])

    a = {}
    a["x"] = padded(np.asarray(x), PAD_NODES)
    flat = padded(np.asarray(src), (P * LANE_WIN + 3) * WIN)
    a["src"] = np.stack([flat[p * LANE_WIN * WIN:(p * LANE_WIN + LANE_WIN + 3) * WIN] for p in range(P)])
    d = np.asarray(dst)
    a["dst"] = np.concatenate([d, np.full(P * LANE_EDGES - EDGES, NODES, d.dtype)])
    a["edge"] = padded(np.asarray(edge_attr_256), P * LANE_EDGES).reshape(P * LANE_WIN, WIN * CH)
    w = np.asarray(L0_gnn_Wqkv).reshape(2, P, 3, CH).transpose(1, 0, 2, 3)
    a["wqkv"] = np.ascontiguousarray(np.stack([w[:, :, 0], w[:, :, 2], w[:, :, 1]], 2).reshape(P, 2, 3 * CH))
    a["w1"] = np.ascontiguousarray(np.asarray(L1_gnn_W1).reshape(2, P, HID).transpose(1, 0, 2))
    a["w2"] = np.ascontiguousarray(np.asarray(L1_gnn_W2).reshape(4, P, CH).transpose(1, 0, 2))
    vectors = [L0_gnn_gamma, L0_gnn_beta, L1_gnn_b1, L1_gnn_bn_gamma, L1_gnn_bn_beta, L1_gnn_b2, L1_gnn_ln_w,
               L1_gnn_ln_b, L1_gnn_gn_w, L1_gnn_gn_b, L1_gnn_gn_ms]
    a["params"] = np.ascontiguousarray(np.concatenate([np.asarray(t).reshape(-1, P).T for t in vectors], 1))

    nc = bacc.Bacc("TRN2", target_bir_lowering=False, num_devices=1)
    args = [nc.dram_tensor(f"in_{n}", t.shape, mybir.dt.from_np(t.dtype), kind="ExternalInput").ap() for n, t in a.items()]
    out = nc.dram_tensor("out_0", (NODES, CH), F32, kind="ExternalOutput").ap()
    build(nc, *args, out)
    r = run_bass_kernel_spmd(nc, [{f"in_{n}": t for n, t in a.items()}], core_ids=[0])
    return r.results[0]["out_0"]
```
